# Optimizing a Trainium2 kernel written in Bass

```python
import numpy as np
import jax
import jax.numpy as jnp

def _softmax(x, axis=-1):
    return jax.nn.softmax(x, axis=axis)

def _gelu(x):
    return jax.nn.gelu(x, approximate=True)

def _silu(x):
    return jax.nn.silu(x)

def _sigmoid(x):
    return jax.nn.sigmoid(x)

def _layernorm(x, axis=-1, eps=1e-05):
    m = jnp.mean(x, axis=axis, keepdims=True)
    v = jnp.var(x, axis=axis, keepdims=True)
    return (x - m) / jnp.sqrt(v + eps)

def _scatter_add(tgt, idx, src, axis=0):
    return tgt.at[idx].add(src)

def _segment_sum(src, seg, n):
    return jax.ops.segment_sum(src, seg, n)
kernel_name = 'mk_gnn_resnorm_d4_gnn_r64_43cb97'

def setup_inputs(seed: int=0):
    np.random.seed(seed)
    _w = jnp.asarray

    def _rec_inputs():
        import jax
        import jax.numpy as jnp
        _gk = jax.random.key(seed)
        x = -0.000202 + 1 * jax.random.normal(jax.random.fold_in(_gk, 1), (50000, 128), jnp.float32)
        src = jax.random.randint(jax.random.fold_in(_gk, 2), (12500,), 0, 50000, jnp.int32)
        dst = jnp.minimum((50000 * jax.random.uniform(jax.random.fold_in(_gk, 3), (12500,)) ** 2.0).astype(jnp.int32), 49999)
        _o = jnp.argsort(dst, stable=True)
        src = src[_o]
        dst = dst[_o]
        edge_attr_128 = 2.93046e-05 + 1.00006 * jax.random.normal(jax.random.fold_in(_gk, 11), (12500, 128), jnp.float32)
        return (x, src, dst, edge_attr_128)
    x, src, dst, edge_attr_128 = _rec_inputs()

    def _L0_gnn_setup():
        import jax, jax.numpy as jnp
        import numpy as np
        N = 50000
        E = 12500
        D = 128
        N_LAYERS = 3

        def _xavier(key, fan_in, fan_out):
            limit = float(np.sqrt(6.0 / (fan_in + fan_out)))
            return jax.random.uniform(key, (fan_in, fan_out), jnp.float32, -limit, limit)

        def _gcn_forward(x, src, dst, norm, Ws, bs):
            n = x.shape[0]
            h = x
            for i, (W, b) in enumerate(zip(Ws, bs)):
                m = (h @ W)[src] * norm[:, None]
                h = jax.ops.segment_sum(m, dst, num_segments=n) + b
                if i < len(Ws) - 1:
                    h = jax.nn.relu(h)
            return h + x
        key = jax.random.key(seed)
        ks = jax.random.split(key, 2 + 2 * N_LAYERS)
        x = jax.random.normal(ks[0], (N, D), jnp.float32)
        edge_index = jax.random.randint(ks[1], (2, E), 0, N, jnp.int32)
        inp = {'x': x, 'edge_index': edge_index}
        for i in range(N_LAYERS):
            inp[f'W{i}'] = _xavier(ks[2 + 2 * i], D, D)
            inp[f'b{i}'] = jax.random.uniform(ks[3 + 2 * i], (D,), jnp.float32, -0.1, 0.1)
        return inp
    _L0_gnn_all = _L0_gnn_setup()
    _L0_gnn_in = {k: v for k, v in _L0_gnn_all.items() if k in ('W0', 'b0', 'W1', 'b1', 'W2', 'b2')}
    del _L0_gnn_all

    def _L1_gnn_setup():
        import jax, jax.numpy as jnp
        import numpy as np
        N, E = (50000, 12500)
        IN_DIM, HID, HEADS, OUT_DIM = (128, 64, 4, 128)
        NEG_SLOPE = 0.2

        def _gat_forward(x, edge_index, W, att_src, att_dst, bias, fc_w, fc_b):
            n = x.shape[0]
            h = (x @ W).reshape(n, HEADS, HID)
            loops = jnp.arange(n, dtype=edge_index.dtype)
            src = jnp.concatenate([edge_index[0], loops])
            dst = jnp.concatenate([edge_index[1], loops])
            a_src = jnp.einsum('nhf,hf->nh', h, att_src)
            a_dst = jnp.einsum('nhf,hf->nh', h, att_dst)
            e = jax.nn.leaky_relu(a_src[src] + a_dst[dst], NEG_SLOPE)
            m = jax.ops.segment_max(e, dst, num_segments=n)
            ex = jnp.exp(e - m[dst])
            denom = jax.ops.segment_sum(ex, dst, num_segments=n)
            alpha = ex / denom[dst]
            msg = h[src] * alpha[:, :, None]
            agg = jax.ops.segment_sum(msg, dst, num_segments=n)
            out = agg.reshape(n, HEADS * HID) + bias
            out = jax.nn.relu(out)
            return out @ fc_w + fc_b
        key = jax.random.key(seed)
        ks = jax.random.split(key, 8)
        s = 1.0 / np.sqrt(IN_DIM)
        x = jax.random.normal(ks[0], (N, IN_DIM), dtype=jnp.float32)
        edge_index = jax.random.randint(ks[1], (2, E), 0, N, dtype=jnp.int64)
        W = jax.random.uniform(ks[2], (IN_DIM, HEADS * HID), jnp.float32, -s, s)
        att_src = jax.random.uniform(ks[3], (HEADS, HID), jnp.float32, -s, s)
        att_dst = jax.random.uniform(ks[4], (HEADS, HID), jnp.float32, -s, s)
        bias = jnp.zeros((HEADS * HID,), jnp.float32)
        sf = 1.0 / np.sqrt(HEADS * HID)
        fc_w = jax.random.uniform(ks[5], (HEADS * HID, OUT_DIM), jnp.float32, -sf, sf)
        fc_b = jax.random.uniform(ks[6], (OUT_DIM,), jnp.float32, -sf, sf)
        return {'x': x, 'edge_index': edge_index, 'W': W, 'att_src': att_src, 'att_dst': att_dst, 'bias': bias, 'fc_w': fc_w, 'fc_b': fc_b}
    _L1_gnn_all = _L1_gnn_setup()
    _L1_gnn_in = {k: v for k, v in _L1_gnn_all.items() if k in ('W', 'att_src', 'att_dst', 'bias', 'fc_w', 'fc_b')}
    del _L1_gnn_all

    def _L2_gnn_setup():
        import jax, jax.numpy as jnp
        import numpy as np
        N_NODES = 100000
        N_EDGES = 10000
        F_DIM = 128
        D_DIM = 128
        ROUNDS = 4
        key = jax.random.key(seed)
        ks = jax.random.split(key, 8)
        s = 1.0 / np.sqrt(D_DIM)
        return {'x': jax.random.normal(ks[0], (N_NODES, F_DIM), dtype=jnp.float32), 'edge_index': jax.random.randint(ks[1], (2, N_EDGES), 0, N_NODES, dtype=jnp.int64), 'Wi': jax.random.normal(ks[2], (F_DIM, D_DIM), dtype=jnp.float32) * s, 'bi': jax.random.normal(ks[3], (D_DIM,), dtype=jnp.float32) * s, 'Wm': jax.random.normal(ks[4], (ROUNDS, D_DIM, D_DIM), dtype=jnp.float32) * s, 'bm': jax.random.normal(ks[5], (ROUNDS, D_DIM), dtype=jnp.float32) * s, 'Wu': jax.random.normal(ks[6], (ROUNDS, D_DIM, D_DIM), dtype=jnp.float32) * s, 'bu': jax.random.normal(ks[7], (ROUNDS, D_DIM), dtype=jnp.float32) * s}
    _L2_gnn_all = _L2_gnn_setup()
    _L2_gnn_in = {k: v for k, v in _L2_gnn_all.items() if k in ('Wi', 'bi', 'Wm', 'bm', 'Wu', 'bu')}
    del _L2_gnn_all

    def _L3_gnn_setup():
        import jax, jax.numpy as jnp
        import numpy as np
        N = 50000
        E = 10000
        D = 128
        H = 2 * D
        BN_EPS = 1e-05

        def _batchnorm(x, gamma, beta):
            mean = jnp.mean(x, axis=0)
            var = jnp.var(x, axis=0)
            return (x - mean) * jax.lax.rsqrt(var + BN_EPS) * gamma + beta
        key = jax.random.key(seed)
        ks = jax.random.split(key, 8)
        h = jax.random.normal(ks[0], (N, D), dtype=jnp.float32)
        edge_index = jax.random.randint(ks[1], (2, E), 0, N, dtype=jnp.int64)
        edge_attr = jax.random.normal(ks[2], (E, D), dtype=jnp.float32)
        W1 = jax.random.normal(ks[3], (D, H), dtype=jnp.float32) * (1.0 / np.sqrt(D))
        g1 = jnp.ones((H,), dtype=jnp.float32)
        b1 = jnp.zeros((H,), dtype=jnp.float32)
        W2 = jax.random.normal(ks[4], (H, D), dtype=jnp.float32) * (1.0 / np.sqrt(H))
        g2 = jnp.ones((D,), dtype=jnp.float32)
        b2 = jnp.zeros((D,), dtype=jnp.float32)
        eps = jnp.zeros((), dtype=jnp.float32)
        return {'h': h, 'edge_index': edge_index, 'edge_attr': edge_attr, 'eps': eps, 'W1': W1, 'g1': g1, 'b1': b1, 'W2': W2, 'g2': g2, 'b2': b2}
    _L3_gnn_all = _L3_gnn_setup()
    _L3_gnn_in = {k: v for k, v in _L3_gnn_all.items() if k in ('eps', 'W1', 'g1', 'b1', 'W2', 'g2', 'b2')}
    del _L3_gnn_all
    return {'x': x, 'src': src, 'dst': dst, 'edge_attr_128': edge_attr_128, 'L0_gnn_W0': _L0_gnn_in['W0'], 'L0_gnn_b0': _L0_gnn_in['b0'], 'L0_gnn_W1': _L0_gnn_in['W1'], 'L0_gnn_b1': _L0_gnn_in['b1'], 'L0_gnn_W2': _L0_gnn_in['W2'], 'L0_gnn_b2': _L0_gnn_in['b2'], 'L1_gnn_W': _L1_gnn_in['W'], 'L1_gnn_att_src': _L1_gnn_in['att_src'], 'L1_gnn_att_dst': _L1_gnn_in['att_dst'], 'L1_gnn_bias': _L1_gnn_in['bias'], 'L1_gnn_fc_w': _L1_gnn_in['fc_w'], 'L1_gnn_fc_b': _L1_gnn_in['fc_b'], 'L2_gnn_Wi': _L2_gnn_in['Wi'], 'L2_gnn_bi': _L2_gnn_in['bi'], 'L2_gnn_Wm': _L2_gnn_in['Wm'], 'L2_gnn_bm': _L2_gnn_in['bm'], 'L2_gnn_Wu': _L2_gnn_in['Wu'], 'L2_gnn_bu': _L2_gnn_in['bu'], 'L3_gnn_eps': _L3_gnn_in['eps'], 'L3_gnn_W1': _L3_gnn_in['W1'], 'L3_gnn_g1': _L3_gnn_in['g1'], 'L3_gnn_b1': _L3_gnn_in['b1'], 'L3_gnn_W2': _L3_gnn_in['W2'], 'L3_gnn_g2': _L3_gnn_in['g2'], 'L3_gnn_b2': _L3_gnn_in['b2']}

def reference(x, src, dst, edge_attr_128, L0_gnn_W0, L0_gnn_b0, L0_gnn_W1, L0_gnn_b1, L0_gnn_W2, L0_gnn_b2, L1_gnn_W, L1_gnn_att_src, L1_gnn_att_dst, L1_gnn_bias, L1_gnn_fc_w, L1_gnn_fc_b, L2_gnn_Wi, L2_gnn_bi, L2_gnn_Wm, L2_gnn_bm, L2_gnn_Wu, L2_gnn_bu, L3_gnn_eps, L3_gnn_W1, L3_gnn_g1, L3_gnn_b1, L3_gnn_W2, L3_gnn_g2, L3_gnn_b2):
    import jax
    import jax.numpy as jnp

    def _L0_gnn_ref(x, edge_index, W0, b0, W1, b1, W2, b2):
        import jax, jax.numpy as jnp
        import numpy as np
        N = 50000
        E = 12500
        D = 128
        N_LAYERS = 3

        def _xavier(key, fan_in, fan_out):
            limit = float(np.sqrt(6.0 / (fan_in + fan_out)))
            return jax.random.uniform(key, (fan_in, fan_out), jnp.float32, -limit, limit)

        def _gcn_forward(x, src, dst, norm, Ws, bs):
            n = x.shape[0]
            h = x
            for i, (W, b) in enumerate(zip(Ws, bs)):
                m = (h @ W)[src] * norm[:, None]
                h = jax.ops.segment_sum(m, dst, num_segments=n) + b
                if i < len(Ws) - 1:
                    h = jax.nn.relu(h)
            return h + x
        n = x.shape[0]
        loop = jnp.arange(n, dtype=edge_index.dtype)
        src = jnp.concatenate([edge_index[0], loop])
        dst = jnp.concatenate([edge_index[1], loop])
        deg = jax.ops.segment_sum(jnp.ones_like(dst, x.dtype), dst, num_segments=n)
        dinv = jax.lax.rsqrt(deg)
        norm = dinv[src] * dinv[dst]
        return _gcn_forward(x, src, dst, norm, (W0, W1, W2), (b0, b1, b2))

    def _L1_gnn_ref(x, edge_index, W, att_src, att_dst, bias, fc_w, fc_b):
        import jax, jax.numpy as jnp
        import numpy as np
        N, E = (50000, 12500)
        IN_DIM, HID, HEADS, OUT_DIM = (128, 64, 4, 128)
        NEG_SLOPE = 0.2

        def _gat_forward(x, edge_index, W, att_src, att_dst, bias, fc_w, fc_b):
            n = x.shape[0]
            h = (x @ W).reshape(n, HEADS, HID)
            loops = jnp.arange(n, dtype=edge_index.dtype)
            src = jnp.concatenate([edge_index[0], loops])
            dst = jnp.concatenate([edge_index[1], loops])
            a_src = jnp.einsum('nhf,hf->nh', h, att_src)
            a_dst = jnp.einsum('nhf,hf->nh', h, att_dst)
            e = jax.nn.leaky_relu(a_src[src] + a_dst[dst], NEG_SLOPE)
            m = jax.ops.segment_max(e, dst, num_segments=n)
            ex = jnp.exp(e - m[dst])
            denom = jax.ops.segment_sum(ex, dst, num_segments=n)
            alpha = ex / denom[dst]
            msg = h[src] * alpha[:, :, None]
            agg = jax.ops.segment_sum(msg, dst, num_segments=n)
            out = agg.reshape(n, HEADS * HID) + bias
            out = jax.nn.relu(out)
            return out @ fc_w + fc_b
        return _gat_forward(x, edge_index, W, att_src, att_dst, bias, fc_w, fc_b)

    def _L2_gnn_ref(x, edge_index, Wi, bi, Wm, bm, Wu, bu):
        import jax, jax.numpy as jnp
        import numpy as np
        N_NODES = 100000
        N_EDGES = 10000
        F_DIM = 128
        D_DIM = 128
        ROUNDS = 4
        num_nodes = x.shape[0]
        src = edge_index[0]
        dst = edge_index[1]
        state = jax.nn.relu(x @ Wi + bi)

        def step(state, params):
            Wm_r, bm_r, Wu_r, bu_r = params
            message = jax.nn.relu(state @ Wm_r + bm_r)
            gathered = message[src]
            aggregated = jax.ops.segment_sum(gathered, dst, num_segments=num_nodes)
            return (state + jax.nn.relu(aggregated @ Wu_r + bu_r), None)
        state, _ = jax.lax.scan(step, state, (Wm, bm, Wu, bu))
        return state

    def _L3_gnn_ref(h, edge_index, edge_attr, eps, W1, g1, b1, W2, g2, b2):
        import jax, jax.numpy as jnp
        import numpy as np
        N = 50000
        E = 10000
        D = 128
        H = 2 * D
        BN_EPS = 1e-05

        def _batchnorm(x, gamma, beta):
            mean = jnp.mean(x, axis=0)
            var = jnp.var(x, axis=0)
            return (x - mean) * jax.lax.rsqrt(var + BN_EPS) * gamma + beta
        n = h.shape[0]
        src = edge_index[0]
        dst = edge_index[1]
        msg = jax.nn.relu(h[src] + edge_attr)
        aggr = jax.ops.segment_sum(msg, dst, num_segments=n)
        z = (1.0 + eps) * h + aggr
        z = jax.nn.relu(_batchnorm(z @ W1, g1, b1))
        z = z @ W2
        z = jax.nn.relu(_batchnorm(z, g2, b2))
        return z + h
    edge_index = jnp.stack([src, dst])
    x = _layernorm(x + _L0_gnn_ref(x, edge_index, L0_gnn_W0, L0_gnn_b0, L0_gnn_W1, L0_gnn_b1, L0_gnn_W2, L0_gnn_b2), axis=-1)
    x = _layernorm(x + _L1_gnn_ref(x, edge_index, L1_gnn_W, L1_gnn_att_src, L1_gnn_att_dst, L1_gnn_bias, L1_gnn_fc_w, L1_gnn_fc_b), axis=-1)
    x = _layernorm(x + _L2_gnn_ref(x, edge_index, L2_gnn_Wi, L2_gnn_bi, L2_gnn_Wm, L2_gnn_bm, L2_gnn_Wu, L2_gnn_bu), axis=-1)
    x = _layernorm(x + _L3_gnn_ref(x, edge_index, edge_attr_128, L3_gnn_eps, L3_gnn_W1, L3_gnn_g1, L3_gnn_b1, L3_gnn_W2, L3_gnn_g2, L3_gnn_b2), axis=-1)
    return x

_drawn_inputs = setup_inputs


def setup_inputs(seed=0):
    import zlib

    import numpy as np

    out = dict(_drawn_inputs(seed))
    spreads = {'L1_gnn_bias': (0.0, 0.1),
     'L3_gnn_g1': (1.0, 0.2),
     'L3_gnn_b1': (0.0, 0.275),
     'L3_gnn_g2': (1.0, 0.2),
     'L3_gnn_b2': (0.0, 0.1)}
    factors = {'L0_gnn_b0': 3.549, 'L1_gnn_att_src': 8.0, 'L1_gnn_att_dst': 8.0}
    for name, (base, spread) in spreads.items():
        noise = np.random.default_rng([zlib.crc32(name.encode()), seed]).standard_normal(out[name].shape)
        drawn = base * np.exp(spread * noise) if base else spread * noise
        out[name] = jnp.asarray(drawn.astype(out[name].dtype))
    for name, factor in factors.items():
        out[name] = (out[name] * factor).astype(out[name].dtype)
    return out
```

```python
import numpy as np
import concourse.bass as bass
from concourse import mybir
from contextlib import ExitStack

F32, BF16, I32 = mybir.dt.float32, mybir.dt.bfloat16, mybir.dt.int32
ALU, ACTF, AX = mybir.AluOpType, mybir.ActivationFunctionType, mybir.AxisListType

MOST = 7
D = 128
GC = 512
LN_EPS = 1e-5
BN_EPS = 1e-5
SLOPE = 0.2
FAR = 1e30


class Signals:

    def __init__(self, nc, ctx):
        self.nc, self.ctx, self.handle, self.base, self.spare = nc, ctx, {}, {}, []

    def __call__(self, name):
        if name not in self.handle:
            if self.spare:
                self.handle[name], self.base[name] = self.spare.pop()
            else:
                self.handle[name], self.base[name] = self.ctx.enter_context(self.nc.semaphore(name)), 0
        return self.handle[name]

    def retire(self, names):
        for name in names:
            self.spare.append((self.handle.pop(name), self.base.pop(name)))

    def at(self, name, n):
        self(name)
        return n + self.base[name]

    def passed(self, totals):
        for name, n in totals.items():
            self(name)
            self.base[name] += n


def build(nc, a, out):
    N = a["x"].shape[0]
    E = a["src"].shape[0]
    EG = -(-E // GC)
    EP = EG * GC
    ET = EP // 128
    NF = N // GC
    R = N - NF * GC
    TJ = next(j for j in (4, 3, 2, 1) if R % j == 0 and (R // j) % 16 == 0 and R // j <= 128) if R else 4
    TP = R // TJ if R else 128
    NG = NF + (R > 0)
    EQ = next(p for p in range(128, 0, -1) if E % p == 0)
    EW = E // EQ
    PADS = EP + 128 - E
    HEADS, HID = a["L1_gnn_att_src"].shape
    HC = HID // 2
    ROUNDS = a["L2_gnn_Wm"].shape[0]
    assert HEADS * HC == D and N + EP < 1 << 24 and EG >= 2 and NG >= 2 and ET <= 128

    ctx = ExitStack()
    with ctx:
        def sb(name, shape, dt=F32):
            return ctx.enter_context(nc.sbuf_tensor(name, shape, dt))

        def dram(name, shape, dt=F32):
            return nc.dram_tensor(name, shape, dt).ap()

        S = Signals(nc, ctx)
        psum = [ctx.enter_context(nc.psum_tensor(f"bank{i}", [128, GC], F32)) for i in range(8)]
        pGram, pMisc = psum[7], psum[6]

        sorted_src = dram("sorted_src", [EP + 128], I32)
        sorted_dst = dram("sorted_dst", [EP + 128], I32)
        sorted_edge = dram("sorted_edge", [EP + 128], I32)
        keep_row = dram("keep_row", [EP])
        count_row = dram("count_row", [EP])
        node_slot = dram("node_slot", [N])
        gcn_table = [dram(f"gcn_table{i}", [2 * EP, D]) for i in range(3)]
        gat_table = dram("gat_table", [2 * EP, D])
        mpn_table = [dram(f"mpn_table{i}", [2 * EP, D]) for i in range(2)]
        x0_slots = dram("x0_slots", [EP, D])
        x2_slots = dram("x2_slots", [EP, D])
        x3_slots = dram("x3_slots", [EP, D])
        z_slots = dram("z_slots", [EP, D])
        x3_nodes = dram("x3_nodes", [N, D])
        y_cols = dram("y_cols", [D, N + EP])

        ident = sb("ident", [128, 128])
        zeros = sb("zeros", [128, D + 1])
        ones_bf = sb("ones_bf", [128, 128], BF16)
        W0, W1, W2 = (sb(f"W{i}", [D, D]) for i in range(3))
        Wg = sb("Wg", [D, 2, D])
        fcw = sb("fcw", [D, 2, D])
        Wi = sb("Wi", [D, D])
        Wm = sb("Wm", [D, ROUNDS, D])
        Wu = sb("Wu", [D, ROUNDS, D])
        V1 = sb("V1", [D, 2, D])
        V2 = sb("V2", [D, 2, D])
        attS, attD, attSD = (sb(n, [D, D]) for n in ("attS", "attD", "attSD"))
        ROWS = 3 + ROUNDS
        row_b2, row_fc, row_bi, row_bu = 0, 1, 2, 3
        rows = sb("rows", [128, ROWS, D])
        bias3 = sb("bias3", [128, ROWS, D], BF16)
        rowb0, rowb1 = sb("rowb0", [128, D]), sb("rowb1", [128, D])
        cu = sb("cu", [128, ROUNDS, D])
        c_all = sb("c_all", [128, D])
        cb = sb("cb", [128, 16])
        c_b0, c_b1, c_gat, c_bm, c_bu, c_cum = 0, 1, 2, 4, 8, 12
        bn = sb("bn", [128, 16])
        b_g1, b_b1, b_g2, b_b2, b_s1, b_t1, b_s2, b_t2 = 0, 2, 4, 5, 6, 8, 10, 11
        eps1 = sb("eps1", [128, 1])
        neg_half = sb("neg_half", [128, 4])
        idx = sb("idx", [128, ET], I32)
        idx_own = sb("idx_own", [128, ET], I32)
        src_i = sb("src_i", [128, ET], I32)
        edge_i = sb("edge_i", [128, ET], I32)
        dst_g = sb("dst_g", [128, ET], I32)
        dst_s = sb("dst_s", [128, ET], I32)
        dinv = sb("dinv", [128, ET])
        last = sb("last", [128, ET])
        nmask = sb("nmask", [128, 4 * NG])
        ystat = sb("ystat", [128, NG + EG, 6])
        small = sb("small", [128, 24])
        gram = sb("gram", [D, D + 1])
        mrow = sb("mrow", [1, D])
        prod = sb("prod", [D, 2, D])
        onesc = sb("onesc", [128, 1])


        loads = []

        def column(dst, vec):
            loads.append((dst, vec.rearrange("(p o) -> p o", o=1)))

        def row(dst, vec):
            loads.append((dst, vec.partition_broadcast(128)))

        for dst, name in ((W0, "L0_gnn_W0"), (W1, "L0_gnn_W1"), (W2, "L0_gnn_W2"), (Wi, "L2_gnn_Wi")):
            loads.append((dst[:, :], a[name]))
        loads.append((Wm[:, :, :], a["L2_gnn_Wm"].rearrange("r i o -> i r o")))
        loads.append((Wu[:, :, :], a["L2_gnn_Wu"].rearrange("r i o -> i r o")))
        loads.append((V1[:, :, :], a["L3_gnn_W1"].rearrange("i (c o) -> i c o", c=2)))
        loads.append((V2[:, :, :], a["L3_gnn_W2"].rearrange("(c i) o -> i c o", c=2)))
        for c in range(2):
            for h in range(HEADS):
                at = HID * h + HC * c
                loads.append((Wg[:, c, HC * h:HC * (h + 1)], a["L1_gnn_W"][:, at:at + HC]))
                loads.append((fcw[HC * h:HC * (h + 1), c, :], a["L1_gnn_fc_w"][at:at + HC, :]))
                column(cb[HC * h:HC * (h + 1), c_gat + c:c_gat + c + 1], a["L1_gnn_bias"][at:at + HC])
            column(bn[:, b_g1 + c:b_g1 + c + 1], a["L3_gnn_g1"][c * D:(c + 1) * D])
            column(bn[:, b_b1 + c:b_b1 + c + 1], a["L3_gnn_b1"][c * D:(c + 1) * D])
        column(bn[:, b_g2:b_g2 + 1], a["L3_gnn_g2"])
        column(bn[:, b_b2:b_b2 + 1], a["L3_gnn_b2"])
        column(cb[:, c_b0:c_b0 + 1], a["L0_gnn_b0"])
        column(cb[:, c_b1:c_b1 + 1], a["L0_gnn_b1"])
        row(rowb0[:, :], a["L0_gnn_b0"])
        row(rowb1[:, :], a["L0_gnn_b1"])
        row(rows[:, row_b2, :], a["L0_gnn_b2"])
        row(rows[:, row_fc, :], a["L1_gnn_fc_b"])
        row(rows[:, row_bi, :], a["L2_gnn_bi"])
        for r in range(ROUNDS):
            column(cb[:, c_bm + r:c_bm + r + 1], a["L2_gnn_bm"][r])
            column(cb[:, c_bu + r:c_bu + r + 1], a["L2_gnn_bu"][r])
            row(rows[:, row_bu + r, :], a["L2_gnn_bu"][r])
        row(eps1[:, :], a["L3_gnn_eps"])

        def tick(eng, name="pool_tick"):
            eng.sem_inc(S(name), 1)

        class Chain:

            def __init__(self, eng, name):
                self.eng, self.name, self.n = eng, name, 0

            def after(self, ins):
                ins.then_inc(S(self.name), 1)
                self.n += 1
                self.eng.wait_ge(S(self.name), S.at(self.name, self.n))

            def close(self):
                S.passed({self.name: self.n})
                self.n = 0

        with ExitStack() as scratch:
            def tmp(name, shape, dt=F32):
                return scratch.enter_context(nc.sbuf_tensor(name, shape, dt))

            wraw = tmp("wraw", [D, HEADS * HID])
            attb = tmp("attb", [D, 2, HEADS * HID])
            attp = tmp("attp", [D, 2, HEADS * HID])
            att4 = tmp("att4", [D, 3, HEADS])
            hi, mid, lo = (tmp(n, [128, ROWS, D], BF16) for n in ("hi", "mid", "lo"))
            rest = tmp("rest", [128, ROWS, D])
            loads.append((wraw[:, :], a["L1_gnn_W"]))
            row(attb[:, 0, :], a["L1_gnn_att_src"].rearrange("h f -> (h f)"))
            row(attb[:, 1, :], a["L1_gnn_att_dst"].rearrange("h f -> (h f)"))
            dA, sA, eA = (tmp(n, [EQ, EW], I32) for n in ("dA", "sA", "eA"))
            dN = tmp("dN", [EQ, 1], I32)
            loads.append((dA[:, :], a["dst"].rearrange("(p w) -> p w", w=EW)))
            loads.append((sA[:, :], a["src"].rearrange("(p w) -> p w", w=EW)))
            loads.append((dN[0:EQ - 1, :], a["dst"][EW:E].rearrange("(p w) -> p w", w=EW)[:, 0:1]))
            viol = tmp("viol", [EQ, EW])
            violc = tmp("violc", [EQ, 1])
            ones_f = tmp("ones_f", [128, 1])
            flag = tmp("flag", [1, 1], I32)
            pad_d, pad_z = tmp("pad_d", [1, PADS], I32), tmp("pad_z", [1, PADS], I32)
            iota_i = tmp("iota_i", [128, 128], I32)
            iota_f = tmp("iota_f", [128, 128])

            with nc.Block() as block:
                @block.sync
                def _(sp):
                    with nc.allow_non_contiguous_dma(reason="bias columns"):
                        for dst, src in loads:
                            sp.dma_start(dst, src).then_inc(S("weights"), 16)
                    sp.wait_ge(S("weights"), S.at("weights", 16 * len(loads)))

                @block.gpsimd
                def _(pool):
                    nc.gpsimd.memset(neg_half[:, :], -0.5)
                    nc.gpsimd.memset(onesc[:, :], 1.0)
                    nc.gpsimd.iota(iota_i[:, :], [[1, 128]], base=0, channel_multiplier=-1)
                    nc.gpsimd.iota(eA[:, :], [[1, EW]], base=0, channel_multiplier=EW)
                    nc.gpsimd.iota(pad_d[:, :], [[1, PADS]], base=N + E, channel_multiplier=0).then_inc(S("iotas"), 1)
                    nc.gpsimd.memset(pad_z[:, :], 0)

                @block.vector
                def _(dve):
                    ch = Chain(dve, "dve_setup")
                    nc.vector.memset(ones_bf[:, :], 1.0)
                    nc.vector.memset(zeros[:, :], 0.0)
                    nc.vector.memset(ones_f[:, :], 1.0)
                    ch.after(nc.vector.memset(viol[:, :], 0.0))
                    dve.wait_ge(S("iotas"), S.at("iotas", 1))
                    ch.after(nc.vector.tensor_copy(iota_f[:, :], iota_i[:, :]))
                    ch.after(nc.vector.tensor_scalar(ident[:, :], iota_f[:, :], 0.0, None, ALU.is_equal))
                    dve.wait_ge(S("weights"), S.at("weights", 16 * len(loads)))
                    for i in range(2):
                        ch.after(nc.vector.tensor_tensor(attp[:, i, :], wraw[:, :], attb[:, i, :], ALU.mult))
                    ch.after(nc.vector.tensor_reduce(att4[:, 0:2, :].rearrange("p i h -> p (i h)"),
                                                     attp[:, :, :].rearrange("p i (h f) -> p (i h) f", h=HEADS),
                                                     AX.X, ALU.add))
                    ch.after(nc.vector.tensor_tensor(att4[:, 2, :], att4[:, 0, :], att4[:, 1, :], ALU.add))
                    for i, w in enumerate((attS, attD, attSD)):
                        for h in range(HEADS):
                            nc.vector.tensor_copy(w[:, HC * h:HC * (h + 1)], att4[:, i, h:h + 1].to_broadcast([D, HC]))
                    ch.after(nc.vector.tensor_copy(hi[:, :, :], rows[:, :, :]))
                    ch.after(nc.vector.tensor_tensor(rest[:, :, :], rows[:, :, :], hi[:, :, :], ALU.subtract))
                    ch.after(nc.vector.tensor_copy(mid[:, :, :], rest[:, :, :]))
                    ch.after(nc.vector.tensor_tensor(lo[:, :, :], rest[:, :, :], mid[:, :, :], ALU.subtract))
                    ch.after(nc.vector.tensor_scalar(bias3[:, :, :], hi[:, :, :], ident[:, 0:1], None, ALU.mult))
                    for i, part in ((1, mid), (2, lo)):
                        ch.after(nc.vector.scalar_tensor_tensor(bias3[:, :, :], part[:, :, :], ident[:, i:i + 1],
                                                                bias3[:, :, :], ALU.mult, ALU.add))
                    ch.after(nc.vector.tensor_scalar(cu[:, :, :], rows[:, row_bu:row_bu + ROUNDS, :], 0.0, None, ALU.max))
                    ch.after(nc.vector.tensor_tensor(c_all[:, :], cu[:, 0, :], cu[:, 1, :], ALU.add))
                    for r in range(2, ROUNDS):
                        ch.after(nc.vector.tensor_tensor(c_all[:, :], c_all[:, :], cu[:, r, :], ALU.add))
                    ch.after(nc.vector.tensor_scalar(cb[:, c_bu:c_bu + ROUNDS], cb[:, c_bu:c_bu + ROUNDS], 0.0, None, ALU.max))
                    ch.after(nc.vector.memset(cb[:, c_cum:c_cum + 1], 0.0))
                    for r in range(1, ROUNDS):
                        ch.after(nc.vector.tensor_tensor(cb[:, c_cum + r:c_cum + r + 1], cb[:, c_cum + r - 1:c_cum + r],
                                                         cb[:, c_bu + r - 1:c_bu + r], ALU.add))
                    S("cum")
                    nc.vector.tensor_scalar(eps1[:, :], eps1[:, :], 1.0, None, ALU.add).then_inc(S("cum"), 1)
                    dve.wait_ge(S("cum_p"), S.at("cum_p", 1))
                    ch.after(nc.vector.tensor_tensor(cb[:, c_bm:c_bm + ROUNDS], cb[:, c_bm:c_bm + ROUNDS],
                                                     pMisc[:, 0:ROUNDS], ALU.add))
                    ch.after(nc.vector.tensor_tensor(viol[:, 0:EW - 1], dA[:, 1:EW], dA[:, 0:EW - 1], ALU.is_lt))
                    ch.after(nc.vector.tensor_tensor(viol[0:EQ - 1, EW - 1:EW], dN[0:EQ - 1, :],
                                                     dA[0:EQ - 1, EW - 1:EW], ALU.is_lt))
                    nc.vector.tensor_reduce(violc[:, :], viol[:, :], AX.X, ALU.add).then_inc(S("violc"), 1)
                    dve.wait_ge(S("viol_p"), S.at("viol_p", 1))
                    ch.after(nc.vector.tensor_copy(flag[:, :], pMisc[0:1, 8:9]))
                    ch.close()

                @block.tensor
                def _(pe):
                    pe.wait_ge(S("cum"), S.at("cum", 1))
                    for r in range(ROUNDS):
                        ins = nc.tensor.matmul(pMisc[:, r:r + 1], Wm[:, r, :], cb[:, c_cum + r:c_cum + r + 1],
                                               start=True, stop=True)
                    ins.then_inc(S("cum_p"), 1)
                    pe.wait_ge(S("violc"), S.at("violc", 1))
                    nc.tensor.matmul(pMisc[0:1, 8:9], violc[:, :], ones_f[0:EQ, :],
                                     start=True, stop=True).then_inc(S("viol_p"), 1)
            S.passed({"weights": 16 * len(loads), "iotas": 1, "cum": 1, "cum_p": 1, "violc": 1, "viol_p": 1})

            EF = E // 128
            ER = E - EF * 128
            DT_ = EF + (ER > 0)
            drow = tmp("drow", [128, E], I32)
            irow = tmp("irow", [128, E], I32)
            before_me = tmp("before_me", [128, E], BF16)
            equal_me = tmp("equal_me", [128, E], BF16)
            me = tmp("me", [128, 3, 1])
            me_i = tmp("me_i", [128, 4], I32)

            with nc.Block() as block:
                @block.sync
                def _(sp):
                    sp.dma_start(sorted_dst[E:EP + 128].rearrange("(o w) -> o w", o=1), pad_d[:, :]).then_inc(S("pads"), 16)
                    sp.dma_start(sorted_src[E:EP + 128].rearrange("(o w) -> o w", o=1), pad_z[:, :]).then_inc(S("pads"), 16)
                    sp.dma_start(sorted_edge[E:EP + 128].rearrange("(o w) -> o w", o=1), pad_z[:, :]).then_inc(S("pads"), 16)
                    sp.wait_ge(S("pads"), S.at("pads", 48))
                    unsorted = sp.value_load(flag[0:1, 0:1], min_val=0, max_val=E)
                    with sp.If(unsorted == 0):
                        for to, frm in ((sorted_dst, dA), (sorted_src, sA), (sorted_edge, eA)):
                            sp.dma_start(to[0:E].rearrange("(p w) -> p w", w=EW), frm[:, :]).then_inc(S("copied"), 16)
                        sp.wait_ge(S("copied"), S.at("copied", 48))

                @block.vector
                def _(dve):
                    unsorted = dve.value_load(flag[0:1, 0:1], min_val=0, max_val=E)
                    with dve.If(unsorted > 0):
                        dve.wait_ge(S("rank_in"), S.at("rank_in", 1))

                        def tile(t, P):
                            dve.wait_ge(S("me_in"), S.at("me_in", t + 1))
                            nc.vector.tensor_scalar(before_me[0:P, :], irow[0:P, :], me[0:P, 1, :], None,
                                                    ALU.is_lt).then_inc(S("rk0"), 1)
                            dve.wait_ge(S("rk0"), S.at("rk0", t + 1))
                            nc.vector.scalar_tensor_tensor(equal_me[0:P, :], drow[0:P, :], me[0:P, 0, :], before_me[0:P, :],
                                                           ALU.is_equal, ALU.mult).then_inc(S("rk1"), 1)
                            dve.wait_ge(S("rk1"), S.at("rk1", t + 1))
                            nc.vector.scalar_tensor_tensor(before_me[0:P, :], drow[0:P, :], me[0:P, 0, :], equal_me[0:P, :],
                                                           ALU.is_lt, ALU.add, accum_out=me[0:P, 2, :]).then_inc(S("rk2"), 1)
                            dve.wait_ge(S("rk2"), S.at("rk2", t + 1))
                            nc.vector.tensor_copy(me_i[0:P, 3:4], me[0:P, 2, :]).then_inc(S("rank"), 1)

                        with dve.Fori(0, EF) as t:
                            tile(t, 128)
                        if ER:
                            tile(EF, ER)

                @block.gpsimd
                def _(pool):
                    unsorted = pool.value_load(flag[0:1, 0:1], min_val=0, max_val=E)
                    with pool.If(unsorted > 0):
                        nc.gpsimd.iota(irow[:, :], [[1, E]], base=0, channel_multiplier=0).then_inc(S("rank_iota"), 1)
                        pool.dma_start(drow[:, :], a["dst"].partition_broadcast(128)).then_inc(S("rank_row"), 16)
                        pool.wait_ge(S("rank_iota"), S.at("rank_iota", 1))
                        pool.wait_ge(S("rank_row"), S.at("rank_row", 16))
                        nc.gpsimd.memset(me_i[:, :], 0).then_inc(S("rank_in"), 1)
                        pool.wait_ge(S("rank_in"), S.at("rank_in", 1))

                        def tile(t, P):
                            for i, frm in ((0, a["dst"]), (1, a["src"])):
                                pool.dma_start(me_i[0:P, i:i + 1],
                                               frm[bass.ds(t * 128, P)].rearrange("(p o) -> p o", o=1)).then_inc(S("me_ld"), 16)
                            pool.wait_ge(S("me_ld"), S.at("me_ld", t * 32 + 32))
                            tick(pool)
                            nc.gpsimd.tensor_copy(me[0:P, 0, :], me_i[0:P, 0:1]).then_inc(S("me_d"), 1)
                            pool.wait_ge(S("me_d"), S.at("me_d", t + 1))
                            tick(pool)
                            nc.gpsimd.tensor_copy(me_i[0:P, 2:3], pos[0:P, :]).then_inc(S("me_p"), 1)
                            pool.wait_ge(S("me_p"), S.at("me_p", t + 1))
                            tick(pool)
                            nc.gpsimd.tensor_copy(me[0:P, 1, :], me_i[0:P, 2:3]).then_inc(S("me_in"), 1)
                            pool.wait_ge(S("me_in"), S.at("me_in", t + 1))
                            nc.gpsimd.tensor_tensor(pos[:, :], pos[:, :], step128[:, :], ALU.add).then_inc(S("me_n"), 1)
                            pool.wait_ge(S("me_n"), S.at("me_n", t + 1))
                            pool.wait_ge(S("rank"), S.at("rank", t + 1))
                            tick(pool)
                            for i, to in ((0, sorted_dst), (1, sorted_src), (2, sorted_edge)):
                                nc.gpsimd.indirect_dma_start(
                                    out=to.rearrange("(n o) -> n o", o=1), in_=me_i[0:P, i:i + 1], in_offset=None,
                                    out_offset=bass.IndirectOffsetOnAxis(ap=me_i[0:P, 3:4], axis=0)).then_inc(S("me_out"), 16)
                            pool.wait_ge(S("me_out"), S.at("me_out", t * 48 + 48))

                        pos, step128 = iota_i[:, 0:1], iota_i[:, 1:2]
                        nc.gpsimd.iota(pos, [[0, 1]], base=0, channel_multiplier=1).then_inc(S("me_c"), 1)
                        nc.gpsimd.iota(step128, [[0, 1]], base=128, channel_multiplier=0).then_inc(S("me_c"), 1)
                        pool.wait_ge(S("me_c"), S.at("me_c", 2))
                        with pool.Fori(0, EF) as t:
                            tile(t, 128)
                        if ER:
                            tile(EF, ER)
            S.passed({"pads": 48})

        NP_ = next(p for p in range(128, 0, -1) if N % p == 0)
        with ExitStack() as scratch:
            def tmp(name, shape, dt=F32):
                return scratch.enter_context(nc.sbuf_tensor(name, shape, dt))

            dT, sT, eT, pT, nT = (tmp(n, [ET, 128], I32) for n in ("dT", "sT", "eT", "pT", "nT"))
            flags = tmp("flags", [ET, 6, 128])
            real = tmp("real", [ET, 128])
            keep1, count1 = tmp("keep_line", [1, EP]), tmp("count_line", [1, EP])
            one1 = tmp("one1", [1, 1])
            cols = tmp("cols", [128, 5, ET])
            row_i, far_i = tmp("row_i", [128, ET], I32), tmp("far_i", [128, ET], I32)
            row_f, far_f = tmp("row_f", [128, ET]), tmp("far_f", [128, ET])
            w0, w1 = tmp("w0", [128, ET]), tmp("w1", [128, ET])
            none = tmp("none", [NP_, N // NP_])
            pos = tmp("pos", [128, ET])
            half = tmp("half", [128, ET])
            posN = tmp("posN", [128, 4 * NG])
            own = tmp("own", [128, ET])
            U = 3
            sti = [tmp(f"sti{u}", [128, 8], I32) for u in range(U)]
            stv = [tmp(f"stv{u}", [128, 8]) for u in range(U)]
            tiles = [(sorted_dst, dT), (sorted_src, sT), (sorted_edge, eT)]

            def as_tiles(t, first=0):
                return t[first:first + EP].rearrange("(t p) -> t p", p=128)

            with nc.Block() as block:
                @block.sync
                def _(sp):
                    for frm, to in tiles:
                        sp.dma_start(to[:, :], as_tiles(frm)).then_inc(S("tiles_in"), 16)
                    sp.dma_start(nT[:, :], as_tiles(sorted_dst, 1)).then_inc(S("tiles_in"), 16)
                    sp.dma_start(pT[1:ET, :], sorted_dst[127:EP - 1].rearrange("(t p) -> t p", p=128)).then_inc(S("tiles_in"), 16)
                    sp.dma_start(pT[0:1, 1:128], sorted_dst[0:127].rearrange("(t p) -> t p", t=1)).then_inc(S("tiles_in"), 16)
                    sp.wait_ge(S("keep_ok"), S.at("keep_ok", 1))
                    sp.dma_start(as_tiles(keep_row), flags[:, 3, :]).then_inc(S("rows_io"), 16)
                    sp.wait_ge(S("rows_io"), S.at("rows_io", 16))
                    sp.dma_start(keep1[:, :], keep_row.rearrange("(o w) -> o w", o=1)).then_inc(S("rows_io"), 16)
                    sp.wait_ge(S("rows_io"), S.at("rows_io", 32))
                    sp.nop().then_inc(S("keep1_in"), 1)
                    sp.wait_ge(S("count_ok"), S.at("count_ok", 1))
                    sp.dma_start(count_row.rearrange("(o w) -> o w", o=1), count1[:, :]).then_inc(S("rows_io"), 16)
                    sp.wait_ge(S("rows_io"), S.at("rows_io", 48))
                    sp.dma_start(flags[:, 5, :], as_tiles(count_row)).then_inc(S("rows_io"), 16)
                    sp.wait_ge(S("none_ok"), S.at("none_ok", 1))
                    sp.dma_start(node_slot.rearrange("(p w) -> p w", p=NP_), none[:, :]).then_inc(S("none_out"), 16)
                    sp.wait_ge(S("rows_io"), S.at("rows_io", 64))
                    sp.wait_ge(S("none_out"), S.at("none_out", 16))

                @block.gpsimd
                def _(pool):
                    nc.gpsimd.iota(row_i[:, :], [[GC, EG], [1, 4]], base=0, channel_multiplier=4)
                    nc.gpsimd.iota(far_i[:, :], [[128, ET]], base=N, channel_multiplier=1).then_inc(S("slot_iotas"), 1)
                    nc.gpsimd.memset(half[:, :], -0.5)

                @block.vector
                def _(dve):
                    ch = Chain(dve, "dve_setup")
                    nc.vector.memset(pT[0:1, 0:1], -1).then_inc(S("first_prev"), 1)
                    nc.vector.memset(one1[:, :], 1.0)
                    nc.vector.memset(none[:, :], -1.0).then_inc(S("none_ok"), 1)
                    dve.wait_ge(S("slot_iotas"), S.at("slot_iotas", 1))
                    nc.vector.tensor_copy(row_f[:, :], row_i[:, :])
                    nc.vector.tensor_copy(far_f[:, :], far_i[:, :])
                    dve.wait_ge(S("first_prev"), S.at("first_prev", 1))
                    dve.wait_ge(S("tiles_in"), S.at("tiles_in", 96))
                    nc.vector.tensor_tensor(flags[:, 3, :], dT[:, :], pT[:, :], ALU.is_equal).then_inc(S("keep_ok"), 1)
                    for i, t in enumerate((dT, sT, eT)):
                        nc.vector.tensor_copy(flags[:, i, :], t[:, :])
                    nc.vector.tensor_scalar(real[:, :], dT[:, :], float(N), None, ALU.is_lt)
                    ch.after(nc.vector.tensor_tensor(flags[:, 4, :], dT[:, :], nT[:, :], ALU.not_equal))
                    ch.after(nc.vector.tensor_tensor(flags[:, 4, :], flags[:, 4, :], real[:, :], ALU.mult))
                    dve.wait_ge(S("keep1_in"), S.at("keep1_in", 1))
                    nc.vector.tensor_tensor_scan(count1[:, :], keep1[:, :], one1[:, 0:1].to_broadcast([1, EP]), 0.0,
                                                 ALU.mult, ALU.add).then_inc(S("count_ok"), 1)
                    dve.wait_ge(S("flags_p"), S.at("flags_p", 1))
                    ch.after(nc.vector.tensor_copy(cols[:, 0:4, :], pMisc[:, 0:4 * ET].rearrange("p (i t) -> p i t", i=4)))
                    ch.after(nc.vector.tensor_copy(cols[:, 4, :], pGram[:, 0:ET]))
                    nc.vector.tensor_copy(src_i[:, :], cols[:, 1, :])
                    nc.vector.tensor_copy(edge_i[:, :], cols[:, 2, :])
                    nc.vector.tensor_copy(last[:, :], cols[:, 3, :])
                    ch.after(nc.vector.tensor_scalar(w0[:, :], cols[:, 0, :], float(N), None, ALU.is_lt))
                    ch.after(nc.vector.tensor_tensor(dst_g[:, :], w0[:, :], cols[:, 0, :], ALU.mult))
                    ch.after(nc.vector.tensor_tensor(w0[:, :], cols[:, 0, :], far_f[:, :], ALU.subtract))
                    ch.after(nc.vector.tensor_tensor(w0[:, :], w0[:, :], cols[:, 3, :], ALU.mult))
                    ch.after(nc.vector.tensor_tensor(dst_s[:, :], w0[:, :], far_f[:, :], ALU.add))
                    ch.after(nc.vector.tensor_scalar(cols[:, 4, :], cols[:, 4, :], 1.0, None, ALU.add))
                    ch.close()

                @block.tensor
                def _(pe):
                    pe.wait_ge(S("count_ok"), S.at("count_ok", 1))
                    pe.wait_ge(S("rows_io"), S.at("rows_io", 64))
                    for at, i in enumerate((0, 1, 2, 4)):
                        nc.tensor.transpose(pMisc[:, at * ET:(at + 1) * ET], flags[:, i, :], ident[0:ET, 0:ET])
                    nc.tensor.transpose(pGram[:, 0:ET], flags[:, 5, :], ident[0:ET, 0:ET]).then_inc(S("flags_p"), 1)
            S.passed({"tiles_in": 96, "keep_ok": 1, "rows_io": 64, "none_out": 16, "keep1_in": 1, "count_ok": 1, "none_ok": 1,
                      "slot_iotas": 1, "first_prev": 1, "flags_p": 1})

            with nc.Block() as block:
                @block.gpsimd
                def _(pool):
                    nc.gpsimd.tensor_tensor(dinv[:, :], cols[:, 4, :], half[:, :], ALU.pow)

                    def scatter_group(k, u, r):
                        if r is not None:
                            pool.wait_ge(S(f"ns_out{u}"), r)
                            tick(pool)
                        nc.gpsimd.tensor_copy(sti[u][:, 0:4], dst_s[:, bass.ds(4 * k, 4)])
                        nc.gpsimd.tensor_copy(stv[u][:, 0:4], row_f[:, bass.ds(4 * k, 4)]).then_inc(S("ns_in"), 1)
                        pool.wait_ge(S("ns_in"), k + 1)
                        tick(pool)
                        for j in range(4):
                            nc.gpsimd.indirect_dma_start(
                                out=node_slot.rearrange("(n o) -> n o", o=1), in_=stv[u][:, j:j + 1], in_offset=None,
                                out_offset=bass.IndirectOffsetOnAxis(ap=sti[u][:, j:j + 1], axis=0),
                                bounds_check=N - 1, oob_is_err=False).then_inc(S(f"ns_out{u}"), 16)

                    for k in range(min(U, EG)):
                        scatter_group(k, k, None)
                    if EG // U > 1:
                        with pool.Fori(1, EG // U) as b:
                            for u in range(U):
                                scatter_group(b * U + u, u, b * 64)
                    for k in range(max(U, EG // U * U), EG):
                        scatter_group(k, k % U, k // U * 64)
                    for u in range(U):
                        pool.wait_ge(S(f"ns_out{u}"), 64 * len(range(u, EG, U)))
            S.passed({"ns_in": EG})

            with nc.Block() as block:
                @block.sync
                def _(sp):
                    with nc.allow_non_contiguous_dma(reason="a node's slot for each row of a group"):
                        sp.dma_start(posN[:, 0:4 * NF].rearrange("p (g j) -> p g j", j=4),
                                     node_slot[0:NF * GC].rearrange("(g p j) -> p g j", p=128, j=4)).then_inc(S("pos_n"), 16)
                        if R:
                            sp.dma_start(posN[0:TP, 4 * NF:4 * NF + TJ],
                                         node_slot[NF * GC:N].rearrange("(p j) -> p j", j=TJ)).then_inc(S("pos_n"), 16)

                @block.gpsimd
                def _(pool):
                    def gather_group(k, u, r):
                        if r is not None:
                            pool.wait_ge(S("pg_kept"), k - U + 1)
                        nc.gpsimd.tensor_copy(sti[u][:, 4:8], dst_g[:, bass.ds(4 * k, 4)])
                        nc.gpsimd.tensor_copy(sti[u][:, 0:4], src_i[:, bass.ds(4 * k, 4)]).then_inc(S("pg_in"), 1)
                        pool.wait_ge(S("pg_in"), k + 1)
                        tick(pool)
                        for j in range(8):
                            nc.gpsimd.indirect_dma_start(
                                out=stv[u][:, j:j + 1], out_offset=None, in_=node_slot.rearrange("(n o) -> n o", o=1),
                                in_offset=bass.IndirectOffsetOnAxis(ap=sti[u][:, j:j + 1], axis=0)).then_inc(S(f"pg_out{u}"), 16)

                    def keep_group(k, u, n):
                        pool.wait_ge(S(f"pg_out{u}"), n)
                        nc.gpsimd.tensor_copy(pos[:, bass.ds(4 * k, 4)], stv[u][:, 0:4])
                        nc.gpsimd.tensor_copy(own[:, bass.ds(4 * k, 4)], stv[u][:, 4:8]).then_inc(S("pg_kept"), 1)

                    for k in range(min(U, EG)):
                        gather_group(k, k, None)
                    if EG // U > 1:
                        with pool.Fori(1, EG // U) as b:
                            for u in range(U):
                                keep_group(b * U + u - U, u, b * 128)
                                gather_group(b * U + u, u, b)
                    for k in range(max(U, EG // U * U), EG):
                        keep_group(k - U, k % U, k // U * 128)
                        gather_group(k, k % U, k // U)
                    for k in range(max(0, EG - U), EG):
                        keep_group(k, k % U, (k // U + 1) * 128)
            with nc.Block() as block:
                @block.vector
                def _(dve):
                    ch = Chain(dve, "dve_setup")
                    nc.vector.tensor_scalar(w0[:, :], row_f[:, :], float(EP), None, ALU.add)
                    ch.after(nc.vector.tensor_scalar(w1[:, :], pos[:, :], 0.0, None, ALU.is_ge))
                    ch.after(nc.vector.tensor_tensor(pos[:, :], pos[:, :], w0[:, :], ALU.subtract))
                    ch.after(nc.vector.tensor_tensor(pos[:, :], pos[:, :], w1[:, :], ALU.mult))
                    ch.after(nc.vector.tensor_tensor(idx[:, :], pos[:, :], w0[:, :], ALU.add))
                    ch.after(nc.vector.tensor_scalar(idx_own[:, :], own[:, :], 0.0, None, ALU.max))
                    dve.wait_ge(S("pos_n"), 16 + 16 * (R > 0))
                    nc.vector.tensor_scalar(nmask[:, 0:4 * NF], posN[:, 0:4 * NF], 0.0, eps1[:, 0:1], ALU.is_lt, ALU.mult)
                    if R:
                        nc.vector.tensor_scalar(nmask[0:TP, 4 * NF:4 * NF + TJ], posN[0:TP, 4 * NF:4 * NF + TJ], 0.0,
                                                eps1[0:TP, 0:1], ALU.is_lt, ALU.mult)
                    ch.after(nc.vector.memset(ystat[:, 0, :], 0.0))
                    ch.close()

        for u in range(MOST):
            S(f"gathered{u}")
            S(f"scattered{u}")
        S.retire(["weights", "iotas", "cum", "cum_p", "violc", "viol_p", "pads", "tiles_in", "keep_ok", "rows_io",
                  "none_out", "keep1_in", "count_ok", "none_ok", "slot_iotas", "first_prev", "flags_p", "ns_in"])

        phases = 0
        held = ctx.enter_context(ExitStack())
        SHAPES = {"A": [128, GC + 1], "Mx": [128, GC + 1], "Sc0": [128, GC + 1], "Sc1": [128, GC + 1],
                  "keep": [128, GC], "soft": [128, 3, GC], "zm": [128, 4, D + 1], "st": [128, 4, 6],
                  "mv": [128, 4, 2], "vpe": [128, 4], "rstd": [128, 4], "idxs": [128, 8], "G": [128, 4, D], "G2": [128, 4, D],
                  "Dn": [128, 4, D], "O": [128, 4, D], **{f"t{i}": [128, GC] for i in range(8)}}
        buffers = {name: [] for name in SHAPES}
        G, G2, Dn, O, keep, soft, zm = (buffers[n] for n in ("G", "G2", "Dn", "O", "keep", "soft", "zm"))
        A, Mx, Sc0, Sc1 = (buffers[n] for n in ("A", "Mx", "Sc0", "Sc1"))
        st, mv, vpe, rstd, idxs = (buffers[n] for n in ("st", "mv", "vpe", "rstd", "idxs"))
        t0, t1, t2, t3, t4, t5, t6, t7 = (buffers[f"t{i}"] for i in range(8))
        pA, pB = [], []

        def in_flight(n, banks, names):
            nonlocal U, phases
            U, phases = n, phases + 1
            pA[:] = psum[0:n]
            pB[:] = psum[0:n] if banks == 1 else psum[n:2 * n]
            held.close()
            names = names.split() + ["st", "mv", "vpe", "rstd", "idxs"]
            for name in buffers:
                buffers[name][:] = [held.enter_context(nc.sbuf_tensor(
                    f"{name}_{phases}_{u}", SHAPES[name], I32 if name == "idxs" else F32))
                    for u in range(n)] if name in names else []
            with nc.Block() as block:
                @block.vector
                def _(dve):
                    for name in ("A", "Mx", "Sc0", "Sc1"):
                        if name in names:
                            nc.vector.memset(buffers[name][n - 1][:, :], 0.0)
                    for z in zm:
                        nc.vector.memset(z[:, :, :], 1.0)

        def nm(t):
            return t[:, 0:GC].rearrange("p (j d) -> p j d", j=4)

        def shape(k, dense=True):
            return (TP, TJ) if dense and isinstance(k, int) and k >= NF else (128, 4)

        def steps(eng, steps_n, groups, stage, *loads):
            nb = -(-groups // U)

            def body(b):
                for s in range(steps_n):
                    for u in range(U):
                        t = s - u * steps_n // U
                        back = 1 if t < 0 else 0
                        k, r = b * U + (u - U * back), b - back
                        if isinstance(k, int) and not 0 <= k < groups:
                            continue
                        step = t + steps_n * back
                        if stage:
                            stage(step, u, k, r)
                        for ahead, load in loads:
                            if step == ahead and not (isinstance(k, int) and k + U >= groups):
                                load(u, k + U, r + 1)

            for k in range(min(U, groups)):
                for _, load in loads:
                    load(k, k, 0)
            if nb >= 4:
                body(0)
                with eng.Fori(1, nb - 2) as b:
                    body(b)
                for b in range(nb - 2, nb + 1):
                    body(b)
            else:
                for b in range(nb + 1):
                    body(b)



        def fresh(k):
            return isinstance(k, int) and k < U

        def finish(groups, engine, **dma):
            tot = dict.fromkeys(engine, groups)
            for name, per in dma.items():
                for u in range(U):
                    tot[f"{name}{u}"] = per * len(range(u, groups, U))
            S.passed(tot)


        CREDITED = {"biased_rows": "vector", "scaled_rows": "scalar", "state_rows": "scalar", "state_updated": "vector", "segments_summed": "vector",
                    "update_rows": "scalar", "messages": "scalar", "cols_psum": "tensor", "z_masked": "gpsimd", "y_moments": "vector", "loop_added": "vector",
                    "residual1": "vector", "residual3": "vector"}

        def transposes(src, bank, P=128, J=4):
            for j in range(J):
                ins = nc.tensor.transpose(bank[:, j * P:(j + 1) * P], src[0:P, j, :], ident[0:P, 0:P])
            return ins

        def back_transposes(cols, bank, P=128, J=4):
            for j in range(J):
                ins = nc.tensor.transpose(bank[0:P, j * D:(j + 1) * D], cols[:, j * P:(j + 1) * P], ident[:, :])
            return ins

        def to_node_major(bank, parts, P=128, J=4, row=None):
            if row is not None:
                for j in range(J):
                    nc.tensor.matmul(bank[0:P, j * D:(j + 1) * D], ones_bf[:, 0:P], bias3[:, row, :],
                                     start=(j == 0), stop=False, skip_group_check=True)
            for j in range(J):
                for i, (cols, w) in enumerate(parts):
                    ins = nc.tensor.matmul(bank[0:P, j * D:(j + 1) * D], cols[:, j * P:(j + 1) * P], w,
                                           start=(row is None and j == 0 and i == 0),
                                           stop=(i == len(parts) - 1), skip_group_check=True)
            return ins

        def feature_major(bank, parts, C=GC):
            for i, (cols, w) in enumerate(parts):
                ins = nc.tensor.matmul(bank[:, 0:C], w, cols[:, 0:C], start=(i == 0), stop=(i == len(parts) - 1))
            return ins

        def stats(dve, u, k, P, J, src, tag):
            dve.wait_ge(S(f"residual{tag}"), S.at(f"residual{tag}", k + 1))
            for j in range(J):
                ins = nc.vector.bn_stats(st[u][0:P, j, :], src[0:P, j, :])
            ins.then_inc(S(f"moments{tag}"), 1)
            dve.wait_ge(S(f"moments{tag}"), S.at(f"moments{tag}", k + 1))
            tick(dve, "vector_tick")
            for j in range(J):
                ins = nc.vector.bn_aggr(mv[u][0:P, j, :], st[u][0:P, j, :])
            ins.then_inc(S(f"variance{tag}"), 1)
            dve.wait_ge(S(f"variance{tag}"), S.at(f"variance{tag}", k + 1))
            nc.vector.tensor_scalar(vpe[u][0:P, 0:J], mv[u][0:P, 0:J, 1], LN_EPS, None,
                                    ALU.add).then_inc(S(f"var_eps{tag}"), 1)

        def inv_std(pool, u, k, P, J, tag):
            pool.wait_ge(S(f"var_eps{tag}"), S.at(f"var_eps{tag}", k + 1))
            nc.gpsimd.tensor_tensor(rstd[u][0:P, 0:J], vpe[u][0:P, 0:J], neg_half[0:P, 0:J],
                                    ALU.pow).then_inc(S(f"inv_std{tag}"), 1)

        def normalise(dve, u, k, P, J, src, dst, tag):
            dve.wait_ge(S(f"inv_std{tag}"), S.at(f"inv_std{tag}", k + 1))
            for j in range(J):
                ins = nc.vector.tensor_scalar(dst[0:P, j, :], src[0:P, j, :], mv[u][0:P, j, 0:1],
                                              rstd[u][0:P, j:j + 1], ALU.subtract, ALU.mult)
            ins.then_inc(S(f"normed{tag}"), 1)

        def ln_signals(*tags):
            return [f"{n}{t}" for t in tags for n in ("residual", "moments", "variance", "var_eps", "inv_std", "normed")]

        def scan(dst, d0, d1, before, op0, op1):
            return nc.vector.tensor_tensor_scan(dst[:, 1:GC + 1], d0, d1, before[:, GC:GC + 1], op0, op1)

        def gather(pool, u, k, cols, table, dst, at):
            nc.gpsimd.tensor_copy(idxs[u][:, at:at + 4], cols[:, bass.ds(4 * k, 4)]).then_inc(S(f"indices{at}"), 1)
            pool.wait_ge(S(f"indices{at}"), S.at(f"indices{at}", k + 1))
            tick(pool)
            for j in range(4):
                nc.gpsimd.indirect_dma_start(
                    out=dst[u][:, j, :], out_offset=None, in_=table,
                    in_offset=bass.IndirectOffsetOnAxis(ap=idxs[u][:, at + j:at + j + 1], axis=0),
                ).then_inc(S(f"gathered{u}"), 16)

        def scatter(pool, u, k, src, table):
            nc.gpsimd.tensor_copy(idxs[u][:, 0:4], dst_s[:, bass.ds(4 * k, 4)]).then_inc(S("indices0"), 1)
            pool.wait_ge(S("indices0"), S.at("indices0", k + 1))
            tick(pool)
            for j in range(4):
                nc.gpsimd.indirect_dma_start(
                    out=table, in_=src[u][:, j, :], in_offset=None,
                    out_offset=bass.IndirectOffsetOnAxis(ap=idxs[u][:, j:j + 1], axis=0),
                    bounds_check=N - 1, oob_is_err=False).then_inc(S(f"scattered{u}"), 16)

        def slot_rows(t, k, half=0):
            return t[bass.ds(k * GC + half * EP, GC), :].rearrange("(p j) d -> p j d", j=4)

        def node_rows(t, k):
            P, J = shape(k)
            return t[bass.ds(k * GC, P * J), :].rearrange("(p j) d -> p j d", j=J)

        def keep_cols(k):
            return keep_row[bass.ds(k * GC, GC)].partition_broadcast(128)

        with nc.Block() as block:
            @block.vector
            def _(dve):
                for name, owner in CREDITED.items():
                    if owner == "vector":
                        dve.nop().then_inc(S(name), MOST)

            @block.scalar
            def _(act):
                for name, owner in CREDITED.items():
                    if owner == "scalar":
                        act.nop().then_inc(S(name), MOST)

            @block.gpsimd
            def _(pool):
                for name, owner in CREDITED.items():
                    if owner == "gpsimd":
                        pool.nop().then_inc(S(name), MOST)

            @block.tensor
            def _(pe):
                for name, owner in CREDITED.items():
                    if owner == "tensor":
                        pe.nop().then_inc(S(name), MOST)
        S.passed({name: MOST for name in CREDITED})

        def chain(groups, dense):
            n_steps = 15 if dense else 12
            per_store = 16 if dense else 16 * 5

            def sp_load(u, k, r):
                if not fresh(k):
                    sp_.wait_ge(S("residual1"), S.at("residual1", k + 1 - U))
                P, J = shape(k)
                sp_.dma_start(G[u][0:P, 0:J, :], node_rows(a["x"], k)).then_inc(S(f"loaded{u}"), 16)

            def pool_load(u, k, r):
                if not fresh(k):
                    pool_.wait_ge(S("residual1"), S.at("residual1", k + 1 - U))
                    pool_.wait_ge(S(f"kept{u}"), S.at(f"kept{u}", (r - 1 + 1) * 16))
                gather(pool_, u, k, src_i, a["x"], G, 0)

            def arrived(eng, u, r):
                eng.wait_ge(S(f"loaded{u}"), S.at(f"loaded{u}", (r + 1) * 16)) if dense else eng.wait_ge(S(f"gathered{u}"), S.at(f"gathered{u}", (r + 1) * 64))

            with nc.Block() as block:
                @block.sync
                def _(sp):
                    nonlocal sp_
                    sp_ = sp

                    def stage(s, u, k, r):
                        if dense and s == 12:
                            P, J = shape(k)
                            sp.wait_ge(S("normed3"), S.at("normed3", k + 1))
                            sp.dma_start(node_rows(x3_nodes, k), O[u][0:P, 0:J, :]).then_inc(S(f"stored{u}"), 16)
                        if not dense:
                            if s == 0:
                                sp.wait_ge(S(f"gathered{u}"), S.at(f"gathered{u}", (r + 1) * 64))
                                sp.dma_start(slot_rows(gcn_table[0], k, 1), G[u][:, :, :]).then_inc(S(f"kept{u}"), 16)
                            elif s == 2:
                                sp.wait_ge(S("h1_rows"), S.at("h1_rows", k + 1))
                                sp.dma_start(slot_rows(gcn_table[1], k, 1), O[u][:, :, :]).then_inc(S(f"stored{u}"), 16)
                            elif s == 3:
                                sp.wait_ge(S("h2_rows"), S.at("h2_rows", k + 1))
                                sp.dma_start(slot_rows(gcn_table[2], k, 1), G2[u][:, :, :]).then_inc(S(f"stored{u}"), 16)
                            elif s == 4:
                                sp.wait_ge(S("normed1"), S.at("normed1", k + 1))
                                sp.dma_start(slot_rows(gat_table, k, 1), nm(t4[u])).then_inc(S(f"stored{u}"), 16)
                            elif s == 11:
                                sp.wait_ge(S("state_rows"), S.at("state_rows", k + 1))
                                for t in mpn_table:
                                    sp.dma_start(slot_rows(t, k, 1), Dn[u][:, :, :]).then_inc(S(f"stored{u}"), 16)

                    steps(sp, n_steps, groups, stage, *([(3, sp_load)] if dense else []))
                    for u in range(min(U, groups)):
                        sp.wait_ge(S(f"stored{u}"), S.at(f"stored{u}", per_store * len(range(u, groups, U))))
                    if not dense:
                        for u in range(U):
                            if groups > u:
                                sp.wait_ge(S(f"kept{u}"), S.at(f"kept{u}", (len(range(u, groups, U)) - 1 + 1) * 16))

                @block.gpsimd
                def _(pool):
                    nonlocal pool_
                    pool_ = pool

                    def stage(s, u, k, r):
                        P, J = shape(k, dense)
                        if s == 3:
                            inv_std(pool, u, k, P, J, 1)
                        elif s == 8:
                            inv_std(pool, u, k, P, J, 2)
                        elif s == 10 and dense:
                            pool.wait_ge(S("normed2"), S.at("normed2", k + 1))
                            nc.gpsimd.tensor_tensor(nm(t4[u])[0:P, 0:J, :], nm(t5[u])[0:P, 0:J, :],
                                                    c_all[0:P, :].unsqueeze(1).to_broadcast([P, J, D]),
                                                    ALU.add).then_inc(S("x2_with_gains"), 1)
                        elif s == 11 and dense:
                            inv_std(pool, u, k, P, J, 3)
                        elif s == 13:
                            pool.wait_ge(S("normed3"), S.at("normed3", k + 1))
                            nc.gpsimd.tensor_tensor(zm[u][0:P, 0:J, 0:D], O[u][0:P, 0:J, :],
                                                    nmask[0:P, bass.ds(4 * k, J)].unsqueeze(2).to_broadcast([P, J, D]),
                                                    ALU.mult).then_inc(S("z_masked"), 1)

                    steps(pool, n_steps, groups, stage, *([] if dense else [(3, pool_load)]))

                @block.tensor
                def _(pe):
                    def stage(s, u, k, r):
                        P, J = shape(k, dense)
                        C = P * J
                        if s == 0:
                            arrived(pe, u, r)
                            if not fresh(k):
                                pe.wait_ge(S("residual3" if dense else "state_rows"),
                                           S.at("residual3" if dense else "state_rows", k + 1 - U))
                            transposes(G[u], pA[u], P, J).then_inc(S("x_transposed"), 1)
                        elif s == 1:
                            pe.wait_ge(S("x_cols"), S.at("x_cols", k + 1))
                            feature_major(pB[u], [(t0[u], W0[:, :])], C).then_inc(S("h1_product"), 1)
                        elif s == 2:
                            pe.wait_ge(S("h1_cols"), S.at("h1_cols", k + 1))
                            if not dense:
                                back_transposes(t1[u], pB[u]).then_inc(S("h1_back"), 1)
                            feature_major(pA[u], [(t1[u], W1[:, :])], C).then_inc(S("h2_product"), 1)
                        elif s == 3:
                            pe.wait_ge(S("h2_cols"), S.at("h2_cols", k + 1))
                            if not dense:
                                back_transposes(t2[u], pA[u]).then_inc(S("h2_back"), 1)
                                pe.wait_ge(S("h1_rows"), S.at("h1_rows", k + 1))
                            to_node_major(pB[u], [(t2[u], W2[:, :])], P, J, row_b2).then_inc(S("h3_product"), 1)
                        elif s == 5:
                            pe.wait_ge(S("normed1"), S.at("normed1", k + 1))
                            transposes(nm(t4[u]), pA[u], P, J).then_inc(S("x1_transposed"), 1)
                        elif s == 6:
                            pe.wait_ge(S("x1_cols"), S.at("x1_cols", k + 1))
                            feature_major(pB[u], [(t0[u], Wg[:, 0, :])], C).then_inc(S("head_product0"), 1)
                        elif s == 7:
                            pe.wait_ge(S("head_relu0"), S.at("head_relu0", k + 1))
                            feature_major(pA[u], [(t0[u], Wg[:, 1, :])], C).then_inc(S("head_product1"), 1)
                        elif s == 8:
                            pe.wait_ge(S("head_relu1"), S.at("head_relu1", k + 1))
                            to_node_major(pB[u], [(t1[u], fcw[:, 0, :]), (t2[u], fcw[:, 1, :])], P, J,
                                          row_fc).then_inc(S("gat_product"), 1)
                        elif s == 10:
                            pe.wait_ge(S("normed2"), S.at("normed2", k + 1))
                            transposes(nm(t5[u]), pA[u], P, J).then_inc(S("x2_transposed"), 1)
                        elif s == 11:
                            pe.wait_ge(S("x2_cols"), S.at("x2_cols", k + 1))
                            to_node_major(pB[u], [(t0[u], Wi[:, :])], P, J, row_bi).then_inc(S("state_product"), 1)
                        elif s == 14:
                            pe.wait_ge(S("z_masked"), S.at("z_masked", k + 1))
                            for j in range(J):
                                nc.tensor.matmul(pGram[:, 0:D + 1], zm[u][0:P, j, 0:D], zm[u][0:P, j, :],
                                                 start=False, stop=False, skip_group_check=True)

                    steps(pe, n_steps, groups, stage)

                @block.scalar
                def _(act):
                    def relu(out_, in_, bias=0.0):
                        return nc.scalar.activation(out_, in_, ACTF.Relu, bias=bias)

                    def stage(s, u, k, r):
                        P, J = shape(k, dense)
                        C = P * J
                        if s == 0:
                            act.wait_ge(S("x_transposed"), S.at("x_transposed", k + 1))
                            nc.scalar.copy(t0[u][:, 0:C], pA[u][:, 0:C]).then_inc(S("x_cols"), 1)
                        elif s == 1:
                            act.wait_ge(S("h1_product"), S.at("h1_product", k + 1))
                            relu(t1[u][:, 0:C], pB[u][:, 0:C], cb[:, c_b0:c_b0 + 1]).then_inc(S("h1_cols"), 1)
                        elif s == 2:
                            act.wait_ge(S("h2_product"), S.at("h2_product", k + 1))
                            relu(t2[u][:, 0:C], pA[u][:, 0:C], cb[:, c_b1:c_b1 + 1]).then_inc(S("h2_cols"), 1)
                        elif s == 5:
                            act.wait_ge(S("x1_transposed"), S.at("x1_transposed", k + 1))
                            nc.scalar.copy(t0[u][:, 0:C], pA[u][:, 0:C]).then_inc(S("x1_cols"), 1)
                        elif s == 6:
                            act.wait_ge(S("head_product0"), S.at("head_product0", k + 1))
                            relu(t1[u][:, 0:C], pB[u][:, 0:C], cb[:, c_gat:c_gat + 1]).then_inc(S("head_relu0"), 1)
                        elif s == 7:
                            act.wait_ge(S("head_product1"), S.at("head_product1", k + 1))
                            relu(t2[u][:, 0:C], pA[u][:, 0:C], cb[:, c_gat + 1:c_gat + 2]).then_inc(S("head_relu1"), 1)
                        elif s == 10:
                            act.wait_ge(S("x2_transposed"), S.at("x2_transposed", k + 1))
                            nc.scalar.copy(t0[u][:, 0:C], pA[u][:, 0:C]).then_inc(S("x2_cols"), 1)
                        elif s == 11 and not dense:
                            act.wait_ge(S("state_product"), S.at("state_product", k + 1))
                            if not fresh(k):
                                act.wait_ge(S(f"stored{u}"), S.at(f"stored{u}", r * per_store))
                            relu(Dn[u][:, :, :], nm(pB[u])).then_inc(S("state_rows"), 1)

                    steps(act, n_steps, groups, stage)

                @block.vector
                def _(dve):
                    def stage(s, u, k, r):
                        P, J = shape(k, dense)
                        if s == 2 and not dense:
                            dve.wait_ge(S("h1_back"), S.at("h1_back", k + 1))
                            if not fresh(k):
                                dve.wait_ge(S(f"stored{u}"), S.at(f"stored{u}", r * per_store))
                            nc.vector.tensor_copy(O[u][:, :, :], nm(pB[u])).then_inc(S("h1_rows"), 1)
                        if s == 3:
                            if not dense:
                                dve.wait_ge(S("h2_back"), S.at("h2_back", k + 1))
                                nc.vector.tensor_copy(G2[u][:, :, :], nm(pA[u])).then_inc(S("h2_rows"), 1)
                            dve.wait_ge(S("h3_product"), S.at("h3_product", k + 1))
                            arrived(dve, u, r)
                            nc.vector.scalar_tensor_tensor(nm(t3[u])[0:P, 0:J, :], G[u][0:P, 0:J, :], 2.0,
                                                           nm(pB[u])[0:P, 0:J, :], ALU.mult,
                                                           ALU.add).then_inc(S("residual1"), 1)
                            stats(dve, u, k, P, J, nm(t3[u]), 1)
                        elif s == 4:
                            normalise(dve, u, k, P, J, nm(t3[u]), nm(t4[u]), 1)
                        elif s == 8:
                            dve.wait_ge(S("gat_product"), S.at("gat_product", k + 1))
                            dve.wait_ge(S("normed1"), S.at("normed1", k + 1))
                            nc.vector.tensor_tensor(nm(t3[u])[0:P, 0:J, :], nm(t4[u])[0:P, 0:J, :],
                                                    nm(pB[u])[0:P, 0:J, :], ALU.add).then_inc(S("residual2"), 1)
                            stats(dve, u, k, P, J, nm(t3[u]), 2)
                        elif s == 9:
                            normalise(dve, u, k, P, J, nm(t3[u]), nm(t5[u]), 2)
                        elif s == 11 and dense:
                            dve.wait_ge(S("state_product"), S.at("state_product", k + 1))
                            dve.wait_ge(S("x2_with_gains"), S.at("x2_with_gains", k + 1))
                            nc.vector.scalar_tensor_tensor(nm(t3[u])[0:P, 0:J, :], nm(pB[u])[0:P, 0:J, :], 0.0,
                                                           nm(t4[u])[0:P, 0:J, :], ALU.max,
                                                           ALU.add).then_inc(S("residual3"), 1)
                            stats(dve, u, k, P, J, nm(t3[u]), 3)
                        elif s == 12:
                            if not fresh(k):
                                dve.wait_ge(S(f"stored{u}"), S.at(f"stored{u}", r * per_store))
                            normalise(dve, u, k, P, J, nm(t3[u]), O[u], 3)

                    steps(dve, n_steps, groups, stage)

            names = ["x_transposed", "x_cols", "h1_product", "h1_cols", "h2_product", "h2_cols", "h3_product", "x1_transposed", "x1_cols", "head_product0", "head_product1", "head_relu0", "head_relu1", "gat_product",
                     "x2_transposed", "x2_cols", "state_product"] + ln_signals(1, 2)
            if dense:
                finish(groups, names + ln_signals(3) + ["x2_with_gains", "z_masked"], loaded=16, stored=16)
            else:
                finish(groups, names + ["h1_back", "h2_back", "h1_rows", "h2_rows", "state_rows", "indices0"], gathered=64,
                       kept=16, stored=per_store)

        sp_ = pool_ = None
        in_flight(4, 2, "G G2 Dn O t0 t1 t2 t3 t4 t5")
        chain(EG, False)

        with nc.Block() as block:
            @block.sync
            def _(sp):
                def stage(s, u, k, r):
                    sp.wait_ge(S("scaled_rows"), S.at("scaled_rows", k + 1))
                    sp.dma_start(slot_rows(x0_slots, k), G[u][:, :, :]).then_inc(S(f"stored{u}"), 16)
                    sp.dma_start(slot_rows(gcn_table[0], k), O[u][:, :, :]).then_inc(S(f"stored{u}"), 16)

                steps(sp, 1, EG, stage)
                for u in range(min(U, EG)):
                    sp.wait_ge(S(f"stored{u}"), S.at(f"stored{u}", 32 * len(range(u, EG, U))))

            @block.gpsimd
            def _(pool):
                def load(u, k, r):
                    if not fresh(k):
                        if not fresh(k):
                            pool.wait_ge(S(f"stored{u}"), S.at(f"stored{u}", r * 32))
                    gather(pool, u, k, dst_g, a["x"], G, 0)

                steps(pool, 1, EG, None, (0, load))

            @block.scalar
            def _(act):
                def stage(s, u, k, r):
                    act.wait_ge(S(f"gathered{u}"), S.at(f"gathered{u}", (r + 1) * 64))
                    if not fresh(k):
                        act.wait_ge(S(f"stored{u}"), S.at(f"stored{u}", r * 32))
                    for j in range(4):
                        ins = nc.scalar.activation(O[u][:, j, :], G[u][:, j, :], ACTF.Copy,
                                                   scale=dinv[:, bass.ds(4 * k + j, 1)])
                    ins.then_inc(S("scaled_rows"), 1)

                steps(act, 1, EG, stage)
        finish(EG, ["scaled_rows", "indices0"], gathered=64, stored=32)

        def gcn_layer(i):
            final = i == 2
            W = (W0, W1, W2)[i]
            row_b = (rowb0[:, :], rowb1[:, :], rows[:, row_b2, :])[i]
            per_load = 48 if final else 32
            n_steps = 3 if final else 2

            with nc.Block() as block:
                @block.sync
                def _(sp):
                    def load(u, k, r):
                        if not fresh(k) and final:
                            sp.wait_ge(S("residual1"), S.at("residual1", k + 1 - U))
                        if not fresh(k) and not final:
                            sp.wait_ge(S("loop_added"), S.at("loop_added", k + 1 - U))
                        sp.dma_start(Dn[u][:, :, :], slot_rows(gcn_table[i], k)).then_inc(S(f"loaded{u}"), 16)
                        sp.dma_start(keep[u][:, :], keep_cols(k)).then_inc(S(f"loaded{u}"), 16)
                        if final:
                            sp.dma_start(G2[u][:, :, :], slot_rows(x0_slots, k)).then_inc(S(f"loaded{u}"), 16)

                    def stage(s, u, k, r):
                        if s == n_steps - 1:
                            sp.wait_ge(S("normed1" if final else "scaled_rows"), S.at("normed1" if final else "scaled_rows", k + 1))
                            sp.dma_start(slot_rows(gat_table if final else gcn_table[i + 1], k),
                                         O[u][:, :, :]).then_inc(S(f"stored{u}"), 16)

                    steps(sp, n_steps, EG, stage, (1 if final else 0, load))
                    for u in range(min(U, EG)):
                        sp.wait_ge(S(f"stored{u}"), S.at(f"stored{u}", 16 * len(range(u, EG, U))))

                @block.gpsimd
                def _(pool):
                    def load(u, k, r):
                        if not fresh(k):
                            pool.wait_ge(S("columns_ready"), S.at("columns_ready", k + 1 - U))
                        gather(pool, u, k, idx, gcn_table[i], G, 0)

                    def stage(s, u, k, r):
                        if final and s == 1:
                            inv_std(pool, u, k, 128, 4, 1)

                    steps(pool, n_steps, EG, stage, (0, load))

                @block.tensor
                def _(pe):
                    def stage(s, u, k, r):
                        if s == 0:
                            pe.wait_ge(S(f"gathered{u}"), S.at(f"gathered{u}", (r + 1) * 64))
                            pe.wait_ge(S(f"loaded{u}"), S.at(f"loaded{u}", (r + 1) * per_load))
                            if not fresh(k):
                                pe.wait_ge(S("biased_rows"), S.at("biased_rows", k + 1 - U))
                            transposes(G[u], pA[u])
                            transposes(Dn[u], pB[u]).then_inc(S("columns_ready"), 1)
                        elif s == 1:
                            pe.wait_ge(S("loop_added"), S.at("loop_added", k + 1))
                            to_node_major(pA[u], [(t0[u], W[:, :])]).then_inc(S("message_product"), 1)

                    steps(pe, n_steps, EG, stage)

                @block.vector
                def _(dve):
                    def stage(s, u, k, r):
                        if s == 0:
                            dve.wait_ge(S("columns_ready"), S.at("columns_ready", k + 1))
                            dve.wait_ge(S(f"loaded{u}"), S.at(f"loaded{u}", (r + 1) * per_load))
                            dve.wait_ge(S("segments_summed"), S.at("segments_summed", k))
                            scan(A[u], keep[u][:, :], pA[u][:, :], A[u - 1], ALU.mult, ALU.add).then_inc(S("segments_summed"), 1)
                            dve.wait_ge(S("segments_summed"), S.at("segments_summed", k + 1))
                            nc.vector.tensor_tensor(t0[u][:, :], A[u][:, 1:GC + 1], pB[u][:, :],
                                                    ALU.add).then_inc(S("loop_added"), 1)
                        elif s == 1:
                            dve.wait_ge(S("message_product"), S.at("message_product", k + 1))
                            if not final and not fresh(k):
                                dve.wait_ge(S("scaled_rows"), S.at("scaled_rows", k + 1 - U))
                            for j in range(4):
                                ins = nc.vector.scalar_tensor_tensor(
                                    nm(t1[u])[:, j, :], pA[u][:, j * D:(j + 1) * D], dinv[:, bass.ds(4 * k + j, 1)],
                                    row_b, ALU.mult, ALU.add)
                            ins.then_inc(S("biased_rows"), 1)
                            if final:
                                dve.wait_ge(S("biased_rows"), S.at("biased_rows", k + 1))
                                nc.vector.scalar_tensor_tensor(nm(t2[u]), G2[u][:, :, :], 2.0, nm(t1[u]), ALU.mult,
                                                               ALU.add).then_inc(S("residual1"), 1)
                                stats(dve, u, k, 128, 4, nm(t2[u]), 1)
                        else:
                            if not fresh(k):
                                dve.wait_ge(S(f"stored{u}"), S.at(f"stored{u}", r * 16))
                            normalise(dve, u, k, 128, 4, nm(t2[u]), O[u], 1)

                    steps(dve, n_steps, EG, stage)

                if not final:
                    @block.scalar
                    def _(act):
                        def stage(s, u, k, r):
                            if s == 1:
                                act.wait_ge(S("biased_rows"), S.at("biased_rows", k + 1))
                                if not fresh(k):
                                    act.wait_ge(S(f"stored{u}"), S.at(f"stored{u}", r * 16))
                                for j in range(4):
                                    ins = nc.scalar.activation(O[u][:, j, :], nm(t1[u])[:, j, :], ACTF.Relu,
                                                               scale=dinv[:, bass.ds(4 * k + j, 1)])
                                ins.then_inc(S("scaled_rows"), 1)

                        steps(act, n_steps, EG, stage)
            finish(EG, ["columns_ready", "segments_summed", "loop_added", "message_product", "biased_rows", "indices0"] + (ln_signals(1) if final else ["scaled_rows"]),
                   gathered=64, loaded=per_load, stored=16)

        in_flight(4, 2, "G G2 Dn O keep A t0 t1 t2")
        for i in range(3):
            gcn_layer(i)

        in_flight(4, 2, "G G2 Dn O keep soft A Mx Sc0 Sc1 t0 t1 t2 t3 t4 t5 t6 t7")

        with nc.Block() as block:
            @block.sync
            def _(sp):
                def load(u, k, r):
                    if not fresh(k):
                        sp.wait_ge(S("residual2"), S.at("residual2", k + 1 - U))
                    sp.dma_start(keep[u][:, :], keep_cols(k)).then_inc(S(f"loaded{u}"), 16)

                def stage(s, u, k, r):
                    if s == 7:
                        sp.wait_ge(S("normed2"), S.at("normed2", k + 1))
                        sp.dma_start(slot_rows(x2_slots, k), O[u][:, :, :]).then_inc(S(f"stored{u}"), 16)
                    elif s == 9:
                        sp.wait_ge(S("state_rows"), S.at("state_rows", k + 1))
                        sp.dma_start(slot_rows(mpn_table[0], k), nm(t7[u])).then_inc(S(f"stored{u}"), 16)

                steps(sp, 10, EG, stage, (6, load))
                for u in range(min(U, EG)):
                    sp.wait_ge(S(f"stored{u}"), S.at(f"stored{u}", 32 * len(range(u, EG, U))))

            @block.gpsimd
            def _(pool):
                def load_source(u, k, r):
                    if not fresh(k):
                        pool.wait_ge(S("x1_transposed"), S.at("x1_transposed", k + 1 - U))
                    gather(pool, u, k, idx, gat_table, G, 0)

                def load_own(u, k, r):
                    if not fresh(k):
                        pool.wait_ge(S("residual2"), S.at("residual2", k + 1 - U))
                    gather(pool, u, k, idx_own, gat_table, Dn, 4)

                def stage(s, u, k, r):
                    if s == 6:
                        inv_std(pool, u, k, 128, 4, 2)

                steps(pool, 10, EG, stage, (0, load_source), (6, load_own))

            @block.tensor
            def _(pe):
                def stage(s, u, k, r):
                    if s == 0:
                        pe.wait_ge(S(f"gathered{u}"), S.at(f"gathered{u}", (r + 1) * 128))
                        if not fresh(k):
                            pe.wait_ge(S("state_rows"), S.at("state_rows", k + 1 - U))
                        transposes(G[u], pA[u])
                        transposes(Dn[u], pB[u]).then_inc(S("x1_transposed"), 1)
                    elif s == 1:
                        pe.wait_ge(S("x1_cols"), S.at("x1_cols", k + 1))
                        feature_major(pA[u], [(t0[u], attS[:, :]), (t1[u], attD[:, :])])
                        feature_major(pB[u], [(t1[u], attSD[:, :])]).then_inc(S("scores_product"), 1)
                    elif s == 3 or s == 5:
                        c = s // 2 - 1
                        pe.wait_ge(S("weighted0" if c else "scores"), S.at("weighted0" if c else "scores", k + 1))
                        feature_major(pA[u], [(t0[u], Wg[:, c, :])])
                        feature_major(pB[u], [(t1[u], Wg[:, c, :])]).then_inc(S(f"weighted_product{c}"), 1)
                    elif s == 6:
                        pe.wait_ge(S("head_relu1"), S.at("head_relu1", k + 1))
                        to_node_major(pA[u], [(G2[u][:, :, :].rearrange("p j d -> p (j d)"), fcw[:, 0, :]),
                                              (t6[u], fcw[:, 1, :])], row=row_fc).then_inc(S("gat_product"), 1)
                    elif s == 8:
                        pe.wait_ge(S("normed2"), S.at("normed2", k + 1))
                        transposes(O[u], pB[u]).then_inc(S("x2_transposed"), 1)
                    elif s == 9:
                        pe.wait_ge(S("x2_cols"), S.at("x2_cols", k + 1))
                        to_node_major(pA[u], [(t0[u], Wi[:, :])], row=row_bi).then_inc(S("state_product"), 1)

                steps(pe, 10, EG, stage)

            @block.scalar
            def _(act):
                def stage(s, u, k, r):
                    if s == 0:
                        act.wait_ge(S("x1_transposed"), S.at("x1_transposed", k + 1))
                        nc.scalar.copy(t0[u][:, :], pA[u][:, :])
                        nc.scalar.copy(t1[u][:, :], pB[u][:, :]).then_inc(S("x1_cols"), 1)
                    elif s == 1:
                        act.wait_ge(S("scores_product"), S.at("scores_product", k + 1))
                        nc.scalar.copy(soft[u][:, 0, :], pA[u][:, :])
                        nc.scalar.copy(soft[u][:, 1, :], pB[u][:, :]).then_inc(S("scores"), 1)
                    elif s == 2:
                        act.wait_ge(S("exponents"), S.at("exponents", k + 1))
                        nc.scalar.activation(soft[u][:, :, :], soft[u][:, :, :], ACTF.Exp).then_inc(S("exponentials"), 1)
                    elif s == 4:
                        act.wait_ge(S("head_mean0"), S.at("head_mean0", k + 1))
                        nc.scalar.activation(G2[u][:, :, :].rearrange("p j d -> p (j d)"), t4[u][:, :], ACTF.Relu,
                                             bias=cb[:, c_gat:c_gat + 1]).then_inc(S("head_relu0"), 1)
                    elif s == 5:
                        act.wait_ge(S("head_mean1"), S.at("head_mean1", k + 1))
                        nc.scalar.activation(t6[u][:, :], t3[u][:, :], ACTF.Relu,
                                             bias=cb[:, c_gat + 1:c_gat + 2]).then_inc(S("head_relu1"), 1)
                    elif s == 8:
                        act.wait_ge(S("x2_transposed"), S.at("x2_transposed", k + 1))
                        nc.scalar.copy(t0[u][:, :], pB[u][:, :]).then_inc(S("x2_cols"), 1)
                    elif s == 9:
                        act.wait_ge(S("state_product"), S.at("state_product", k + 1))
                        if not fresh(k):
                            act.wait_ge(S(f"stored{u}"), S.at(f"stored{u}", r * 32))
                        nc.scalar.activation(t7[u][:, :], pA[u][:, :], ACTF.Relu).then_inc(S("state_rows"), 1)

                steps(act, 10, EG, stage)

            @block.vector
            def _(dve):
                def stt(out_, in0, scalar, in1, op0, op1):
                    return nc.vector.scalar_tensor_tensor(out_, in0, scalar, in1, op0, op1)

                def tt(out_, in0, in1, op):
                    return nc.vector.tensor_tensor(out_, in0, in1, op)

                def stage(s, u, k, r):
                    decay, p_edge, p_loop = soft[u][:, 0, :], soft[u][:, 1, :], soft[u][:, 2, :]
                    m_now, m_before = Mx[u][:, 1:GC + 1], Mx[u][:, 0:GC]
                    if s == 2:
                        dve.wait_ge(S("scores"), S.at("scores", k + 1))
                        dve.wait_ge(S(f"loaded{u}"), S.at(f"loaded{u}", (r + 1) * 16))
                        stt(t2[u][:, :], soft[u][:, 0, :], SLOPE, soft[u][:, 0, :], ALU.mult, ALU.max)
                        stt(t3[u][:, :], soft[u][:, 1, :], SLOPE, soft[u][:, 1, :], ALU.mult, ALU.max)
                        nc.vector.tensor_scalar(t5[u][:, :], keep[u][:, :], -1.0, FAR, ALU.add,
                                                ALU.mult).then_inc(S("leaky_scores"), 1)
                        dve.wait_ge(S("leaky_scores"), S.at("leaky_scores", k + 1))
                        tt(t4[u][:, :], t2[u][:, :], t3[u][:, :], ALU.max).then_inc(S("scores_with_loop"), 1)
                        dve.wait_ge(S("scores_with_loop"), S.at("scores_with_loop", k + 1))
                        dve.wait_ge(S("maxima"), S.at("maxima", k))
                        nc.vector.tensor_copy(Mx[u][:, 0:1], Mx[u - 1][:, GC:GC + 1])
                        scan(Mx[u], t5[u][:, :], t4[u][:, :], Mx[u - 1], ALU.add, ALU.max).then_inc(S("maxima"), 1)
                        dve.wait_ge(S("maxima"), S.at("maxima", k + 1))
                        tt(soft[u][:, 1, :], t2[u][:, :], m_now, ALU.subtract)
                        tt(soft[u][:, 2, :], t3[u][:, :], m_now, ALU.subtract)
                        tt(soft[u][:, 0, :], m_before, t5[u][:, :], ALU.add).then_inc(S("exponents_part"), 1)
                        dve.wait_ge(S("exponents_part"), S.at("exponents_part", k + 1))
                        tt(soft[u][:, 0, :], soft[u][:, 0, :], m_now, ALU.subtract).then_inc(S("exponents"), 1)
                    elif s == 3:
                        dve.wait_ge(S("exponentials"), S.at("exponentials", k + 1))
                        dve.wait_ge(S("segments_summed"), S.at("segments_summed", k))
                        scan(A[u], decay, p_edge, A[u - 1], ALU.mult, ALU.add).then_inc(S("segments_summed"), 1)
                        dve.wait_ge(S("segments_summed"), S.at("segments_summed", k + 1))
                        tt(t5[u][:, :], A[u][:, 1:GC + 1], p_loop, ALU.add).then_inc(S("denominator"), 1)
                        dve.wait_ge(S("denominator"), S.at("denominator", k + 1))
                        nc.vector.reciprocal(t5[u][:, :], t5[u][:, :]).then_inc(S("inv_denominator"), 1)
                    elif s == 4 or s == 5:
                        c = s - 4
                        Sc, res = (Sc0, t4) if c == 0 else (Sc1, t3)
                        dve.wait_ge(S(f"weighted_product{c}"), S.at(f"weighted_product{c}", k + 1))
                        dve.wait_ge(S(f"head_mean0" if c else "inv_denominator"), S.at(f"head_mean0" if c else "inv_denominator", k + 1))
                        tt(t2[u][:, :], p_edge, pA[u][:, :], ALU.mult)
                        tt(t3[u][:, :], p_loop, pB[u][:, :], ALU.mult).then_inc(S(f"weighted{c}"), 1)
                        dve.wait_ge(S(f"weighted{c}"), S.at(f"weighted{c}", k + 1))
                        dve.wait_ge(S(f"weighted_sums{c}"), S.at(f"weighted_sums{c}", k))
                        scan(Sc[u], decay, t2[u][:, :], Sc[u - 1], ALU.mult, ALU.add).then_inc(S(f"weighted_sums{c}"), 1)
                        dve.wait_ge(S(f"weighted_sums{c}"), S.at(f"weighted_sums{c}", k + 1))
                        tt(t2[u][:, :], Sc[u][:, 1:GC + 1], t3[u][:, :], ALU.add).then_inc(S(f"numerator{c}"), 1)
                        dve.wait_ge(S(f"numerator{c}"), S.at(f"numerator{c}", k + 1))
                        dve.wait_ge(S("inv_denominator"), S.at("inv_denominator", k + 1))
                        tt(res[u][:, :], t2[u][:, :], t5[u][:, :], ALU.mult).then_inc(S(f"head_mean{c}"), 1)
                    elif s == 6:
                        dve.wait_ge(S("gat_product"), S.at("gat_product", k + 1))
                        tt(nm(t2[u]), Dn[u][:, :, :], nm(pA[u]), ALU.add).then_inc(S("residual2"), 1)
                        stats(dve, u, k, 128, 4, nm(t2[u]), 2)
                    elif s == 7:
                        if not fresh(k):
                            dve.wait_ge(S(f"stored{u}"), S.at(f"stored{u}", r * 32))
                        normalise(dve, u, k, 128, 4, nm(t2[u]), O[u], 2)

                steps(dve, 10, EG, stage)
        finish(EG, ["x1_transposed", "x1_cols", "scores_product", "scores", "leaky_scores", "scores_with_loop", "maxima", "exponents_part", "exponents", "exponentials", "segments_summed",
                    "denominator", "inv_denominator", "weighted_product0", "weighted_product1", "weighted0", "weighted1", "weighted_sums0", "weighted_sums1", "numerator0", "numerator1",
                    "head_mean0", "head_mean1", "head_relu0", "head_relu1", "gat_product", "x2_transposed", "x2_cols", "state_product", "state_rows", "indices0", "indices4"]
               + ln_signals(2), gathered=128, loaded=16, stored=32)
        S.retire(["scores_product", "scores", "leaky_scores", "scores_with_loop", "maxima", "exponents_part", "exponents",
                  "exponentials", "denominator", "inv_denominator", "weighted_product0", "weighted_product1", "weighted0", "weighted1",
                  "weighted_sums0", "weighted_sums1", "numerator0", "numerator1", "head_mean0", "head_mean1"])

        def mpn_round(i):
            final = i == ROUNDS - 1
            per_load = 48 if final else 32
            n_steps = 4 if final else 3

            with nc.Block() as block:
                @block.sync
                def _(sp):
                    def load(u, k, r):
                        if not fresh(k):
                            sp.wait_ge(S("state_shifted"), S.at("state_shifted", k + 1 - U))
                        sp.dma_start(Dn[u][:, :, :], slot_rows(mpn_table[i % 2], k)).then_inc(S(f"loaded{u}"), 16)
                        sp.dma_start(keep[u][:, :], keep_cols(k)).then_inc(S(f"loaded{u}"), 16)
                        if final:
                            sp.dma_start(G2[u][:, :, :], slot_rows(x2_slots, k)).then_inc(S(f"loaded{u}"), 16)

                    def stage(s, u, k, r):
                        if s == n_steps - 1:
                            sp.wait_ge(S("normed3" if final else "state_updated"), S.at("normed3" if final else "state_updated", k + 1))
                            sp.dma_start(slot_rows(x3_slots if final else mpn_table[(i + 1) % 2], k),
                                         O[u][:, :, :]).then_inc(S(f"stored{u}"), 16)

                    steps(sp, n_steps, EG, stage, (1, load))
                    for u in range(min(U, EG)):
                        sp.wait_ge(S(f"stored{u}"), S.at(f"stored{u}", 16 * len(range(u, EG, U))))

                @block.gpsimd
                def _(pool):
                    def load(u, k, r):
                        if not fresh(k):
                            pool.wait_ge(S("cols_psum"), S.at("cols_psum", k + 1 - U))
                        gather(pool, u, k, idx, mpn_table[i % 2], G, 0)

                    def stage(s, u, k, r):
                        if s == 2 and final:
                            inv_std(pool, u, k, 128, 4, 3)

                    steps(pool, n_steps, EG, stage, (0, load))

                @block.tensor
                def _(pe):
                    def stage(s, u, k, r):
                        if s == 0:
                            pe.wait_ge(S(f"gathered{u}"), S.at(f"gathered{u}", (r + 1) * 64))
                            if not fresh(k):
                                pe.wait_ge(S("update_rows"), S.at("update_rows", k + 1 - U))
                            transposes(G[u], pA[u]).then_inc(S("cols_psum"), 1)
                        elif s == 1:
                            pe.wait_ge(S("cols_copied"), S.at("cols_copied", k + 1))
                            feature_major(pB[u], [(t0[u], Wm[:, i, :])]).then_inc(S("message_product"), 1)
                        elif s == 2:
                            pe.wait_ge(S("segments_summed"), S.at("segments_summed", k + 1))
                            to_node_major(pA[u], [(A[u][:, 1:GC + 1], Wu[:, i, :])], row=row_bu + i).then_inc(S("update_product"), 1)

                    steps(pe, n_steps, EG, stage)

                @block.scalar
                def _(act):
                    def stage(s, u, k, r):
                        if s == 0:
                            act.wait_ge(S("cols_psum"), S.at("cols_psum", k + 1))
                            nc.scalar.copy(t0[u][:, :], pA[u][:, :]).then_inc(S("cols_copied"), 1)
                        elif s == 1:
                            act.wait_ge(S("message_product"), S.at("message_product", k + 1))
                            if not fresh(k):
                                act.wait_ge(S("segments_summed"), S.at("segments_summed", k + 1 - U))
                            nc.scalar.activation(t1[u][:, :], pB[u][:, :], ACTF.Relu,
                                                 bias=cb[:, c_bm + i:c_bm + i + 1]).then_inc(S("messages"), 1)
                        elif s == 2:
                            act.wait_ge(S("update_product"), S.at("update_product", k + 1))
                            if not fresh(k):
                                act.wait_ge(S("state_updated"), S.at("state_updated", k + 1 - U))
                            nc.scalar.activation(t2[u][:, :], pA[u][:, :], ACTF.Relu).then_inc(S("update_rows"), 1)

                    steps(act, n_steps, EG, stage)

                @block.vector
                def _(dve):
                    def stage(s, u, k, r):
                        if s == 1:
                            dve.wait_ge(S("messages"), S.at("messages", k + 1))
                            dve.wait_ge(S(f"loaded{u}"), S.at(f"loaded{u}", (r + 1) * per_load))
                            dve.wait_ge(S("segments_summed"), S.at("segments_summed", k))
                            scan(A[u], keep[u][:, :], t1[u][:, :], A[u - 1], ALU.mult, ALU.add).then_inc(S("segments_summed"), 1)
                            ins = nc.vector.tensor_tensor(nm(t3[u]), Dn[u][:, :, :],
                                                          cu[:, i, :].unsqueeze(1).to_broadcast([128, 4, D]),
                                                          ALU.subtract)
                            if final:
                                ins = nc.vector.tensor_tensor(nm(t4[u]), G2[u][:, :, :],
                                                              c_all[:, :].unsqueeze(1).to_broadcast([128, 4, D]), ALU.add)
                            ins.then_inc(S("state_shifted"), 1)
                        elif s == 2:
                            dve.wait_ge(S("update_rows"), S.at("update_rows", k + 1))
                            dve.wait_ge(S("state_shifted"), S.at("state_shifted", k + 1))
                            if final:
                                nc.vector.tensor_tensor(t5[u][:, :], t2[u][:, :], t3[u][:, :], ALU.add).then_inc(S("state_updated"), 1)
                                dve.wait_ge(S("state_updated"), S.at("state_updated", k + 1))
                                nc.vector.tensor_tensor(t5[u][:, :], t5[u][:, :], t4[u][:, :], ALU.add).then_inc(S("residual3"), 1)
                                stats(dve, u, k, 128, 4, nm(t5[u]), 3)
                            else:
                                if not fresh(k):
                                    dve.wait_ge(S(f"stored{u}"), S.at(f"stored{u}", r * 16))
                                nc.vector.tensor_tensor(O[u][:, :, :], nm(t2[u]), nm(t3[u]), ALU.add).then_inc(S("state_updated"), 1)
                        elif s == 3:
                            if not fresh(k):
                                dve.wait_ge(S(f"stored{u}"), S.at(f"stored{u}", r * 16))
                            normalise(dve, u, k, 128, 4, nm(t5[u]), O[u], 3)

                    steps(dve, n_steps, EG, stage)
            finish(EG, ["cols_psum", "cols_copied", "message_product", "messages", "segments_summed", "update_product", "update_rows", "state_updated", "state_shifted", "indices0"]
                   + (ln_signals(3) if final else []), gathered=64, loaded=per_load, stored=16)

        in_flight(6, 1, "G G2 Dn O keep A t0 t1 t2 t3 t4 t5")
        for i in range(ROUNDS):
            mpn_round(i)

        in_flight(7, 1, "G O zm t0 t1 t2 t3 t4 t5")
        with nc.Block() as block:
            @block.tensor
            def _(pe):
                nc.tensor.matmul(pGram[:, 0:D + 1], ident[:, :], zeros[:, :], start=True, stop=False,
                                 skip_group_check=True)
        chain(NG, True)
        in_flight(6, 1, "G G2 Dn keep A zm t0 t1 t2")

        with nc.Block() as block:
            @block.sync
            def _(sp):
                def load(u, k, r):
                    if not fresh(k):
                        if not fresh(k):
                            sp.wait_ge(S(f"scattered{u}"), S.at(f"scattered{u}", r * 64))
                    sp.dma_start(Dn[u][:, :, :], slot_rows(x3_slots, k)).then_inc(S(f"loaded{u}"), 16)

                steps(sp, 1, EG, None, (0, load))

            @block.gpsimd
            def _(pool):
                def stage(s, u, k, r):
                    pool.wait_ge(S(f"loaded{u}"), S.at(f"loaded{u}", (r + 1) * 16))
                    if not fresh(k):
                        pool.wait_ge(S(f"scattered{u}"), S.at(f"scattered{u}", r * 64))
                    scatter(pool, u, k, Dn, x3_nodes)

                steps(pool, 1, EG, stage)
                for u in range(min(U, EG)):
                    pool.wait_ge(S(f"scattered{u}"), S.at(f"scattered{u}", 64 * len(range(u, EG, U))))
        finish(EG, ["indices0"], loaded=16, scattered=64)

        with nc.Block() as block:
            @block.sync
            def _(sp):
                def load(u, k, r):
                    if not fresh(k):
                        sp.wait_ge(S("z_rows"), S.at("z_rows", k + 1 - U))
                    sp.dma_start(Dn[u][:, :, :], slot_rows(x3_slots, k)).then_inc(S(f"loaded{u}"), 16)
                    sp.dma_start(keep[u][:, :], keep_cols(k)).then_inc(S(f"loaded{u}"), 16)

                def stage(s, u, k, r):
                    if s == 3:
                        sp.wait_ge(S("z_masked"), S.at("z_masked", k + 1))
                        sp.dma_start(slot_rows(z_slots, k), zm[u][:, :, 0:D]).then_inc(S(f"stored{u}"), 16)

                steps(sp, 5, EG, stage, (2, load))
                for u in range(min(U, EG)):
                    sp.wait_ge(S(f"stored{u}"), S.at(f"stored{u}", 16 * len(range(u, EG, U))))

            @block.gpsimd
            def _(pool):
                def load(u, k, r):
                    if not fresh(k):
                        pool.wait_ge(S("edge_sums"), S.at("edge_sums", k + 1 - U))
                    gather(pool, u, k, src_i, x3_nodes, G, 0)
                    gather(pool, u, k, edge_i, a["edge_attr_128"], G2, 4)

                steps(pool, 5, EG, None, (0, load))

            @block.tensor
            def _(pe):
                def stage(s, u, k, r):
                    if s == 1:
                        pe.wait_ge(S("messages"), S.at("messages", k + 1))
                        transposes(nm(t1[u]), pA[u]).then_inc(S("cols_psum"), 1)
                    elif s == 2:
                        pe.wait_ge(S("segments_summed"), S.at("segments_summed", k + 1))
                        back_transposes(A[u][:, 1:GC + 1], pB[u]).then_inc(S("message_product"), 1)
                    elif s == 4:
                        pe.wait_ge(S("z_masked"), S.at("z_masked", k + 1))
                        for j in range(4):
                            ins = nc.tensor.matmul(pGram[:, 0:D + 1], zm[u][:, j, 0:D], zm[u][:, j, :], start=False,
                                                   stop=False, skip_group_check=True)
                        ins.then_inc(S("gram_added"), 1)

                steps(pe, 5, EG, stage)
                nc.tensor.matmul(pGram[:, 0:D + 1], ident[:, :], zeros[:, :], start=False, stop=True, skip_group_check=True)

            @block.scalar
            def _(act):
                def stage(s, u, k, r):
                    if s == 0:
                        act.wait_ge(S("edge_sums"), S.at("edge_sums", k + 1))
                        if not fresh(k):
                            act.wait_ge(S("cols_psum"), S.at("cols_psum", k + 1 - U))
                        nc.scalar.activation(t1[u][:, :], t0[u][:, :], ACTF.Relu).then_inc(S("messages"), 1)
                    elif s == 2:
                        act.wait_ge(S("z_rows"), S.at("z_rows", k + 1))
                        if not fresh(k):
                            act.wait_ge(S(f"stored{u}"), S.at(f"stored{u}", r * 16))
                            act.wait_ge(S("gram_added"), S.at("gram_added", k + 1 - U))
                        for j in range(4):
                            ins = nc.scalar.activation(zm[u][:, j, 0:D], nm(t2[u])[:, j, :], ACTF.Copy,
                                                       scale=last[:, bass.ds(4 * k + j, 1)])
                        ins.then_inc(S("z_masked"), 1)

                steps(act, 5, EG, stage)

            @block.vector
            def _(dve):
                def stage(s, u, k, r):
                    if s == 0:
                        dve.wait_ge(S(f"gathered{u}"), S.at(f"gathered{u}", (r + 1) * 128))
                        if not fresh(k):
                            dve.wait_ge(S("messages"), S.at("messages", k + 1 - U))
                        nc.vector.tensor_tensor(nm(t0[u]), G[u][:, :, :], G2[u][:, :, :], ALU.add).then_inc(S("edge_sums"), 1)
                    elif s == 1:
                        dve.wait_ge(S("cols_psum"), S.at("cols_psum", k + 1))
                        dve.wait_ge(S(f"loaded{u}"), S.at(f"loaded{u}", (r + 1) * 32))
                        dve.wait_ge(S("segments_summed"), S.at("segments_summed", k))
                        scan(A[u], keep[u][:, :], pA[u][:, :], A[u - 1], ALU.mult, ALU.add).then_inc(S("segments_summed"), 1)
                    elif s == 2:
                        dve.wait_ge(S("message_product"), S.at("message_product", k + 1))
                        if not fresh(k):
                            dve.wait_ge(S("z_masked"), S.at("z_masked", k + 1 - U))
                        nc.vector.scalar_tensor_tensor(nm(t2[u]), Dn[u][:, :, :], eps1[:, 0:1], nm(pB[u]), ALU.mult,
                                                       ALU.add).then_inc(S("z_rows"), 1)

                steps(dve, 5, EG, stage)
        finish(EG, ["edge_sums", "messages", "cols_psum", "segments_summed", "message_product", "z_rows", "z_masked", "gram_added", "indices0", "indices4"], gathered=128,
               loaded=32, stored=16)

        with nc.Block() as block:
            @block.gpsimd
            def _(pool):
                nc.gpsimd.memset(small[:, 14:16], -0.5).then_inc(S("bn1_half"), 1)
                pool.wait_ge(S("bn1_half"), S.at("bn1_half", 1))
                pool.wait_ge(S("bn1_var"), S.at("bn1_var", 1))
                nc.gpsimd.tensor_tensor(small[:, 12:14], small[:, 8:10], small[:, 14:16], ALU.pow).then_inc(S("bn1_rstd"), 1)

            @block.vector
            def _(dve):
                ch = Chain(dve, "dve_setup")
                nc.vector.tensor_scalar(gram[:, :], pGram[:, 0:D + 1], 1.0 / N, None, ALU.mult).then_inc(S("gram_in"), 1)
                dve.wait_ge(S("mrow_p"), S.at("mrow_p", 1))
                nc.vector.tensor_copy(mrow[:, :], pMisc[0:1, 0:D]).then_inc(S("mrow_in"), 1)
                dve.wait_ge(S("outer_p"), S.at("outer_p", 1))
                nc.vector.tensor_tensor(gram[:, 0:D], gram[:, 0:D], pMisc[:, 128:256], ALU.subtract).then_inc(S("cov"), 1)
                dve.wait_ge(S("cw_p"), S.at("cw_p", 1))
                nc.vector.tensor_tensor(prod[:, :, :], V1[:, :, :],
                                        pMisc[:, 256:512].rearrange("p (c o) -> p c o", c=2), ALU.mult).then_inc(S("cwp"), 1)
                dve.wait_ge(S("mv_p"), S.at("mv_p", 1))
                ch.after(nc.vector.tensor_copy(small[:, 0:4], pA[0][:, 0:4]))
                nc.vector.tensor_scalar(small[:, 8:10], small[:, 2:4], BN_EPS, None, ALU.add).then_inc(S("bn1_var"), 1)
                dve.wait_ge(S("bn1_rstd"), S.at("bn1_rstd", 1))
                ch.after(nc.vector.tensor_tensor(bn[:, b_s1:b_s1 + 2], bn[:, b_g1:b_g1 + 2], small[:, 12:14], ALU.mult))
                ch.after(nc.vector.tensor_tensor(small[:, 4:6], small[:, 0:2], bn[:, b_s1:b_s1 + 2], ALU.mult))
                ch.after(nc.vector.tensor_tensor(bn[:, b_t1:b_t1 + 2], bn[:, b_b1:b_b1 + 2], small[:, 4:6], ALU.subtract))
                nc.vector.tensor_scalar(small[:, 6:8], bn[:, b_t1:b_t1 + 2], 0.0, None, ALU.max).then_inc(S("r0"), 1)
                dve.wait_ge(S("y0_p"), S.at("y0_p", 1))
                ch.after(nc.vector.tensor_copy(small[:, 16:17], pMisc[:, 0:1]))
                ch.close()

            @block.tensor
            def _(pe):
                pe.wait_ge(S("gram_in"), S.at("gram_in", 1))
                nc.tensor.transpose(pMisc[0:1, 0:D], gram[:, D:D + 1], ident[:, :]).then_inc(S("mrow_p"), 1)
                pe.wait_ge(S("mrow_in"), S.at("mrow_in", 1))
                nc.tensor.matmul(pMisc[:, 128:256], mrow[:, :], mrow[:, :], start=True, stop=True).then_inc(S("outer_p"), 1)
                pe.wait_ge(S("cov"), S.at("cov", 1))
                nc.tensor.matmul(pMisc[:, 256:512], gram[:, 0:D], V1[:, :, :], start=True, stop=True).then_inc(S("cw_p"), 1)
                pe.wait_ge(S("cwp"), S.at("cwp", 1))
                for c in range(2):
                    nc.tensor.matmul(pA[0][:, c:c + 1], V1[:, c, :], gram[:, D:D + 1], start=True, stop=True)
                for c in range(2):
                    ins = nc.tensor.matmul(pA[0][:, 2 + c:3 + c], prod[:, c, :], onesc[:, :], start=True, stop=True)
                ins.then_inc(S("mv_p"), 1)
                pe.wait_ge(S("r0"), S.at("r0", 1))
                for c in range(2):
                    ins = nc.tensor.matmul(pMisc[:, 0:1], V2[:, c, :], small[:, 6 + c:7 + c], start=(c == 0), stop=(c == 1))
                ins.then_inc(S("y0_p"), 1)

        def mlp(groups, dense):
            col0, g0 = (0, 0) if dense else (N, NG)

            with nc.Block() as block:
                @block.sync
                def _(sp):
                    def load(u, k, r):
                        P, J = shape(k, dense)
                        if not fresh(k):
                            sp.wait_ge(S("z_nodes" if dense else "cols_psum"), S.at("z_nodes" if dense else "cols_psum", k + 1 - U))
                        rows_ = node_rows(x3_nodes, k) if dense else slot_rows(z_slots, k)
                        sp.dma_start(G[u][0:P, 0:J, :], rows_).then_inc(S(f"loaded{u}"), 16)

                    def stage(s, u, k, r):
                        if s == 2:
                            P, J = shape(k, dense)
                            sp.wait_ge(S("y_copied"), S.at("y_copied", k + 1))
                            sp.dma_start(y_cols[:, bass.ds(k * GC + col0, P * J)], t4[u][:, 0:P * J]).then_inc(S(f"stored{u}"), 16)

                    steps(sp, 3, groups, stage, (1, load))
                    for u in range(min(U, groups)):
                        sp.wait_ge(S(f"stored{u}"), S.at(f"stored{u}", 16 * len(range(u, groups, U))))

                if dense:
                    @block.gpsimd
                    def _(pool):
                        def stage(s, u, k, r):
                            if s == 0:
                                P, J = shape(k)
                                pool.wait_ge(S(f"loaded{u}"), S.at(f"loaded{u}", (r + 1) * 16))
                                if not fresh(k):
                                    pool.wait_ge(S("cols_psum"), S.at("cols_psum", k + 1 - U))
                                nc.gpsimd.tensor_tensor(nm(t0[u])[0:P, 0:J, :], G[u][0:P, 0:J, :],
                                                        nmask[0:P, bass.ds(4 * k, J)].unsqueeze(2).to_broadcast([P, J, D]),
                                                        ALU.mult).then_inc(S("z_nodes"), 1)

                        steps(pool, 3, groups, stage)

                @block.tensor
                def _(pe):
                    def stage(s, u, k, r):
                        P, J = shape(k, dense)
                        C = P * J
                        if s == 0:
                            pe.wait_ge(S("z_nodes"), S.at("z_nodes", k + 1)) if dense else pe.wait_ge(S(f"loaded{u}"), S.at(f"loaded{u}", (r + 1) * 16))
                            transposes(nm(t0[u]) if dense else G[u], pA[u], P, J).then_inc(S("cols_psum"), 1)
                        elif s == 1:
                            pe.wait_ge(S("cols_copied"), S.at("cols_copied", k + 1))
                            feature_major(pB[u], [(t1[u], V1[:, 0, :])], C)
                            feature_major(pA[u], [(t1[u], V1[:, 1, :])], C).then_inc(S("hidden_product"), 1)
                        elif s == 2:
                            pe.wait_ge(S("hidden_cols"), S.at("hidden_cols", k + 1))
                            feature_major(pB[u], [(t2[u], V2[:, 0, :]), (t3[u], V2[:, 1, :])], C).then_inc(S("y_product"), 1)

                    steps(pe, 3, groups, stage)

                @block.scalar
                def _(act):
                    def stage(s, u, k, r):
                        P, J = shape(k, dense)
                        C = P * J
                        if s == 0:
                            act.wait_ge(S("cols_psum"), S.at("cols_psum", k + 1))
                            nc.scalar.copy(t1[u][:, 0:C], pA[u][:, 0:C]).then_inc(S("cols_copied"), 1)
                        elif s == 1:
                            act.wait_ge(S("hidden_product"), S.at("hidden_product", k + 1))
                            nc.scalar.activation(t2[u][:, 0:C], pB[u][:, 0:C], ACTF.Relu, bias=bn[:, b_t1:b_t1 + 1],
                                                 scale=bn[:, b_s1:b_s1 + 1])
                            nc.scalar.activation(t3[u][:, 0:C], pA[u][:, 0:C], ACTF.Relu, bias=bn[:, b_t1 + 1:b_t1 + 2],
                                                 scale=bn[:, b_s1 + 1:b_s1 + 2]).then_inc(S("hidden_cols"), 1)
                        elif s == 2:
                            act.wait_ge(S("y_product"), S.at("y_product", k + 1))
                            if not fresh(k):
                                act.wait_ge(S(f"stored{u}"), S.at(f"stored{u}", r * 16))
                            if not fresh(k):
                                act.wait_ge(S("y_moments"), S.at("y_moments", k + 1 - U))
                            nc.scalar.copy(t4[u][:, 0:C], pB[u][:, 0:C]).then_inc(S("y_copied"), 1)

                    steps(act, 3, groups, stage)

                @block.vector
                def _(dve):
                    def stage(s, u, k, r):
                        if s == 2:
                            P, J = shape(k, dense)
                            dve.wait_ge(S("y_copied"), S.at("y_copied", k + 1))
                            nc.vector.bn_stats(ystat[:, bass.ds(k + g0, 1), :].rearrange("p o s -> p (o s)"),
                                               t4[u][:, 0:P * J]).then_inc(S("y_moments"), 1)

                    steps(dve, 3, groups, stage)
            finish(groups, ["cols_psum", "cols_copied", "hidden_product", "hidden_cols", "y_product", "y_copied", "y_moments"] + (["z_nodes"] if dense else []),
                   loaded=16, stored=16)

        in_flight(4, 2, "G t0 t1 t2 t3 t4")
        mlp(EG, False)
        mlp(NG, True)

        with nc.Block() as block:
            @block.gpsimd
            def _(pool):
                pool.wait_ge(S("bn2_var"), S.at("bn2_var", 1))
                nc.gpsimd.tensor_tensor(small[:, 12:13], small[:, 8:9], small[:, 14:15], ALU.pow).then_inc(S("bn2_rstd"), 1)

            @block.vector
            def _(dve):
                ch = Chain(dve, "dve_setup")
                M = N + EP
                mean, var, y0 = small[:, 0:1], small[:, 1:2], small[:, 16:17]
                m, e, f = small[:, 2:3], small[:, 3:4], small[:, 4:5]

                def tt(o, x, y, op):
                    ch.after(nc.vector.tensor_tensor(o, x, y, op))

                def ts(o, x, s1, s2=None, op0=ALU.mult, op1=ALU.bypass):
                    ch.after(nc.vector.tensor_scalar(o, x, s1, s2, op0, op1) if s2 is not None
                             else nc.vector.tensor_scalar(o, x, s1, None, op0))

                ch.after(nc.vector.bn_aggr(small[:, 0:2], ystat[:, :, :].rearrange("p g s -> p (g s)")))
                tt(e, mean, y0, ALU.subtract)
                ts(e, e, EP / N)
                tt(m, mean, e, ALU.add)
                tt(e, e, e, ALU.mult)
                tt(e, e, var, ALU.add)
                ts(e, e, M / N)
                tt(f, y0, m, ALU.subtract)
                tt(f, f, f, ALU.mult)
                ts(f, f, EP / N)
                tt(e, e, f, ALU.subtract)
                nc.vector.tensor_scalar(small[:, 8:9], e, 0.0, BN_EPS, ALU.max, ALU.add).then_inc(S("bn2_var"), 1)
                dve.wait_ge(S("bn2_rstd"), S.at("bn2_rstd", 1))
                tt(bn[:, b_s2:b_s2 + 1], bn[:, b_g2:b_g2 + 1], small[:, 12:13], ALU.mult)
                tt(e, m, bn[:, b_s2:b_s2 + 1], ALU.mult)
                tt(bn[:, b_t2:b_t2 + 1], bn[:, b_b2:b_b2 + 1], e, ALU.subtract)
                ch.close()

        def last_norm(groups, dense):
            col0 = 0 if dense else N
            per_store, kind = (16, "stored") if dense else (64, "scattered")

            with nc.Block() as block:
                @block.sync
                def _(sp):
                    def load(u, k, r):
                        P, J = shape(k, dense)
                        if not fresh(k):
                            sp.wait_ge(S("residual1"), S.at("residual1", k + 1 - U))
                        sp.dma_start(t1[u][:, 0:P * J], y_cols[:, bass.ds(k * GC + col0, P * J)]).then_inc(S(f"loaded{u}"), 16)
                        rows_ = node_rows(x3_nodes, k) if dense else slot_rows(x3_slots, k)
                        sp.dma_start(Dn[u][0:P, 0:J, :], rows_).then_inc(S(f"loaded{u}"), 16)

                    def stage(s, u, k, r):
                        if s == 1 and dense:
                            P, J = shape(k)
                            sp.wait_ge(S("normed1"), S.at("normed1", k + 1))
                            sp.dma_start(node_rows(out, k), O[u][0:P, 0:J, :]).then_inc(S(f"stored{u}"), 16)

                    steps(sp, 2, groups, stage, (0, load))
                    if dense:
                        for u in range(min(U, groups)):
                            sp.wait_ge(S(f"stored{u}"), S.at(f"stored{u}", 16 * len(range(u, groups, U))))

                @block.gpsimd
                def _(pool):
                    def stage(s, u, k, r):
                        P, J = shape(k, dense)
                        if s == 0:
                            inv_std(pool, u, k, P, J, 1)
                        elif not dense:
                            pool.wait_ge(S("normed1"), S.at("normed1", k + 1))
                            scatter(pool, u, k, O, out)

                    steps(pool, 2, groups, stage)
                    if not dense:
                        for u in range(min(U, groups)):
                            pool.wait_ge(S(f"scattered{u}"), S.at(f"scattered{u}", 64 * len(range(u, groups, U))))

                @block.tensor
                def _(pe):
                    def stage(s, u, k, r):
                        if s == 0:
                            P, J = shape(k, dense)
                            pe.wait_ge(S("hidden_cols"), S.at("hidden_cols", k + 1))
                            if not fresh(k):
                                pe.wait_ge(S("residual1"), S.at("residual1", k + 1 - U))
                            back_transposes(t0[u], pA[u], P, J).then_inc(S("cols_psum"), 1)

                    steps(pe, 2, groups, stage)

                @block.scalar
                def _(act):
                    def stage(s, u, k, r):
                        if s == 0:
                            P, J = shape(k, dense)
                            act.wait_ge(S(f"loaded{u}"), S.at(f"loaded{u}", (r + 1) * 32))
                            if not fresh(k):
                                act.wait_ge(S("cols_psum"), S.at("cols_psum", k + 1 - U))
                            nc.scalar.activation(t0[u][:, 0:P * J], t1[u][:, 0:P * J], ACTF.Relu, bias=bn[:, b_t2:b_t2 + 1],
                                                 scale=bn[:, b_s2:b_s2 + 1]).then_inc(S("hidden_cols"), 1)

                    steps(act, 2, groups, stage)

                @block.vector
                def _(dve):
                    def stage(s, u, k, r):
                        P, J = shape(k, dense)
                        if s == 0:
                            dve.wait_ge(S("cols_psum"), S.at("cols_psum", k + 1))
                            dve.wait_ge(S(f"loaded{u}"), S.at(f"loaded{u}", (r + 1) * 32))
                            if not fresh(k):
                                dve.wait_ge(S("normed1"), S.at("normed1", k + 1 - U))
                            nc.vector.scalar_tensor_tensor(nm(t3[u])[0:P, 0:J, :], Dn[u][0:P, 0:J, :], 2.0,
                                                           nm(pA[u])[0:P, 0:J, :], ALU.mult,
                                                           ALU.add).then_inc(S("residual1"), 1)
                            stats(dve, u, k, P, J, nm(t3[u]), 1)
                        else:
                            if not fresh(k):
                                dve.wait_ge(S(f"{kind}{u}"), S.at(f"{kind}{u}", r * per_store))
                            normalise(dve, u, k, P, J, nm(t3[u]), O[u], 1)

                    steps(dve, 2, groups, stage)
            finish(groups, ["hidden_cols", "cols_psum"] + ln_signals(1) + ([] if dense else ["indices0"]), loaded=32,
                   **{kind: per_store})

        in_flight(7, 1, "Dn O t0 t1 t3")
        last_norm(NG, True)
        last_norm(EG, False)


_INPUTS = ["x", "src", "dst", "edge_attr_128", "L0_gnn_W0", "L0_gnn_b0", "L0_gnn_W1", "L0_gnn_b1", "L0_gnn_W2",
           "L0_gnn_b2", "L1_gnn_W", "L1_gnn_att_src", "L1_gnn_att_dst", "L1_gnn_bias", "L1_gnn_fc_w", "L1_gnn_fc_b",
           "L2_gnn_Wi", "L2_gnn_bi", "L2_gnn_Wm", "L2_gnn_bm", "L2_gnn_Wu", "L2_gnn_bu", "L3_gnn_eps", "L3_gnn_W1",
           "L3_gnn_g1", "L3_gnn_b1", "L3_gnn_W2", "L3_gnn_g2", "L3_gnn_b2"]


def kernel(**inputs):
    import concourse.bacc as bacc
    from concourse.bass_utils import run_bass_kernel_spmd

    nc = bacc.Bacc("TRN2", target_bir_lowering=False, num_devices=1)
    arrays, views = {}, {}
    for name in _INPUTS:
        v = np.asarray(inputs[name])
        v = np.ascontiguousarray(v.reshape(v.shape or (1,)))
        arrays[f"in_{name}"] = v
        views[name] = nc.dram_tensor(f"in_{name}", v.shape, mybir.dt.from_np(v.dtype), kind="ExternalInput").ap()
    out = nc.dram_tensor("out", views["x"].shape, F32, kind="ExternalOutput").ap()
    build(nc, views, out)
    got = run_bass_kernel_spmd(nc, [arrays], core_ids=[0])
    return got.results[0]["out"]
```

```python
import numpy as np
import concourse.bass as bass
from concourse import mybir
from contextlib import ExitStack

F32, BF16, I32 = mybir.dt.float32, mybir.dt.bfloat16, mybir.dt.int32
ALU, ACTF, AX = mybir.AluOpType, mybir.ActivationFunctionType, mybir.AxisListType

MOST = 7
D = 128
GC = 512
LN_EPS = 1e-5
BN_EPS = 1e-5
SLOPE = 0.2
FAR = 1e30


class Signals:

    def __init__(self, nc, ctx):
        self.nc, self.ctx, self.handle, self.base, self.spare = nc, ctx, {}, {}, []

    def __call__(self, name):
        if name not in self.handle:
            if self.spare:
                self.handle[name], self.base[name] = self.spare.pop()
            else:
                self.handle[name], self.base[name] = self.ctx.enter_context(self.nc.semaphore(name)), 0
        return self.handle[name]

    def retire(self, names):
        for name in names:
            self.spare.append((self.handle.pop(name), self.base.pop(name)))

    def at(self, name, n):
        self(name)
        return n + self.base[name]

    def passed(self, totals):
        for name, n in totals.items():
            self(name)
            self.base[name] += n


def build(nc, a, out):
    N = a["x"].shape[0]
    E = a["src"].shape[0]
    EG = -(-E // GC)
    EP = EG * GC
    ET = EP // 128
    NF = N // GC
    R = N - NF * GC
    TJ = next(j for j in (4, 3, 2, 1) if R % j == 0 and (R // j) % 16 == 0 and R // j <= 128) if R else 4
    TP = R // TJ if R else 128
    NG = NF + (R > 0)
    EQ = next(p for p in range(128, 0, -1) if E % p == 0)
    EW = E // EQ
    PADS = EP + 128 - E
    HEADS, HID = a["L1_gnn_att_src"].shape
    HC = HID // 2
    ROUNDS = a["L2_gnn_Wm"].shape[0]
    assert HEADS * HC == D and N + EP < 1 << 24 and EG >= 2 and NG >= 2 and ET <= 128

    ctx = ExitStack()
    with ctx:
        def sb(name, shape, dt=F32):
            return ctx.enter_context(nc.sbuf_tensor(name, shape, dt))

        def dram(name, shape, dt=F32):
            return nc.dram_tensor(name, shape, dt).ap()

        S = Signals(nc, ctx)
        psum = [ctx.enter_context(nc.psum_tensor(f"bank{i}", [128, GC], F32)) for i in range(8)]
        pGram, pMisc = psum[7], psum[6]

        sorted_src = dram("sorted_src", [EP + 128], I32)
        sorted_dst = dram("sorted_dst", [EP + 128], I32)
        sorted_edge = dram("sorted_edge", [EP + 128], I32)
        keep_row = dram("keep_row", [EP])
        count_row = dram("count_row", [EP])
        way_row = dram("way_row", [EP])
        node_slot = dram("node_slot", [N])
        gcn_table = [dram(f"gcn_table{i}", [2 * EP, D]) for i in range(3)]
        gat_table = dram("gat_table", [2 * EP, D])
        mpn_table = [dram(f"mpn_table{i}", [2 * EP, D]) for i in range(2)]
        x0_slots = dram("x0_slots", [EP, D])
        x2_slots = dram("x2_slots", [EP, D])
        x3_table = dram("x3_table", [2 * EP, D])
        attr_slots = dram("attr_slots", [EP, D])
        z_slots = dram("z_slots", [EP, D])
        x3_nodes = dram("x3_nodes", [N, D])
        y_cols = dram("y_cols", [D, N + EP])

        ident = sb("ident", [128, 128])
        zeros = sb("zeros", [128, D + 1])
        ones_bf = sb("ones_bf", [128, 128], BF16)
        W0, W1, W2 = (sb(f"W{i}", [D, D]) for i in range(3))
        Wg = sb("Wg", [D, 2, D])
        fcw = sb("fcw", [D, 2, D])
        Wi = sb("Wi", [D, D])
        Wm = sb("Wm", [D, ROUNDS, D])
        Wu = sb("Wu", [D, ROUNDS, D])
        V1 = sb("V1", [D, 2, D])
        V2 = sb("V2", [D, 2, D])
        attS, attD, attSD = (sb(n, [D, D]) for n in ("attS", "attD", "attSD"))
        ROWS = 3 + ROUNDS
        row_b2, row_fc, row_bi, row_bu = 0, 1, 2, 3
        rows = sb("rows", [128, ROWS, D])
        bias3 = sb("bias3", [128, ROWS, D], BF16)
        rowb0, rowb1 = sb("rowb0", [128, D]), sb("rowb1", [128, D])
        cu = sb("cu", [128, ROUNDS, D])
        c_all = sb("c_all", [128, D])
        cb = sb("cb", [128, 16])
        c_b0, c_b1, c_gat, c_bm, c_bu, c_cum = 0, 1, 2, 4, 8, 12
        bn = sb("bn", [128, 16])
        b_g1, b_b1, b_g2, b_b2, b_s1, b_t1, b_s2, b_t2 = 0, 2, 4, 5, 6, 8, 10, 11
        eps1 = sb("eps1", [128, 1])
        neg_half = sb("neg_half", [128, 4])
        neg_far = sb("neg_far", [128, 1])
        idx = sb("idx", [128, ET], I32)
        idx_own = sb("idx_own", [128, ET], I32)
        src_i = sb("src_i", [128, ET], I32)
        edge_i = sb("edge_i", [128, ET], I32)
        dst_g = sb("dst_g", [128, ET], I32)
        dst_s = sb("dst_s", [128, ET], I32)
        dinv = sb("dinv", [128, ET])
        LOOKUPS = 4
        row_f = sb("row_f", [128, ET])
        pos = sb("pos", [128, ET])
        posN = sb("posN", [128, 4 * NG])
        w0, w1 = sb("w0", [128, ET]), sb("w1", [128, ET])
        sti = [sb(f"sti{u}", [128, 4], I32) for u in range(LOOKUPS)]
        stv = [sb(f"stv{u}", [128, 4]) for u in range(LOOKUPS)]
        last = sb("last", [128, ET])
        nmask = sb("nmask", [128, 4 * NG])
        ystat = sb("ystat", [128, NG + EG, 6])
        small = sb("small", [128, 24])
        gram = sb("gram", [D, D + 1])
        mrow = sb("mrow", [1, D])
        prod = sb("prod", [D, 2, D])
        onesc = sb("onesc", [128, 1])


        loads = []

        def column(dst, vec):
            loads.append((dst, vec.rearrange("(p o) -> p o", o=1)))

        def row(dst, vec):
            loads.append((dst, vec.partition_broadcast(128)))

        for dst, name in ((W0, "L0_gnn_W0"), (W1, "L0_gnn_W1"), (W2, "L0_gnn_W2"), (Wi, "L2_gnn_Wi")):
            loads.append((dst[:, :], a[name]))
        loads.append((Wm[:, :, :], a["L2_gnn_Wm"].rearrange("r i o -> i r o")))
        loads.append((Wu[:, :, :], a["L2_gnn_Wu"].rearrange("r i o -> i r o")))
        loads.append((V1[:, :, :], a["L3_gnn_W1"].rearrange("i (c o) -> i c o", c=2)))
        loads.append((V2[:, :, :], a["L3_gnn_W2"].rearrange("(c i) o -> i c o", c=2)))
        for c in range(2):
            for h in range(HEADS):
                at = HID * h + HC * c
                loads.append((Wg[:, c, HC * h:HC * (h + 1)], a["L1_gnn_W"][:, at:at + HC]))
                loads.append((fcw[HC * h:HC * (h + 1), c, :], a["L1_gnn_fc_w"][at:at + HC, :]))
                column(cb[HC * h:HC * (h + 1), c_gat + c:c_gat + c + 1], a["L1_gnn_bias"][at:at + HC])
            column(bn[:, b_g1 + c:b_g1 + c + 1], a["L3_gnn_g1"][c * D:(c + 1) * D])
            column(bn[:, b_b1 + c:b_b1 + c + 1], a["L3_gnn_b1"][c * D:(c + 1) * D])
        column(bn[:, b_g2:b_g2 + 1], a["L3_gnn_g2"])
        column(bn[:, b_b2:b_b2 + 1], a["L3_gnn_b2"])
        column(cb[:, c_b0:c_b0 + 1], a["L0_gnn_b0"])
        column(cb[:, c_b1:c_b1 + 1], a["L0_gnn_b1"])
        row(rowb0[:, :], a["L0_gnn_b0"])
        row(rowb1[:, :], a["L0_gnn_b1"])
        row(rows[:, row_b2, :], a["L0_gnn_b2"])
        row(rows[:, row_fc, :], a["L1_gnn_fc_b"])
        row(rows[:, row_bi, :], a["L2_gnn_bi"])
        for r in range(ROUNDS):
            column(cb[:, c_bm + r:c_bm + r + 1], a["L2_gnn_bm"][r])
            column(cb[:, c_bu + r:c_bu + r + 1], a["L2_gnn_bu"][r])
            row(rows[:, row_bu + r, :], a["L2_gnn_bu"][r])
        row(eps1[:, :], a["L3_gnn_eps"])

        def tick(eng, name="pool_tick"):
            eng.sem_inc(S(name), 1)

        class Chain:

            def __init__(self, eng, name):
                self.eng, self.name, self.n = eng, name, 0

            def after(self, ins):
                ins.then_inc(S(self.name), 1)
                self.n += 1
                self.eng.wait_ge(S(self.name), S.at(self.name, self.n))

            def close(self):
                S.passed({self.name: self.n})
                self.n = 0

        with ExitStack() as scratch:
            def tmp(name, shape, dt=F32):
                return scratch.enter_context(nc.sbuf_tensor(name, shape, dt))

            wraw = tmp("wraw", [D, HEADS * HID])
            attb = tmp("attb", [D, 2, HEADS * HID])
            attp = tmp("attp", [D, 2, HEADS * HID])
            att4 = tmp("att4", [D, 3, HEADS])
            hi, mid, lo = (tmp(n, [128, ROWS, D], BF16) for n in ("hi", "mid", "lo"))
            rest = tmp("rest", [128, ROWS, D])
            loads.append((wraw[:, :], a["L1_gnn_W"]))
            row(attb[:, 0, :], a["L1_gnn_att_src"].rearrange("h f -> (h f)"))
            row(attb[:, 1, :], a["L1_gnn_att_dst"].rearrange("h f -> (h f)"))
            dA, sA, eA = (tmp(n, [EQ, EW], I32) for n in ("dA", "sA", "eA"))
            dN = tmp("dN", [EQ, 1], I32)
            loads.append((dA[:, :], a["dst"].rearrange("(p w) -> p w", w=EW)))
            loads.append((sA[:, :], a["src"].rearrange("(p w) -> p w", w=EW)))
            loads.append((dN[0:EQ - 1, :], a["dst"][EW:E].rearrange("(p w) -> p w", w=EW)[:, 0:1]))
            viol = tmp("viol", [EQ, EW])
            violc = tmp("violc", [EQ, 1])
            ones_f = tmp("ones_f", [128, 1])
            flag = tmp("flag", [1, 1], I32)
            pad_d, pad_z = tmp("pad_d", [1, PADS], I32), tmp("pad_z", [1, PADS], I32)
            iota_i = tmp("iota_i", [128, 128], I32)
            iota_f = tmp("iota_f", [128, 128])

            with nc.Block() as block:
                @block.sync
                def _(sp):
                    with nc.allow_non_contiguous_dma(reason="bias columns"):
                        for dst, src in loads:
                            sp.dma_start(dst, src).then_inc(S("weights"), 16)
                    sp.wait_ge(S("weights"), S.at("weights", 16 * len(loads)))

                @block.gpsimd
                def _(pool):
                    nc.gpsimd.memset(neg_half[:, :], -0.5)
                    nc.gpsimd.memset(neg_far[:, :], -FAR)
                    nc.gpsimd.memset(onesc[:, :], 1.0)
                    nc.gpsimd.iota(iota_i[:, :], [[1, 128]], base=0, channel_multiplier=-1)
                    nc.gpsimd.iota(eA[:, :], [[1, EW]], base=0, channel_multiplier=EW)
                    nc.gpsimd.iota(pad_d[:, :], [[1, PADS]], base=N + E, channel_multiplier=0).then_inc(S("iotas"), 1)
                    nc.gpsimd.memset(pad_z[:, :], 0)

                @block.vector
                def _(dve):
                    ch = Chain(dve, "dve_setup")
                    nc.vector.memset(ones_bf[:, :], 1.0)
                    nc.vector.memset(zeros[:, :], 0.0)
                    nc.vector.memset(ones_f[:, :], 1.0)
                    ch.after(nc.vector.memset(viol[:, :], 0.0))
                    dve.wait_ge(S("iotas"), S.at("iotas", 1))
                    ch.after(nc.vector.tensor_copy(iota_f[:, :], iota_i[:, :]))
                    ch.after(nc.vector.tensor_scalar(ident[:, :], iota_f[:, :], 0.0, None, ALU.is_equal))
                    dve.wait_ge(S("weights"), S.at("weights", 16 * len(loads)))
                    for i in range(2):
                        ch.after(nc.vector.tensor_tensor(attp[:, i, :], wraw[:, :], attb[:, i, :], ALU.mult))
                    ch.after(nc.vector.tensor_reduce(att4[:, 0:2, :].rearrange("p i h -> p (i h)"),
                                                     attp[:, :, :].rearrange("p i (h f) -> p (i h) f", h=HEADS),
                                                     AX.X, ALU.add))
                    ch.after(nc.vector.tensor_tensor(att4[:, 2, :], att4[:, 0, :], att4[:, 1, :], ALU.add))
                    for i, w in enumerate((attS, attD, attSD)):
                        for h in range(HEADS):
                            nc.vector.tensor_copy(w[:, HC * h:HC * (h + 1)], att4[:, i, h:h + 1].to_broadcast([D, HC]))
                    ch.after(nc.vector.tensor_copy(hi[:, :, :], rows[:, :, :]))
                    ch.after(nc.vector.tensor_tensor(rest[:, :, :], rows[:, :, :], hi[:, :, :], ALU.subtract))
                    ch.after(nc.vector.tensor_copy(mid[:, :, :], rest[:, :, :]))
                    ch.after(nc.vector.tensor_tensor(lo[:, :, :], rest[:, :, :], mid[:, :, :], ALU.subtract))
                    ch.after(nc.vector.tensor_scalar(bias3[:, :, :], hi[:, :, :], ident[:, 0:1], None, ALU.mult))
                    for i, part in ((1, mid), (2, lo)):
                        ch.after(nc.vector.scalar_tensor_tensor(bias3[:, :, :], part[:, :, :], ident[:, i:i + 1],
                                                                bias3[:, :, :], ALU.mult, ALU.add))
                    ch.after(nc.vector.tensor_scalar(cu[:, :, :], rows[:, row_bu:row_bu + ROUNDS, :], 0.0, None, ALU.max))
                    ch.after(nc.vector.tensor_tensor(c_all[:, :], cu[:, 0, :], cu[:, 1, :], ALU.add))
                    for r in range(2, ROUNDS):
                        ch.after(nc.vector.tensor_tensor(c_all[:, :], c_all[:, :], cu[:, r, :], ALU.add))
                    ch.after(nc.vector.tensor_scalar(cb[:, c_bu:c_bu + ROUNDS], cb[:, c_bu:c_bu + ROUNDS], 0.0, None, ALU.max))
                    ch.after(nc.vector.memset(cb[:, c_cum:c_cum + 1], 0.0))
                    for r in range(1, ROUNDS):
                        ch.after(nc.vector.tensor_tensor(cb[:, c_cum + r:c_cum + r + 1], cb[:, c_cum + r - 1:c_cum + r],
                                                         cb[:, c_bu + r - 1:c_bu + r], ALU.add))
                    S("cum")
                    nc.vector.tensor_scalar(eps1[:, :], eps1[:, :], 1.0, None, ALU.add).then_inc(S("cum"), 1)
                    dve.wait_ge(S("cum_p"), S.at("cum_p", 1))
                    ch.after(nc.vector.tensor_tensor(cb[:, c_bm:c_bm + ROUNDS], cb[:, c_bm:c_bm + ROUNDS],
                                                     pMisc[:, 0:ROUNDS], ALU.add))
                    ch.after(nc.vector.tensor_tensor(viol[:, 0:EW - 1], dA[:, 1:EW], dA[:, 0:EW - 1], ALU.is_lt))
                    ch.after(nc.vector.tensor_tensor(viol[0:EQ - 1, EW - 1:EW], dN[0:EQ - 1, :],
                                                     dA[0:EQ - 1, EW - 1:EW], ALU.is_lt))
                    nc.vector.tensor_reduce(violc[:, :], viol[:, :], AX.X, ALU.add).then_inc(S("violc"), 1)
                    dve.wait_ge(S("viol_p"), S.at("viol_p", 1))
                    ch.after(nc.vector.tensor_copy(flag[:, :], pMisc[0:1, 8:9]))
                    ch.close()

                @block.tensor
                def _(pe):
                    pe.wait_ge(S("cum"), S.at("cum", 1))
                    for r in range(ROUNDS):
                        ins = nc.tensor.matmul(pMisc[:, r:r + 1], Wm[:, r, :], cb[:, c_cum + r:c_cum + r + 1],
                                               start=True, stop=True)
                    ins.then_inc(S("cum_p"), 1)
                    pe.wait_ge(S("violc"), S.at("violc", 1))
                    nc.tensor.matmul(pMisc[0:1, 8:9], violc[:, :], ones_f[0:EQ, :],
                                     start=True, stop=True).then_inc(S("viol_p"), 1)
            S.passed({"weights": 16 * len(loads), "iotas": 1, "cum": 1, "cum_p": 1, "violc": 1, "viol_p": 1})

            EF = E // 128
            ER = E - EF * 128
            DT_ = EF + (ER > 0)
            drow = tmp("drow", [128, E], I32)
            irow = tmp("irow", [128, E], I32)
            before_me = tmp("before_me", [128, E], BF16)
            equal_me = tmp("equal_me", [128, E], BF16)
            me = tmp("me", [128, 3, 1])
            me_i = tmp("me_i", [128, 4], I32)

            with nc.Block() as block:
                @block.sync
                def _(sp):
                    sp.dma_start(sorted_dst[E:EP + 128].rearrange("(o w) -> o w", o=1), pad_d[:, :]).then_inc(S("pads"), 16)
                    sp.dma_start(sorted_src[E:EP + 128].rearrange("(o w) -> o w", o=1), pad_z[:, :]).then_inc(S("pads"), 16)
                    sp.dma_start(sorted_edge[E:EP + 128].rearrange("(o w) -> o w", o=1), pad_z[:, :]).then_inc(S("pads"), 16)
                    sp.wait_ge(S("pads"), S.at("pads", 48))
                    unsorted = sp.value_load(flag[0:1, 0:1], min_val=0, max_val=E)
                    with sp.If(unsorted == 0):
                        for to, frm in ((sorted_dst, dA), (sorted_src, sA), (sorted_edge, eA)):
                            sp.dma_start(to[0:E].rearrange("(p w) -> p w", w=EW), frm[:, :]).then_inc(S("copied"), 16)
                        sp.wait_ge(S("copied"), S.at("copied", 48))

                @block.vector
                def _(dve):
                    unsorted = dve.value_load(flag[0:1, 0:1], min_val=0, max_val=E)
                    with dve.If(unsorted > 0):
                        dve.wait_ge(S("rank_in"), S.at("rank_in", 1))

                        def tile(t, P):
                            dve.wait_ge(S("me_in"), S.at("me_in", t + 1))
                            nc.vector.tensor_scalar(before_me[0:P, :], irow[0:P, :], me[0:P, 1, :], None,
                                                    ALU.is_lt).then_inc(S("rk0"), 1)
                            dve.wait_ge(S("rk0"), S.at("rk0", t + 1))
                            nc.vector.scalar_tensor_tensor(equal_me[0:P, :], drow[0:P, :], me[0:P, 0, :], before_me[0:P, :],
                                                           ALU.is_equal, ALU.mult).then_inc(S("rk1"), 1)
                            dve.wait_ge(S("rk1"), S.at("rk1", t + 1))
                            nc.vector.scalar_tensor_tensor(before_me[0:P, :], drow[0:P, :], me[0:P, 0, :], equal_me[0:P, :],
                                                           ALU.is_lt, ALU.add, accum_out=me[0:P, 2, :]).then_inc(S("rk2"), 1)
                            dve.wait_ge(S("rk2"), S.at("rk2", t + 1))
                            nc.vector.tensor_copy(me_i[0:P, 3:4], me[0:P, 2, :]).then_inc(S("rank"), 1)

                        with dve.Fori(0, EF) as t:
                            tile(t, 128)
                        if ER:
                            tile(EF, ER)

                @block.gpsimd
                def _(pool):
                    unsorted = pool.value_load(flag[0:1, 0:1], min_val=0, max_val=E)
                    with pool.If(unsorted > 0):
                        nc.gpsimd.iota(irow[:, :], [[1, E]], base=0, channel_multiplier=0).then_inc(S("rank_iota"), 1)
                        pool.dma_start(drow[:, :], a["dst"].partition_broadcast(128)).then_inc(S("rank_row"), 16)
                        pool.wait_ge(S("rank_iota"), S.at("rank_iota", 1))
                        pool.wait_ge(S("rank_row"), S.at("rank_row", 16))
                        nc.gpsimd.memset(me_i[:, :], 0).then_inc(S("rank_in"), 1)
                        pool.wait_ge(S("rank_in"), S.at("rank_in", 1))

                        def tile(t, P):
                            for i, frm in ((0, a["dst"]), (1, a["src"])):
                                pool.dma_start(me_i[0:P, i:i + 1],
                                               frm[bass.ds(t * 128, P)].rearrange("(p o) -> p o", o=1)).then_inc(S("me_ld"), 16)
                            pool.wait_ge(S("me_ld"), S.at("me_ld", t * 32 + 32))
                            tick(pool)
                            nc.gpsimd.tensor_copy(me[0:P, 0, :], me_i[0:P, 0:1]).then_inc(S("me_d"), 1)
                            pool.wait_ge(S("me_d"), S.at("me_d", t + 1))
                            tick(pool)
                            nc.gpsimd.tensor_copy(me_i[0:P, 2:3], pos[0:P, :]).then_inc(S("me_p"), 1)
                            pool.wait_ge(S("me_p"), S.at("me_p", t + 1))
                            tick(pool)
                            nc.gpsimd.tensor_copy(me[0:P, 1, :], me_i[0:P, 2:3]).then_inc(S("me_in"), 1)
                            pool.wait_ge(S("me_in"), S.at("me_in", t + 1))
                            nc.gpsimd.tensor_tensor(pos[:, :], pos[:, :], step128[:, :], ALU.add).then_inc(S("me_n"), 1)
                            pool.wait_ge(S("me_n"), S.at("me_n", t + 1))
                            pool.wait_ge(S("rank"), S.at("rank", t + 1))
                            tick(pool)
                            for i, to in ((0, sorted_dst), (1, sorted_src), (2, sorted_edge)):
                                nc.gpsimd.indirect_dma_start(
                                    out=to.rearrange("(n o) -> n o", o=1), in_=me_i[0:P, i:i + 1], in_offset=None,
                                    out_offset=bass.IndirectOffsetOnAxis(ap=me_i[0:P, 3:4], axis=0)).then_inc(S("me_out"), 16)
                            pool.wait_ge(S("me_out"), S.at("me_out", t * 48 + 48))

                        pos, step128 = iota_i[:, 0:1], iota_i[:, 1:2]
                        nc.gpsimd.iota(pos, [[0, 1]], base=0, channel_multiplier=1).then_inc(S("me_c"), 1)
                        nc.gpsimd.iota(step128, [[0, 1]], base=128, channel_multiplier=0).then_inc(S("me_c"), 1)
                        pool.wait_ge(S("me_c"), S.at("me_c", 2))
                        with pool.Fori(0, EF) as t:
                            tile(t, 128)
                        if ER:
                            tile(EF, ER)
            S.passed({"pads": 48})

        NP_ = next(p for p in range(128, 0, -1) if N % p == 0)
        with ExitStack() as scratch:
            def tmp(name, shape, dt=F32):
                return scratch.enter_context(nc.sbuf_tensor(name, shape, dt))

            dT, sT, eT, pT, nT = (tmp(n, [ET, 128], I32) for n in ("dT", "sT", "eT", "pT", "nT"))
            flags = tmp("flags", [ET, 7, 128])
            real = tmp("real", [ET, 128])
            keep1, count1, way1 = tmp("keep_line", [1, EP + 1]), tmp("count_line", [1, EP]), tmp("way_line", [1, EP])
            way_i, way_j = tmp("way_i", [128, ET], I32), tmp("way_j", [128, ET], I32)
            one1 = tmp("one1", [1, 1])
            cols = tmp("cols", [128, 6, ET])
            row_i, far_i = tmp("row_i", [128, ET], I32), tmp("far_i", [128, ET], I32)
            far_f = tmp("far_f", [128, ET])
            none = tmp("none", [NP_, N // NP_])
            half = tmp("half", [128, ET])
            tiles = [(sorted_dst, dT), (sorted_src, sT), (sorted_edge, eT)]

            def as_tiles(t, first=0):
                return t[first:first + EP].rearrange("(t p) -> t p", p=128)

            with nc.Block() as block:
                @block.sync
                def _(sp):
                    for frm, to in tiles:
                        sp.dma_start(to[:, :], as_tiles(frm)).then_inc(S("tiles_in"), 16)
                    sp.dma_start(nT[:, :], as_tiles(sorted_dst, 1)).then_inc(S("tiles_in"), 16)
                    sp.dma_start(pT[1:ET, :], sorted_dst[127:EP - 1].rearrange("(t p) -> t p", p=128)).then_inc(S("tiles_in"), 16)
                    sp.dma_start(pT[0:1, 1:128], sorted_dst[0:127].rearrange("(t p) -> t p", t=1)).then_inc(S("tiles_in"), 16)
                    sp.wait_ge(S("keep_ok"), S.at("keep_ok", 1))
                    sp.dma_start(as_tiles(keep_row), flags[:, 3, :]).then_inc(S("rows_io"), 16)
                    sp.wait_ge(S("rows_io"), S.at("rows_io", 16))
                    sp.dma_start(keep1[:, 0:EP], keep_row.rearrange("(o w) -> o w", o=1)).then_inc(S("rows_io"), 16)
                    sp.wait_ge(S("rows_io"), S.at("rows_io", 32))
                    sp.nop().then_inc(S("keep1_in"), 1)
                    sp.wait_ge(S("count_ok"), S.at("count_ok", 1))
                    sp.dma_start(count_row.rearrange("(o w) -> o w", o=1), count1[:, :]).then_inc(S("rows_io"), 16)
                    sp.wait_ge(S("rows_io"), S.at("rows_io", 48))
                    sp.dma_start(flags[:, 5, :], as_tiles(count_row)).then_inc(S("rows_io"), 16)
                    sp.wait_ge(S("rows_io"), S.at("rows_io", 64))
                    sp.wait_ge(S("way_ok"), S.at("way_ok", 1))
                    sp.dma_start(way_row.rearrange("(o w) -> o w", o=1), way1[:, :]).then_inc(S("rows_io"), 16)
                    sp.wait_ge(S("rows_io"), S.at("rows_io", 80))
                    sp.dma_start(flags[:, 6, :], as_tiles(way_row)).then_inc(S("rows_io"), 16)
                    sp.wait_ge(S("none_ok"), S.at("none_ok", 1))
                    sp.dma_start(node_slot.rearrange("(p w) -> p w", p=NP_), none[:, :]).then_inc(S("none_out"), 16)
                    sp.wait_ge(S("rows_io"), S.at("rows_io", 96))
                    sp.wait_ge(S("none_out"), S.at("none_out", 16))

                @block.gpsimd
                def _(pool):
                    nc.gpsimd.iota(row_i[:, :], [[GC, EG], [1, 4]], base=0, channel_multiplier=4)
                    nc.gpsimd.iota(far_i[:, :], [[128, ET]], base=N, channel_multiplier=1).then_inc(S("slot_iotas"), 1)
                    nc.gpsimd.memset(half[:, :], -0.5)

                @block.vector
                def _(dve):
                    ch = Chain(dve, "dve_setup")
                    nc.vector.memset(pT[0:1, 0:1], -1).then_inc(S("first_prev"), 1)
                    nc.vector.memset(one1[:, :], 1.0)
                    ch.after(nc.vector.memset(keep1[:, EP:EP + 1], 0.0))
                    nc.vector.memset(none[:, :], -1.0).then_inc(S("none_ok"), 1)
                    dve.wait_ge(S("slot_iotas"), S.at("slot_iotas", 1))
                    nc.vector.tensor_copy(row_f[:, :], row_i[:, :])
                    nc.vector.tensor_copy(far_f[:, :], far_i[:, :])
                    dve.wait_ge(S("first_prev"), S.at("first_prev", 1))
                    dve.wait_ge(S("tiles_in"), S.at("tiles_in", 96))
                    nc.vector.tensor_tensor(flags[:, 3, :], dT[:, :], pT[:, :], ALU.is_equal).then_inc(S("keep_ok"), 1)
                    for i, t in enumerate((dT, sT, eT)):
                        nc.vector.tensor_copy(flags[:, i, :], t[:, :])
                    nc.vector.tensor_scalar(real[:, :], dT[:, :], float(N), None, ALU.is_lt)
                    ch.after(nc.vector.tensor_tensor(flags[:, 4, :], dT[:, :], nT[:, :], ALU.not_equal))
                    ch.after(nc.vector.tensor_tensor(flags[:, 4, :], flags[:, 4, :], real[:, :], ALU.mult))
                    dve.wait_ge(S("keep1_in"), S.at("keep1_in", 1))
                    nc.vector.tensor_tensor_scan(count1[:, :], keep1[:, 0:EP], one1[:, 0:1].to_broadcast([1, EP]), 0.0,
                                                 ALU.mult, ALU.add).then_inc(S("count_ok"), 1)
                    nc.vector.tensor_tensor_scan(way1[:, ::-1], keep1[:, EP:0:-1], keep1[:, EP:0:-1], 0.0,
                                                 ALU.mult, ALU.add).then_inc(S("way_ok"), 1)
                    dve.wait_ge(S("flags_p"), S.at("flags_p", 1))
                    ch.after(nc.vector.tensor_copy(cols[:, 0:4, :], pMisc[:, 0:4 * ET].rearrange("p (i t) -> p i t", i=4)))
                    ch.after(nc.vector.tensor_copy(cols[:, 4:6, :], pGram[:, 0:2 * ET].rearrange("p (i t) -> p i t", i=2)))
                    nc.vector.tensor_copy(src_i[:, :], cols[:, 1, :])
                    nc.vector.tensor_copy(edge_i[:, :], cols[:, 2, :])
                    nc.vector.tensor_copy(last[:, :], cols[:, 3, :])
                    ch.after(nc.vector.tensor_scalar(w0[:, :], cols[:, 0, :], float(N), None, ALU.is_lt))
                    ch.after(nc.vector.tensor_tensor(dst_g[:, :], w0[:, :], cols[:, 0, :], ALU.mult))
                    ch.after(nc.vector.tensor_tensor(w0[:, :], cols[:, 0, :], far_f[:, :], ALU.subtract))
                    ch.after(nc.vector.tensor_tensor(w0[:, :], w0[:, :], cols[:, 3, :], ALU.mult))
                    ch.after(nc.vector.tensor_tensor(dst_s[:, :], w0[:, :], far_f[:, :], ALU.add))
                    ch.after(nc.vector.tensor_scalar(cols[:, 4, :], cols[:, 4, :], 1.0, None, ALU.add))
                    ch.after(nc.vector.tensor_tensor(cols[:, 5, :], cols[:, 5, :], far_f[:, :], ALU.add))
                    ch.after(nc.vector.tensor_scalar(way_i[:, :], cols[:, 5, :], float(-N), None, ALU.add))
                    ch.after(nc.vector.tensor_scalar(way_j[:, :], way_i[:, :], 7, 3, ALU.logical_shift_right,
                                                     ALU.bitwise_and))
                    ch.after(nc.vector.tensor_copy(cols[:, 5, :], way_j[:, :]))
                    ch.after(nc.vector.tensor_scalar(way_j[:, :], way_i[:, :], 127, 2, ALU.bitwise_and,
                                                     ALU.logical_shift_left))
                    ch.after(nc.vector.tensor_copy(w0[:, :], way_j[:, :]))
                    ch.after(nc.vector.tensor_scalar(way_j[:, :], way_i[:, :], 9, 9, ALU.logical_shift_right,
                                                     ALU.logical_shift_left))
                    ch.after(nc.vector.tensor_tensor(w0[:, :], w0[:, :], cols[:, 5, :], ALU.add))
                    ch.after(nc.vector.tensor_copy(w1[:, :], way_j[:, :]))
                    ch.after(nc.vector.tensor_tensor(idx_own[:, :], w0[:, :], w1[:, :], ALU.add))
                    ch.close()

                @block.tensor
                def _(pe):
                    pe.wait_ge(S("count_ok"), S.at("count_ok", 1))
                    pe.wait_ge(S("rows_io"), S.at("rows_io", 96))
                    for at, i in enumerate((0, 1, 2, 4)):
                        nc.tensor.transpose(pMisc[:, at * ET:(at + 1) * ET], flags[:, i, :], ident[0:ET, 0:ET])
                    nc.tensor.transpose(pGram[:, 0:ET], flags[:, 5, :], ident[0:ET, 0:ET])
                    nc.tensor.transpose(pGram[:, ET:2 * ET], flags[:, 6, :], ident[0:ET, 0:ET]).then_inc(S("flags_p"), 1)
            S.passed({"tiles_in": 96, "keep_ok": 1, "rows_io": 96, "way_ok": 1, "none_out": 16, "keep1_in": 1, "count_ok": 1, "none_ok": 1,
                      "slot_iotas": 1, "first_prev": 1, "flags_p": 1})

            with nc.Block() as block:
                @block.gpsimd
                def _(pool):
                    nc.gpsimd.tensor_tensor(dinv[:, :], cols[:, 4, :], half[:, :], ALU.pow)

        for u in range(MOST):
            S(f"gathered{u}")
            S(f"scattered{u}")
        S.retire(["weights", "iotas", "cum", "cum_p", "violc", "viol_p", "pads", "tiles_in", "keep_ok", "rows_io",
                  "none_out", "keep1_in", "count_ok", "way_ok", "none_ok", "slot_iotas", "first_prev", "flags_p"])

        U = phases = 0
        held = ctx.enter_context(ExitStack())
        SHAPES = {"A": [128, GC + 1], "Mx": [128, GC + 1], "Sc0": [128, GC + 1], "Sc1": [128, GC + 1],
                  "keep": [128, GC], "soft": [128, 3, GC], "zm": [128, 4, D + 1], "st": [128, 4, 6],
                  "mv": [128, 4, 2], "vpe": [128, 4], "shift": [128, 4], "rstd": [128, 4], "idxs": [128, 8], "G": [128, 4, D], "G2": [128, 4, D], "attr": [128, D],
                  "Dn": [128, 4, D], "O": [128, 4, D], **{f"t{i}": [128, GC] for i in range(8)}}
        buffers = {name: [] for name in SHAPES}
        G, G2, Dn, O, keep, soft, zm = (buffers[n] for n in ("G", "G2", "Dn", "O", "keep", "soft", "zm"))
        A, Mx, Sc0, Sc1 = (buffers[n] for n in ("A", "Mx", "Sc0", "Sc1"))
        st, mv, vpe, shift, rstd, idxs = (buffers[n] for n in ("st", "mv", "vpe", "shift", "rstd", "idxs"))
        attr = buffers["attr"]
        t0, t1, t2, t3, t4, t5, t6, t7 = (buffers[f"t{i}"] for i in range(8))
        pA, pB = [], []

        def in_flight(n, banks, names):
            nonlocal U, phases
            U, phases = n, phases + 1
            pA[:] = psum[0:n]
            pB[:] = psum[0:n] if banks == 1 else psum[n:2 * n]
            held.close()
            names = names.split() + ["st", "mv", "vpe", "shift", "rstd", "idxs"]
            for name in buffers:
                buffers[name][:] = [held.enter_context(nc.sbuf_tensor(
                    f"{name}_{phases}_{u}", SHAPES[name], I32 if name == "idxs" else F32))
                    for u in range(n)] if name in names else []
            with nc.Block() as block:
                @block.vector
                def _(dve):
                    for name in ("A", "Mx", "Sc0", "Sc1"):
                        if name in names:
                            nc.vector.memset(buffers[name][n - 1][:, :], 0.0)
                    for z in zm:
                        nc.vector.memset(z[:, :, :], 1.0)

        def nm(t):
            return t[:, 0:GC].rearrange("p (j d) -> p j d", j=4)

        def shape(k, dense=True):
            return (TP, TJ) if dense and isinstance(k, int) and k >= NF else (128, 4)

        def steps(eng, steps_n, groups, stage, *loads):
            nb = -(-groups // U)

            def body(b):
                for s in range(steps_n):
                    at_step = []
                    for u in range(U):
                        t = s - u * steps_n // U
                        back = 1 if t < 0 else 0
                        k, r = b * U + (u - U * back), b - back
                        if not isinstance(k, int) or 0 <= k < groups:
                            at_step.append((t + steps_n * back, u, k, r))
                    for step, u, k, r in at_step:
                        if stage:
                            stage(step, u, k, r)
                    for step, u, k, r in at_step:
                        for ahead, load in loads:
                            if step == ahead and not (isinstance(k, int) and k + U >= groups):
                                load(u, k + U, r + 1)

            for k in range(min(U, groups)):
                for _, load in loads:
                    load(k, k, 0)
            if nb >= 4:
                body(0)
                with eng.Fori(1, nb - 2) as b:
                    body(b)
                for b in range(nb - 2, nb + 1):
                    body(b)
            else:
                for b in range(nb + 1):
                    body(b)



        def fresh(k):
            return isinstance(k, int) and k < U

        def finish(groups, engine, **dma):
            tot = dict.fromkeys(engine, groups)
            for name, per in dma.items():
                for u in range(U):
                    tot[f"{name}{u}"] = per * len(range(u, groups, U))
            S.passed(tot)


        CREDITED = {"biased_rows": "vector", "scaled_rows": "scalar", "state_rows": "scalar", "state_updated": "vector", "segments_summed": "vector",
                    "update_rows": "scalar", "messages": "scalar", "cols_psum": "tensor", "z_masked": "gpsimd", "y_moments": "vector", "loop_added": "vector",
                    "residual1": "vector", "residual3": "vector"}

        def transposes(src, bank, P=128, J=4):
            for j in range(J):
                ins = nc.tensor.transpose(bank[:, j * P:(j + 1) * P], src[0:P, j, :], ident[0:P, 0:P])
            return ins

        def back_transposes(cols, bank, P=128, J=4):
            for j in range(J):
                ins = nc.tensor.transpose(bank[0:P, j * D:(j + 1) * D], cols[:, j * P:(j + 1) * P], ident[:, :])
            return ins

        def to_node_major(bank, parts, P=128, J=4, row=None):
            if row is not None:
                nc.tensor.matmul(bank[0:P, 0:J * D].rearrange("p (j d) -> p j d", j=J), ones_bf[:, 0:P],
                                 bias3[:, row, :].unsqueeze(1).to_broadcast([128, J, D]), start=True, stop=False,
                                 skip_group_check=True)
            for j in range(J):
                for i, (cols, w) in enumerate(parts):
                    ins = nc.tensor.matmul(bank[0:P, j * D:(j + 1) * D], cols[:, j * P:(j + 1) * P], w,
                                           start=(row is None and j == 0 and i == 0),
                                           stop=(i == len(parts) - 1), skip_group_check=True)
            return ins

        def feature_major(bank, parts, C=GC):
            for i, (cols, w) in enumerate(parts):
                ins = nc.tensor.matmul(bank[:, 0:C], w, cols[:, 0:C], start=(i == 0), stop=(i == len(parts) - 1))
            return ins

        def stats(dve, u, k, P, J, src, tag, negated=False):
            dve.wait_ge(S(f"residual{tag}"), S.at(f"residual{tag}", k + 1))
            for j in range(J):
                ins = nc.vector.bn_stats(st[u][0:P, j, :], src[0:P, j, :])
            ins.then_inc(S(f"moments{tag}"), 1)
            dve.wait_ge(S(f"moments{tag}"), S.at(f"moments{tag}", k + 1))
            tick(dve, "vector_tick")
            for j in range(J):
                ins = nc.vector.bn_aggr(mv[u][0:P, j, :], st[u][0:P, j, :])
            ins.then_inc(S(f"variance{tag}"), 1)
            dve.wait_ge(S(f"variance{tag}"), S.at(f"variance{tag}", k + 1))
            if negated:
                nc.vector.tensor_scalar(mv[u][0:P, 0:J, 0], mv[u][0:P, 0:J, 0], -1.0, None, ALU.mult)
            nc.vector.tensor_scalar(vpe[u][0:P, 0:J], mv[u][0:P, 0:J, 1], LN_EPS, None,
                                    ALU.add).then_inc(S(f"var_eps{tag}"), 1)

        def inv_std(pool, u, k, P, J, tag, with_shift=False):
            pool.wait_ge(S(f"var_eps{tag}"), S.at(f"var_eps{tag}", k + 1))
            ins = nc.gpsimd.tensor_tensor(rstd[u][0:P, 0:J], vpe[u][0:P, 0:J], neg_half[0:P, 0:J], ALU.pow)
            if with_shift:
                ins.then_inc(S("inv_std_alone"), 1)
                pool.wait_ge(S("inv_std_alone"), S.at("inv_std_alone", k + 1))
                ins = nc.gpsimd.tensor_tensor(shift[u][0:P, 0:J], mv[u][0:P, 0:J, 0], rstd[u][0:P, 0:J], ALU.mult)
            ins.then_inc(S(f"inv_std{tag}"), 1)

        def normalise(dve, u, k, P, J, src, dst, tag):
            dve.wait_ge(S(f"inv_std{tag}"), S.at(f"inv_std{tag}", k + 1))
            for j in range(J):
                ins = nc.vector.tensor_scalar(dst[0:P, j, :], src[0:P, j, :], mv[u][0:P, j, 0:1],
                                              rstd[u][0:P, j:j + 1], ALU.subtract, ALU.mult)
            ins.then_inc(S(f"normed{tag}"), 1)

        def normalise_on_act(act, u, k, P, J, src, dst, tag):
            act.wait_ge(S(f"inv_std{tag}"), S.at(f"inv_std{tag}", k + 1))
            for j in range(J):
                ins = nc.scalar.activation(dst[0:P, j, :], src[0:P, j, :], ACTF.Identity, bias=shift[u][0:P, j:j + 1],
                                           scale=rstd[u][0:P, j:j + 1])
            ins.then_inc(S(f"normed{tag}"), 1)

        def ln_signals(*tags):
            return [f"{n}{t}" for t in tags for n in ("residual", "moments", "variance", "var_eps", "inv_std", "normed")]

        def scan(dst, d0, d1, before, op0, op1):
            return nc.vector.tensor_tensor_scan(dst[:, 1:GC + 1], d0, d1, before[:, GC:GC + 1], op0, op1)

        def gather(pool, u, k, cols, table, dst, at):
            nc.gpsimd.tensor_copy(idxs[u][:, at:at + 4], cols[:, bass.ds(4 * k, 4)]).then_inc(S(f"indices{at}"), 1)
            pool.wait_ge(S(f"indices{at}"), S.at(f"indices{at}", k + 1))
            tick(pool)
            for j in range(4):
                nc.gpsimd.indirect_dma_start(
                    out=dst[u][:, j, :], out_offset=None, in_=table,
                    in_offset=bass.IndirectOffsetOnAxis(ap=idxs[u][:, at + j:at + j + 1], axis=0),
                ).then_inc(S(f"gathered{u}"), 16)

        def place_last_slots(u, k, r):
            pool = pool_
            if not fresh(k):
                pool.wait_ge(S(f"scattered{u}"), S.at(f"scattered{u}", r * 64))
                tick(pool)
            nc.gpsimd.tensor_copy(idxs[u][:, 4:8], dst_s[:, bass.ds(4 * k, 4)])
            nc.gpsimd.tensor_copy(shift[u][:, 0:4], row_f[:, bass.ds(4 * k, 4)]).then_inc(S("slots_in"), 1)
            pool.wait_ge(S("slots_in"), S.at("slots_in", k + 1))
            tick(pool)
            for j in range(4):
                nc.gpsimd.indirect_dma_start(
                    out=node_slot.rearrange("(n o) -> n o", o=1), in_=shift[u][:, j:j + 1], in_offset=None,
                    out_offset=bass.IndirectOffsetOnAxis(ap=idxs[u][:, 4 + j:5 + j], axis=0),
                    bounds_check=N - 1, oob_is_err=False).then_inc(S(f"scattered{u}"), 16)

        def gather_attr(u, t, r):
            pool = pool_
            if not fresh(t):
                pool.wait_ge(S(f"kept{u}"), S.at(f"kept{u}", r * 16))
            nc.gpsimd.tensor_copy(idxs[u][:, 0:1], edge_i[:, bass.ds(t, 1)]).then_inc(S("indices0"), 1)
            pool.wait_ge(S("indices0"), S.at("indices0", t + 1))
            tick(pool)
            nc.gpsimd.indirect_dma_start(
                out=attr[u][:, :], out_offset=None, in_=a["edge_attr_128"],
                in_offset=bass.IndirectOffsetOnAxis(ap=idxs[u][:, 0:1], axis=0)).then_inc(S(f"gathered{u}"), 16)

        def scatter(pool, u, k, src, table):
            nc.gpsimd.tensor_copy(idxs[u][:, 0:4], dst_s[:, bass.ds(4 * k, 4)]).then_inc(S("indices0"), 1)
            pool.wait_ge(S("indices0"), S.at("indices0", k + 1))
            tick(pool)
            for j in range(4):
                nc.gpsimd.indirect_dma_start(
                    out=table, in_=src[u][:, j, :], in_offset=None,
                    out_offset=bass.IndirectOffsetOnAxis(ap=idxs[u][:, j:j + 1], axis=0),
                    bounds_check=N - 1, oob_is_err=False).then_inc(S(f"scattered{u}"), 16)

        def slot_rows(t, k, half=0):
            return t[bass.ds(k * GC + half * EP, GC), :].rearrange("(p j) d -> p j d", j=4)

        def node_rows(t, k):
            P, J = shape(k)
            return t[bass.ds(k * GC, P * J), :].rearrange("(p j) d -> p j d", j=J)

        def keep_cols(k):
            return keep_row[bass.ds(k * GC, GC)].partition_broadcast(128)

        with nc.Block() as block:
            @block.vector
            def _(dve):
                for name, owner in CREDITED.items():
                    if owner == "vector":
                        dve.nop().then_inc(S(name), MOST)

            @block.scalar
            def _(act):
                for name, owner in CREDITED.items():
                    if owner == "scalar":
                        act.nop().then_inc(S(name), MOST)

            @block.gpsimd
            def _(pool):
                for name, owner in CREDITED.items():
                    if owner == "gpsimd":
                        pool.nop().then_inc(S(name), MOST)

            @block.tensor
            def _(pe):
                for name, owner in CREDITED.items():
                    if owner == "tensor":
                        pe.nop().then_inc(S(name), MOST)
        S.passed({name: MOST for name in CREDITED})

        def chain(groups, dense):
            walk = list(range(15)) if dense else [0, 1, "rows of h1", 2, "rows of h2", *range(3, 12), "residual", 12]
            n_steps, after_residual = len(walk), walk.index(3)
            per_store = 16 if dense else 16 * 6

            def sp_load(u, k, r):
                if not fresh(k):
                    sp_.wait_ge(S("residual1"), S.at("residual1", k + 1 - U))
                P, J = shape(k)
                sp_.dma_start(G[u][0:P, 0:J, :], node_rows(a["x"], k)).then_inc(S(f"loaded{u}"), 16)

            def pool_load(u, k, r):
                if not fresh(k):
                    pool_.wait_ge(S("residual1"), S.at("residual1", k + 1 - U))
                    pool_.wait_ge(S(f"kept{u}"), S.at(f"kept{u}", (r - 1 + 1) * 16))
                gather(pool_, u, k, src_i, a["x"], G, 0)

            def arrived(eng, u, r):
                eng.wait_ge(S(f"loaded{u}"), S.at(f"loaded{u}", (r + 1) * 16)) if dense else eng.wait_ge(S(f"gathered{u}"), S.at(f"gathered{u}", (r + 1) * 64))

            with nc.Block() as block:
                @block.sync
                def _(sp):
                    nonlocal sp_
                    sp_ = sp

                    def stage(step, u, k, r):
                        s = walk[step]
                        if dense and s == 12:
                            P, J = shape(k)
                            sp.wait_ge(S("normed3"), S.at("normed3", k + 1))
                            sp.dma_start(node_rows(x3_nodes, k), O[u][0:P, 0:J, :]).then_inc(S(f"stored{u}"), 16)
                        if dense and s == 9:
                            sp.wait_ge(S(f"gathered{u}"), S.at(f"gathered{u}", (r + 1) * 16))
                            sp.dma_start(attr_slots[bass.ds(k * 128, 128), :], attr[u][:, :]).then_inc(S(f"kept{u}"), 16)
                        if not dense:
                            if s == 0:
                                sp.wait_ge(S(f"gathered{u}"), S.at(f"gathered{u}", (r + 1) * 64))
                                sp.dma_start(slot_rows(gcn_table[0], k, 1), G[u][:, :, :]).then_inc(S(f"kept{u}"), 16)
                            elif s == "rows of h1":
                                sp.wait_ge(S("h1_rows"), S.at("h1_rows", k + 1))
                                sp.dma_start(slot_rows(gcn_table[1], k, 1), O[u][:, :, :]).then_inc(S(f"stored{u}"), 16)
                            elif s == "rows of h2":
                                sp.wait_ge(S("h2_rows"), S.at("h2_rows", k + 1))
                                sp.dma_start(slot_rows(gcn_table[2], k, 1), G2[u][:, :, :]).then_inc(S(f"stored{u}"), 16)
                            elif s == 4:
                                sp.wait_ge(S("normed1"), S.at("normed1", k + 1))
                                sp.dma_start(slot_rows(gat_table, k, 1), nm(t4[u])).then_inc(S(f"stored{u}"), 16)
                            elif s == 11:
                                sp.wait_ge(S("state_rows"), S.at("state_rows", k + 1))
                                for t in mpn_table:
                                    sp.dma_start(slot_rows(t, k, 1), Dn[u][:, :, :]).then_inc(S(f"stored{u}"), 16)
                            elif s == 12:
                                sp.wait_ge(S("normed3"), S.at("normed3", k + 1))
                                sp.dma_start(slot_rows(x3_table, k, 1), nm(t5[u])).then_inc(S(f"stored{u}"), 16)

                    steps(sp, n_steps, groups, stage, *([(after_residual, sp_load)] if dense else []))
                    for u in range(min(U, groups)):
                        sp.wait_ge(S(f"stored{u}"), S.at(f"stored{u}", per_store * len(range(u, groups, U))))
                    for u in range(min(U, groups)):
                        sp.wait_ge(S(f"kept{u}"), S.at(f"kept{u}", (len(range(u, groups, U)) - 1 + 1) * 16))

                @block.gpsimd
                def _(pool):
                    nonlocal pool_
                    pool_ = pool

                    def stage(step, u, k, r):
                        s = walk[step]
                        P, J = shape(k, dense)
                        if s == 3:
                            inv_std(pool, u, k, P, J, 1)
                        elif s == 8:
                            inv_std(pool, u, k, P, J, 2)
                        elif s == 10:
                            pool.wait_ge(S("normed2"), S.at("normed2", k + 1))
                            nc.gpsimd.tensor_tensor(nm(t2[u])[0:P, 0:J, :], nm(t5[u])[0:P, 0:J, :],
                                                    c_all[0:P, :].unsqueeze(1).to_broadcast([P, J, D]),
                                                    ALU.add).then_inc(S("x2_with_gains"), 1)
                        elif s == (11 if dense else "residual"):
                            inv_std(pool, u, k, P, J, 3)
                        elif s == 13 and dense:
                            pool.wait_ge(S("normed3"), S.at("normed3", k + 1))
                            nc.gpsimd.tensor_tensor(zm[u][0:P, 0:J, 0:D], O[u][0:P, 0:J, :],
                                                    nmask[0:P, bass.ds(4 * k, J)].unsqueeze(2).to_broadcast([P, J, D]),
                                                    ALU.mult).then_inc(S("z_masked"), 1)

                    steps(pool, n_steps, groups, stage, *([(10, gather_attr)] if dense else [(after_residual, pool_load), (12, place_last_slots)]))
                    if not dense:
                        for u in range(min(U, groups)):
                            pool.wait_ge(S(f"scattered{u}"), S.at(f"scattered{u}", 64 * len(range(u, groups, U))))

                @block.tensor
                def _(pe):
                    def stage(step, u, k, r):
                        s = walk[step]
                        P, J = shape(k, dense)
                        C = P * J
                        if s == 0:
                            arrived(pe, u, r)
                            if not fresh(k):
                                pe.wait_ge(S("residual3"), S.at("residual3", k + 1 - U))
                            transposes(G[u], pA[u], P, J).then_inc(S("x_transposed"), 1)
                        elif s == 1:
                            pe.wait_ge(S("x_cols"), S.at("x_cols", k + 1))
                            feature_major(pB[u], [(t0[u], W0[:, :])], C).then_inc(S("h1_product"), 1)
                        elif s == "rows of h1":
                            pe.wait_ge(S("h1_cols"), S.at("h1_cols", k + 1))
                            back_transposes(t1[u], pB[u]).then_inc(S("h1_back"), 1)
                        elif s == "rows of h2":
                            pe.wait_ge(S("h2_cols"), S.at("h2_cols", k + 1))
                            back_transposes(t2[u], pA[u]).then_inc(S("h2_back"), 1)
                        elif s == 2:
                            pe.wait_ge(S("h1_cols" if dense else "h1_rows"),
                                       S.at("h1_cols" if dense else "h1_rows", k + 1))
                            feature_major(pA[u], [(t1[u], W1[:, :])], C).then_inc(S("h2_product"), 1)
                        elif s == 3:
                            pe.wait_ge(S("h2_cols" if dense else "h2_rows"),
                                       S.at("h2_cols" if dense else "h2_rows", k + 1))
                            to_node_major(pB[u], [(t2[u], W2[:, :])], P, J, row_b2).then_inc(S("h3_product"), 1)
                        elif s == 5:
                            pe.wait_ge(S("normed1"), S.at("normed1", k + 1))
                            transposes(nm(t4[u]), pA[u], P, J).then_inc(S("x1_transposed"), 1)
                        elif s == 6:
                            pe.wait_ge(S("x1_cols"), S.at("x1_cols", k + 1))
                            feature_major(pB[u], [(t0[u], Wg[:, 0, :])], C).then_inc(S("head_product0"), 1)
                        elif s == 7:
                            pe.wait_ge(S("head_relu0"), S.at("head_relu0", k + 1))
                            feature_major(pA[u], [(t0[u], Wg[:, 1, :])], C).then_inc(S("head_product1"), 1)
                        elif s == 8:
                            pe.wait_ge(S("head_relu1"), S.at("head_relu1", k + 1))
                            to_node_major(pB[u], [(t1[u], fcw[:, 0, :]), (t2[u], fcw[:, 1, :])], P, J,
                                          row_fc).then_inc(S("gat_product"), 1)
                        elif s == 10:
                            pe.wait_ge(S("normed2"), S.at("normed2", k + 1))
                            transposes(nm(t5[u]), pA[u], P, J).then_inc(S("x2_transposed"), 1)
                        elif s == 11:
                            pe.wait_ge(S("x2_cols"), S.at("x2_cols", k + 1))
                            to_node_major(pB[u], [(t0[u], Wi[:, :])], P, J, row_bi).then_inc(S("state_product"), 1)
                        elif s == 14:
                            pe.wait_ge(S("z_masked"), S.at("z_masked", k + 1))
                            for j in range(J):
                                nc.tensor.matmul(pGram[:, 0:D + 1], zm[u][0:P, j, 0:D], zm[u][0:P, j, :],
                                                 start=False, stop=False, skip_group_check=True)

                    steps(pe, n_steps, groups, stage)

                @block.scalar
                def _(act):
                    def relu(out_, in_, bias=0.0):
                        return nc.scalar.activation(out_, in_, ACTF.Relu, bias=bias)

                    def stage(step, u, k, r):
                        s = walk[step]
                        P, J = shape(k, dense)
                        C = P * J
                        if s == 0:
                            act.wait_ge(S("x_transposed"), S.at("x_transposed", k + 1))
                            nc.scalar.copy(t0[u][:, 0:C], pA[u][:, 0:C]).then_inc(S("x_cols"), 1)
                        elif s == 1:
                            act.wait_ge(S("h1_product"), S.at("h1_product", k + 1))
                            relu(t1[u][:, 0:C], pB[u][:, 0:C], cb[:, c_b0:c_b0 + 1]).then_inc(S("h1_cols"), 1)
                        elif s == 2:
                            act.wait_ge(S("h2_product"), S.at("h2_product", k + 1))
                            relu(t2[u][:, 0:C], pA[u][:, 0:C], cb[:, c_b1:c_b1 + 1]).then_inc(S("h2_cols"), 1)
                        elif s == 5:
                            act.wait_ge(S("x1_transposed"), S.at("x1_transposed", k + 1))
                            nc.scalar.copy(t0[u][:, 0:C], pA[u][:, 0:C]).then_inc(S("x1_cols"), 1)
                        elif s == 6:
                            act.wait_ge(S("head_product0"), S.at("head_product0", k + 1))
                            relu(t1[u][:, 0:C], pB[u][:, 0:C], cb[:, c_gat:c_gat + 1]).then_inc(S("head_relu0"), 1)
                        elif s == 7:
                            act.wait_ge(S("head_product1"), S.at("head_product1", k + 1))
                            relu(t2[u][:, 0:C], pA[u][:, 0:C], cb[:, c_gat + 1:c_gat + 2]).then_inc(S("head_relu1"), 1)
                        elif s == 10:
                            act.wait_ge(S("x2_transposed"), S.at("x2_transposed", k + 1))
                            nc.scalar.copy(t0[u][:, 0:C], pA[u][:, 0:C]).then_inc(S("x2_cols"), 1)
                        elif s == 11 and not dense:
                            act.wait_ge(S("state_product"), S.at("state_product", k + 1))
                            if not fresh(k):
                                act.wait_ge(S(f"stored{u}"), S.at(f"stored{u}", r * per_store))
                            relu(Dn[u][:, :, :], nm(pB[u])).then_inc(S("state_rows"), 1)

                    steps(act, n_steps, groups, stage)

                @block.vector
                def _(dve):
                    def stage(step, u, k, r):
                        s = walk[step]
                        P, J = shape(k, dense)
                        if s == "rows of h1":
                            dve.wait_ge(S("h1_back"), S.at("h1_back", k + 1))
                            if not fresh(k):
                                dve.wait_ge(S(f"stored{u}"), S.at(f"stored{u}", r * per_store))
                            nc.vector.tensor_copy(O[u][:, :, :], nm(pB[u])).then_inc(S("h1_rows"), 1)
                        elif s == "rows of h2":
                            dve.wait_ge(S("h2_back"), S.at("h2_back", k + 1))
                            nc.vector.tensor_copy(G2[u][:, :, :], nm(pA[u])).then_inc(S("h2_rows"), 1)
                        elif s == 3:
                            dve.wait_ge(S("h3_product"), S.at("h3_product", k + 1))
                            arrived(dve, u, r)
                            nc.vector.scalar_tensor_tensor(nm(t3[u])[0:P, 0:J, :], G[u][0:P, 0:J, :], 2.0,
                                                           nm(pB[u])[0:P, 0:J, :], ALU.mult,
                                                           ALU.add).then_inc(S("residual1"), 1)
                            stats(dve, u, k, P, J, nm(t3[u]), 1)
                        elif s == 4:
                            normalise(dve, u, k, P, J, nm(t3[u]), nm(t4[u]), 1)
                        elif s == 8:
                            dve.wait_ge(S("gat_product"), S.at("gat_product", k + 1))
                            dve.wait_ge(S("normed1"), S.at("normed1", k + 1))
                            nc.vector.tensor_tensor(nm(t3[u])[0:P, 0:J, :], nm(t4[u])[0:P, 0:J, :],
                                                    nm(pB[u])[0:P, 0:J, :], ALU.add).then_inc(S("residual2"), 1)
                            stats(dve, u, k, P, J, nm(t3[u]), 2)
                        elif s == 9:
                            normalise(dve, u, k, P, J, nm(t3[u]), nm(t5[u]), 2)
                        elif s == (11 if dense else "residual"):
                            if dense:
                                dve.wait_ge(S("state_product"), S.at("state_product", k + 1))
                            else:
                                dve.wait_ge(S("state_rows"), S.at("state_rows", k + 1))
                            dve.wait_ge(S("x2_with_gains"), S.at("x2_with_gains", k + 1))
                            nc.vector.scalar_tensor_tensor(nm(t3[u])[0:P, 0:J, :],
                                                           nm(pB[u])[0:P, 0:J, :] if dense else Dn[u][:, :, :], 0.0,
                                                           nm(t2[u])[0:P, 0:J, :], ALU.max,
                                                           ALU.add).then_inc(S("residual3"), 1)
                            stats(dve, u, k, P, J, nm(t3[u]), 3)
                        elif s == 12:
                            if not fresh(k) and dense:
                                dve.wait_ge(S(f"stored{u}"), S.at(f"stored{u}", r * per_store))
                            normalise(dve, u, k, P, J, nm(t3[u]), O[u] if dense else nm(t5[u]), 3)

                    steps(dve, n_steps, groups, stage)

            names = ["x_transposed", "x_cols", "h1_product", "h1_cols", "h2_product", "h2_cols", "h3_product", "x1_transposed", "x1_cols", "head_product0", "head_product1", "head_relu0", "head_relu1", "gat_product",
                     "x2_transposed", "x2_cols", "state_product"] + ln_signals(1, 2, 3) + ["x2_with_gains"]
            if dense:
                finish(groups, names + ["z_masked", "indices0"], loaded=16, stored=16, gathered=16, kept=16)
            else:
                finish(groups, names + ["h1_back", "h2_back", "h1_rows", "h2_rows", "state_rows", "indices0", "slots_in"], gathered=64,
                       scattered=64, kept=16, stored=per_store)

        sp_ = pool_ = None
        in_flight(6, 1, "G G2 Dn O t0 t1 t2 t3 t4 t5")
        chain(EG, False)

        with nc.Block() as block:
            @block.sync
            def _(sp):
                with nc.allow_non_contiguous_dma(reason="a node's slot for each row of a group"):
                    sp.dma_start(posN[:, 0:4 * NF].rearrange("p (g j) -> p g j", j=4),
                                 node_slot[0:NF * GC].rearrange("(g p j) -> p g j", p=128, j=4)).then_inc(S("pos_n"), 16)
                    if R:
                        sp.dma_start(posN[0:TP, 4 * NF:4 * NF + TJ],
                                     node_slot[NF * GC:N].rearrange("(p j) -> p j", j=TJ)).then_inc(S("pos_n"), 16)

            @block.gpsimd
            def _(pool):
                def gather_group(k, u, r):
                    if r is not None:
                        pool.wait_ge(S("pg_kept"), k - LOOKUPS + 1)
                    nc.gpsimd.tensor_copy(sti[u][:, 0:4], src_i[:, bass.ds(4 * k, 4)]).then_inc(S("pg_in"), 1)
                    pool.wait_ge(S("pg_in"), k + 1)
                    tick(pool)
                    for j in range(4):
                        nc.gpsimd.indirect_dma_start(
                            out=stv[u][:, j:j + 1], out_offset=None, in_=node_slot.rearrange("(n o) -> n o", o=1),
                            in_offset=bass.IndirectOffsetOnAxis(ap=sti[u][:, j:j + 1], axis=0)).then_inc(S(f"pg_out{u}"), 16)

                def keep_group(k, u, n):
                    pool.wait_ge(S(f"pg_out{u}"), n)
                    nc.gpsimd.tensor_copy(pos[:, bass.ds(4 * k, 4)], stv[u][:, 0:4]).then_inc(S("pg_kept"), 1)

                for k in range(min(LOOKUPS, EG)):
                    gather_group(k, k, None)
                if EG // LOOKUPS > 1:
                    with pool.Fori(1, EG // LOOKUPS) as b:
                        for u in range(LOOKUPS):
                            keep_group(b * LOOKUPS + u - LOOKUPS, u, b * 64)
                            gather_group(b * LOOKUPS + u, u, b)
                for k in range(max(LOOKUPS, EG // LOOKUPS * LOOKUPS), EG):
                    keep_group(k - LOOKUPS, k % LOOKUPS, k // LOOKUPS * 64)
                    gather_group(k, k % LOOKUPS, k // LOOKUPS)
                for k in range(max(0, EG - LOOKUPS), EG):
                    keep_group(k, k % LOOKUPS, (k // LOOKUPS + 1) * 64)
        with nc.Block() as block:
            @block.vector
            def _(dve):
                ch = Chain(dve, "dve_setup")
                nc.vector.tensor_scalar(w0[:, :], row_f[:, :], float(EP), None, ALU.add)
                ch.after(nc.vector.tensor_scalar(w1[:, :], pos[:, :], 0.0, None, ALU.is_ge))
                ch.after(nc.vector.tensor_tensor(pos[:, :], pos[:, :], w0[:, :], ALU.subtract))
                ch.after(nc.vector.tensor_tensor(pos[:, :], pos[:, :], w1[:, :], ALU.mult))
                ch.after(nc.vector.tensor_tensor(idx[:, :], pos[:, :], w0[:, :], ALU.add))
                dve.wait_ge(S("pos_n"), 16 + 16 * (R > 0))
                nc.vector.tensor_scalar(nmask[:, 0:4 * NF], posN[:, 0:4 * NF], 0.0, eps1[:, 0:1], ALU.is_lt, ALU.mult)
                if R:
                    nc.vector.tensor_scalar(nmask[0:TP, 4 * NF:4 * NF + TJ], posN[0:TP, 4 * NF:4 * NF + TJ], 0.0,
                                            eps1[0:TP, 0:1], ALU.is_lt, ALU.mult)
                nc.vector.memset(ystat[:, 0, :], 0.0)
                ch.close()

        with nc.Block() as block:
            @block.sync
            def _(sp):
                def stage(s, u, k, r):
                    sp.wait_ge(S("scaled_rows"), S.at("scaled_rows", k + 1))
                    sp.dma_start(slot_rows(x0_slots, k), G[u][:, :, :]).then_inc(S(f"stored{u}"), 16)
                    sp.dma_start(slot_rows(gcn_table[0], k), O[u][:, :, :]).then_inc(S(f"stored{u}"), 16)

                steps(sp, 1, EG, stage)
                for u in range(min(U, EG)):
                    sp.wait_ge(S(f"stored{u}"), S.at(f"stored{u}", 32 * len(range(u, EG, U))))

            @block.gpsimd
            def _(pool):
                def load(u, k, r):
                    if not fresh(k):
                        if not fresh(k):
                            pool.wait_ge(S(f"stored{u}"), S.at(f"stored{u}", r * 32))
                    gather(pool, u, k, dst_g, a["x"], G, 0)

                steps(pool, 1, EG, None, (0, load))

            @block.scalar
            def _(act):
                def stage(s, u, k, r):
                    act.wait_ge(S(f"gathered{u}"), S.at(f"gathered{u}", (r + 1) * 64))
                    if not fresh(k):
                        act.wait_ge(S(f"stored{u}"), S.at(f"stored{u}", r * 32))
                    for j in range(4):
                        ins = nc.scalar.activation(O[u][:, j, :], G[u][:, j, :], ACTF.Copy,
                                                   scale=dinv[:, bass.ds(4 * k + j, 1)])
                    ins.then_inc(S("scaled_rows"), 1)

                steps(act, 1, EG, stage)
        finish(EG, ["scaled_rows", "indices0"], gathered=64, stored=32)

        def gcn_layer(i):
            final = i == 2
            W = (W0, W1, W2)[i]
            row_b = (rowb0[:, :], rowb1[:, :], rows[:, row_b2, :])[i]
            per_load = 48 if final else 32
            n_steps = 3 if final else 2

            with nc.Block() as block:
                @block.sync
                def _(sp):
                    def load(u, k, r):
                        if not fresh(k) and final:
                            sp.wait_ge(S("residual1"), S.at("residual1", k + 1 - U))
                        if not fresh(k) and not final:
                            sp.wait_ge(S("loop_added"), S.at("loop_added", k + 1 - U))
                        sp.dma_start(Dn[u][:, :, :], slot_rows(gcn_table[i], k)).then_inc(S(f"loaded{u}"), 16)
                        sp.dma_start(keep[u][:, :], keep_cols(k)).then_inc(S(f"loaded{u}"), 16)
                        if final:
                            sp.dma_start(G2[u][:, :, :], slot_rows(x0_slots, k)).then_inc(S(f"loaded{u}"), 16)

                    def stage(s, u, k, r):
                        if s == n_steps - 1:
                            sp.wait_ge(S("normed1" if final else "scaled_rows"), S.at("normed1" if final else "scaled_rows", k + 1))
                            sp.dma_start(slot_rows(gat_table if final else gcn_table[i + 1], k),
                                         O[u][:, :, :]).then_inc(S(f"stored{u}"), 16)

                    steps(sp, n_steps, EG, stage, (1 if final else 0, load))
                    for u in range(min(U, EG)):
                        sp.wait_ge(S(f"stored{u}"), S.at(f"stored{u}", 16 * len(range(u, EG, U))))

                @block.gpsimd
                def _(pool):
                    def load(u, k, r):
                        if not fresh(k):
                            pool.wait_ge(S("columns_ready"), S.at("columns_ready", k + 1 - U))
                        gather(pool, u, k, idx, gcn_table[i], G, 0)

                    def stage(s, u, k, r):
                        if final and s == 1:
                            inv_std(pool, u, k, 128, 4, 1, with_shift=True)

                    steps(pool, n_steps, EG, stage, (0, load))

                @block.tensor
                def _(pe):
                    def stage(s, u, k, r):
                        if s == 0:
                            pe.wait_ge(S(f"gathered{u}"), S.at(f"gathered{u}", (r + 1) * 64))
                            pe.wait_ge(S(f"loaded{u}"), S.at(f"loaded{u}", (r + 1) * per_load))
                            if not fresh(k):
                                pe.wait_ge(S("biased_rows"), S.at("biased_rows", k + 1 - U))
                            transposes(G[u], pA[u])
                            transposes(Dn[u], pB[u]).then_inc(S("columns_ready"), 1)
                        elif s == 1:
                            pe.wait_ge(S("loop_added"), S.at("loop_added", k + 1))
                            to_node_major(pA[u], [(t0[u], W[:, :])]).then_inc(S("message_product"), 1)

                    steps(pe, n_steps, EG, stage)

                @block.vector
                def _(dve):
                    def stage(s, u, k, r):
                        if s == 0:
                            dve.wait_ge(S("columns_ready"), S.at("columns_ready", k + 1))
                            dve.wait_ge(S(f"loaded{u}"), S.at(f"loaded{u}", (r + 1) * per_load))
                            dve.wait_ge(S("segments_summed"), S.at("segments_summed", k))
                            scan(A[u], keep[u][:, :], pA[u][:, :], A[u - 1], ALU.mult, ALU.add).then_inc(S("segments_summed"), 1)
                            dve.wait_ge(S("segments_summed"), S.at("segments_summed", k + 1))
                            nc.vector.tensor_tensor(t0[u][:, :], A[u][:, 1:GC + 1], pB[u][:, :],
                                                    ALU.add).then_inc(S("loop_added"), 1)
                        elif s == 1:
                            dve.wait_ge(S("message_product"), S.at("message_product", k + 1))
                            if not final and not fresh(k):
                                dve.wait_ge(S("scaled_rows"), S.at("scaled_rows", k + 1 - U))
                            for j in range(4):
                                ins = nc.vector.scalar_tensor_tensor(
                                    nm(t1[u])[:, j, :], pA[u][:, j * D:(j + 1) * D], dinv[:, bass.ds(4 * k + j, 1)],
                                    row_b, ALU.mult, ALU.add)
                            ins.then_inc(S("biased_rows"), 1)
                            if final:
                                dve.wait_ge(S("biased_rows"), S.at("biased_rows", k + 1))
                                if not fresh(k):
                                    dve.wait_ge(S("normed1"), S.at("normed1", k + 1 - U))
                                nc.vector.scalar_tensor_tensor(nm(t2[u]), G2[u][:, :, :], 2.0, nm(t1[u]), ALU.mult,
                                                               ALU.add).then_inc(S("residual1"), 1)
                                stats(dve, u, k, 128, 4, nm(t2[u]), 1, negated=True)

                    steps(dve, n_steps, EG, stage)

                @block.scalar
                def _(act):
                    def stage(s, u, k, r):
                        if s == 2:
                            if not fresh(k):
                                act.wait_ge(S(f"stored{u}"), S.at(f"stored{u}", r * 16))
                            normalise_on_act(act, u, k, 128, 4, nm(t2[u]), O[u], 1)
                        elif s == 1 and not final:
                            act.wait_ge(S("biased_rows"), S.at("biased_rows", k + 1))
                            if not fresh(k):
                                act.wait_ge(S(f"stored{u}"), S.at(f"stored{u}", r * 16))
                            for j in range(4):
                                ins = nc.scalar.activation(O[u][:, j, :], nm(t1[u])[:, j, :], ACTF.Relu,
                                                           scale=dinv[:, bass.ds(4 * k + j, 1)])
                            ins.then_inc(S("scaled_rows"), 1)

                    steps(act, n_steps, EG, stage)

            finish(EG, ["columns_ready", "segments_summed", "loop_added", "message_product", "biased_rows", "indices0"] + (ln_signals(1) + ["inv_std_alone"] if final else ["scaled_rows"]),
                   gathered=64, loaded=per_load, stored=16)

        in_flight(4, 2, "G G2 Dn O keep A t0 t1 t2")
        for i in range(3):
            gcn_layer(i)

        in_flight(4, 2, "G G2 Dn O keep soft A Mx Sc0 Sc1 t0 t1 t2 t3 t4 t5 t6 t7")

        with nc.Block() as block:
            @block.sync
            def _(sp):
                def load(u, k, r):
                    if not fresh(k):
                        sp.wait_ge(S("residual2"), S.at("residual2", k + 1 - U))
                    sp.dma_start(keep[u][:, :], keep_cols(k)).then_inc(S(f"loaded{u}"), 16)

                def stage(s, u, k, r):
                    if s == 7:
                        sp.wait_ge(S("normed2"), S.at("normed2", k + 1))
                        sp.dma_start(slot_rows(x2_slots, k), O[u][:, :, :]).then_inc(S(f"stored{u}"), 16)
                    elif s == 9:
                        sp.wait_ge(S("state_rows"), S.at("state_rows", k + 1))
                        sp.dma_start(slot_rows(mpn_table[0], k), nm(t7[u])).then_inc(S(f"stored{u}"), 16)

                steps(sp, 10, EG, stage, (6, load))
                for u in range(min(U, EG)):
                    sp.wait_ge(S(f"stored{u}"), S.at(f"stored{u}", 32 * len(range(u, EG, U))))

            @block.gpsimd
            def _(pool):
                def load_source(u, k, r):
                    if not fresh(k):
                        pool.wait_ge(S("x1_transposed"), S.at("x1_transposed", k + 1 - U))
                    gather(pool, u, k, idx, gat_table, G, 0)

                def load_own(u, k, r):
                    if not fresh(k):
                        pool.wait_ge(S("residual2"), S.at("residual2", k + 1 - U))
                    gather(pool, u, k, idx_own, gat_table, Dn, 4)

                def stage(s, u, k, r):
                    if s == 2:
                        pool.wait_ge(S("maxima"), S.at("maxima", k + 1))
                        nc.gpsimd.tensor_tensor(soft[u][:, 2, :], t3[u][:, :], Mx[u][:, 1:GC + 1],
                                                ALU.subtract).then_inc(S("loop_exponents"), 1)
                    elif s == 4 or s == 5:
                        c = s - 4
                        pool.wait_ge(S(f"numerator{c}"), S.at(f"numerator{c}", k + 1))
                        nc.gpsimd.tensor_tensor((t4, t3)[c][u][:, :], t2[u][:, :], t5[u][:, :],
                                                ALU.mult).then_inc(S(f"head_mean{c}"), 1)
                    elif s == 6:
                        inv_std(pool, u, k, 128, 4, 2, with_shift=True)

                steps(pool, 10, EG, stage, (0, load_source), (6, load_own))

            @block.tensor
            def _(pe):
                def stage(s, u, k, r):
                    if s == 0:
                        pe.wait_ge(S(f"gathered{u}"), S.at(f"gathered{u}", (r + 1) * 128))
                        if not fresh(k):
                            pe.wait_ge(S("state_rows"), S.at("state_rows", k + 1 - U))
                        transposes(G[u], pA[u])
                        transposes(Dn[u], pB[u]).then_inc(S("x1_transposed"), 1)
                    elif s == 1:
                        pe.wait_ge(S("x1_cols"), S.at("x1_cols", k + 1))
                        feature_major(pA[u], [(t0[u], attS[:, :]), (t1[u], attD[:, :])])
                        feature_major(pB[u], [(t1[u], attSD[:, :])]).then_inc(S("scores_product"), 1)
                    elif s == 3 or s == 5:
                        c = s // 2 - 1
                        pe.wait_ge(S("weighted0" if c else "scores"), S.at("weighted0" if c else "scores", k + 1))
                        feature_major(pA[u], [(t0[u], Wg[:, c, :])])
                        feature_major(pB[u], [(t1[u], Wg[:, c, :])]).then_inc(S(f"weighted_product{c}"), 1)
                    elif s == 6:
                        pe.wait_ge(S("head_relu1"), S.at("head_relu1", k + 1))
                        to_node_major(pA[u], [(G2[u][:, :, :].rearrange("p j d -> p (j d)"), fcw[:, 0, :]),
                                              (t6[u], fcw[:, 1, :])], row=row_fc).then_inc(S("gat_product"), 1)
                    elif s == 8:
                        pe.wait_ge(S("normed2"), S.at("normed2", k + 1))
                        transposes(O[u], pB[u]).then_inc(S("x2_transposed"), 1)
                    elif s == 9:
                        pe.wait_ge(S("x2_cols"), S.at("x2_cols", k + 1))
                        to_node_major(pA[u], [(t0[u], Wi[:, :])], row=row_bi).then_inc(S("state_product"), 1)

                steps(pe, 10, EG, stage)

            @block.scalar
            def _(act):
                def stage(s, u, k, r):
                    if s == 0:
                        act.wait_ge(S("x1_transposed"), S.at("x1_transposed", k + 1))
                        nc.scalar.copy(t0[u][:, :], pA[u][:, :])
                        nc.scalar.copy(t1[u][:, :], pB[u][:, :]).then_inc(S("x1_cols"), 1)
                    elif s == 1:
                        act.wait_ge(S("scores_product"), S.at("scores_product", k + 1))
                        nc.scalar.copy(soft[u][:, 0, :], pA[u][:, :])
                        nc.scalar.copy(soft[u][:, 1, :], pB[u][:, :])
                        act.wait_ge(S(f"loaded{u}"), S.at(f"loaded{u}", (r + 1) * 16))
                        nc.scalar.activation(t5[u][:, :], keep[u][:, :], ACTF.Identity, bias=neg_far[:, 0:1],
                                             scale=FAR).then_inc(S("scores"), 1)
                    elif s == 2:
                        act.wait_ge(S("exponents"), S.at("exponents", k + 1))
                        act.wait_ge(S("loop_exponents"), S.at("loop_exponents", k + 1))
                        nc.scalar.activation(soft[u][:, :, :], soft[u][:, :, :], ACTF.Exp).then_inc(S("exponentials"), 1)
                    elif s == 4:
                        act.wait_ge(S("head_mean0"), S.at("head_mean0", k + 1))
                        nc.scalar.activation(G2[u][:, :, :].rearrange("p j d -> p (j d)"), t4[u][:, :], ACTF.Relu,
                                             bias=cb[:, c_gat:c_gat + 1]).then_inc(S("head_relu0"), 1)
                    elif s == 5:
                        act.wait_ge(S("head_mean1"), S.at("head_mean1", k + 1))
                        nc.scalar.activation(t6[u][:, :], t3[u][:, :], ACTF.Relu,
                                             bias=cb[:, c_gat + 1:c_gat + 2]).then_inc(S("head_relu1"), 1)
                    elif s == 7:
                        if not fresh(k):
                            act.wait_ge(S(f"stored{u}"), S.at(f"stored{u}", r * 32))
                        normalise_on_act(act, u, k, 128, 4, nm(t2[u]), O[u], 2)
                    elif s == 8:
                        act.wait_ge(S("x2_transposed"), S.at("x2_transposed", k + 1))
                        nc.scalar.copy(t0[u][:, :], pB[u][:, :]).then_inc(S("x2_cols"), 1)
                    elif s == 9:
                        act.wait_ge(S("state_product"), S.at("state_product", k + 1))
                        if not fresh(k):
                            act.wait_ge(S(f"stored{u}"), S.at(f"stored{u}", r * 32))
                        nc.scalar.activation(t7[u][:, :], pA[u][:, :], ACTF.Relu).then_inc(S("state_rows"), 1)

                steps(act, 10, EG, stage)

            @block.vector
            def _(dve):
                def stt(out_, in0, scalar, in1, op0, op1):
                    return nc.vector.scalar_tensor_tensor(out_, in0, scalar, in1, op0, op1)

                def tt(out_, in0, in1, op):
                    return nc.vector.tensor_tensor(out_, in0, in1, op)

                def stage(s, u, k, r):
                    decay, p_edge, p_loop = soft[u][:, 0, :], soft[u][:, 1, :], soft[u][:, 2, :]
                    m_now, m_before = Mx[u][:, 1:GC + 1], Mx[u][:, 0:GC]
                    if s == 2:
                        dve.wait_ge(S("scores"), S.at("scores", k + 1))
                        stt(t2[u][:, :], soft[u][:, 0, :], SLOPE, soft[u][:, 0, :], ALU.mult, ALU.max)
                        stt(t3[u][:, :], soft[u][:, 1, :], SLOPE, soft[u][:, 1, :], ALU.mult,
                            ALU.max).then_inc(S("leaky_scores"), 1)
                        dve.wait_ge(S("leaky_scores"), S.at("leaky_scores", k + 1))
                        tt(t4[u][:, :], t2[u][:, :], t3[u][:, :], ALU.max).then_inc(S("scores_with_loop"), 1)
                        dve.wait_ge(S("scores_with_loop"), S.at("scores_with_loop", k + 1))
                        dve.wait_ge(S("maxima"), S.at("maxima", k))
                        nc.vector.tensor_copy(Mx[u][:, 0:1], Mx[u - 1][:, GC:GC + 1])
                        scan(Mx[u], t5[u][:, :], t4[u][:, :], Mx[u - 1], ALU.add, ALU.max).then_inc(S("maxima"), 1)
                        dve.wait_ge(S("maxima"), S.at("maxima", k + 1))
                        tt(soft[u][:, 1, :], t2[u][:, :], m_now, ALU.subtract)
                        tt(soft[u][:, 0, :], m_before, t5[u][:, :], ALU.add).then_inc(S("exponents_part"), 1)
                        dve.wait_ge(S("exponents_part"), S.at("exponents_part", k + 1))
                        tt(soft[u][:, 0, :], soft[u][:, 0, :], m_now, ALU.subtract).then_inc(S("exponents"), 1)
                    elif s == 3:
                        dve.wait_ge(S("exponentials"), S.at("exponentials", k + 1))
                        dve.wait_ge(S("segments_summed"), S.at("segments_summed", k))
                        scan(A[u], decay, p_edge, A[u - 1], ALU.mult, ALU.add).then_inc(S("segments_summed"), 1)
                        dve.wait_ge(S("segments_summed"), S.at("segments_summed", k + 1))
                        tt(t5[u][:, :], A[u][:, 1:GC + 1], p_loop, ALU.add).then_inc(S("denominator"), 1)
                        dve.wait_ge(S("denominator"), S.at("denominator", k + 1))
                        nc.vector.reciprocal(t5[u][:, :], t5[u][:, :]).then_inc(S("inv_denominator"), 1)
                    elif s == 4 or s == 5:
                        c = s - 4
                        Sc = (Sc0, Sc1)[c]
                        dve.wait_ge(S(f"weighted_product{c}"), S.at(f"weighted_product{c}", k + 1))
                        dve.wait_ge(S(f"head_mean0" if c else "inv_denominator"), S.at(f"head_mean0" if c else "inv_denominator", k + 1))
                        tt(t2[u][:, :], p_edge, pA[u][:, :], ALU.mult)
                        tt(t3[u][:, :], p_loop, pB[u][:, :], ALU.mult).then_inc(S(f"weighted{c}"), 1)
                        dve.wait_ge(S(f"weighted{c}"), S.at(f"weighted{c}", k + 1))
                        dve.wait_ge(S(f"weighted_sums{c}"), S.at(f"weighted_sums{c}", k))
                        scan(Sc[u], decay, t2[u][:, :], Sc[u - 1], ALU.mult, ALU.add).then_inc(S(f"weighted_sums{c}"), 1)
                        dve.wait_ge(S(f"weighted_sums{c}"), S.at(f"weighted_sums{c}", k + 1))
                        tt(t2[u][:, :], Sc[u][:, 1:GC + 1], t3[u][:, :], ALU.add).then_inc(S(f"numerator{c}"), 1)
                    elif s == 6:
                        dve.wait_ge(S("gat_product"), S.at("gat_product", k + 1))
                        tt(nm(t2[u]), Dn[u][:, :, :], nm(pA[u]), ALU.add).then_inc(S("residual2"), 1)
                        stats(dve, u, k, 128, 4, nm(t2[u]), 2, negated=True)

                steps(dve, 10, EG, stage)
        finish(EG, ["x1_transposed", "x1_cols", "scores_product", "scores", "leaky_scores", "scores_with_loop", "maxima", "exponents_part", "exponents", "exponentials", "segments_summed",
                    "denominator", "inv_denominator", "weighted_product0", "weighted_product1", "weighted0", "weighted1", "weighted_sums0", "weighted_sums1", "numerator0", "numerator1",
                    "head_mean0", "head_mean1", "head_relu0", "head_relu1", "gat_product", "x2_transposed", "x2_cols", "state_product", "state_rows", "indices0", "indices4"]
               + ln_signals(2) + ["inv_std_alone", "loop_exponents"], gathered=128, loaded=16, stored=32)
        S.retire(["scores_product", "scores", "leaky_scores", "scores_with_loop", "maxima", "exponents_part", "exponents",
                  "exponentials", "denominator", "inv_denominator", "weighted_product0", "weighted_product1", "weighted0", "weighted1",
                  "weighted_sums0", "weighted_sums1", "numerator0", "numerator1", "head_mean0", "head_mean1"])

        def mpn_round(i):
            final = i == ROUNDS - 1
            per_load = 48 if final else 32
            n_steps = 4 if final else 3

            with nc.Block() as block:
                @block.sync
                def _(sp):
                    def load(u, k, r):
                        if not fresh(k):
                            sp.wait_ge(S("state_shifted"), S.at("state_shifted", k + 1 - U))
                        sp.dma_start(Dn[u][:, :, :], slot_rows(mpn_table[i % 2], k)).then_inc(S(f"loaded{u}"), 16)
                        sp.dma_start(keep[u][:, :], keep_cols(k)).then_inc(S(f"loaded{u}"), 16)
                        if final:
                            sp.dma_start(G2[u][:, :, :], slot_rows(x2_slots, k)).then_inc(S(f"loaded{u}"), 16)

                    def stage(s, u, k, r):
                        if s == n_steps - 1:
                            sp.wait_ge(S("normed3" if final else "state_updated"), S.at("normed3" if final else "state_updated", k + 1))
                            sp.dma_start(slot_rows(x3_table if final else mpn_table[(i + 1) % 2], k),
                                         O[u][:, :, :]).then_inc(S(f"stored{u}"), 16)

                    steps(sp, n_steps, EG, stage, (1, load))
                    for u in range(min(U, EG)):
                        sp.wait_ge(S(f"stored{u}"), S.at(f"stored{u}", 16 * len(range(u, EG, U))))

                @block.gpsimd
                def _(pool):
                    def load(u, k, r):
                        if not fresh(k):
                            pool.wait_ge(S("cols_psum"), S.at("cols_psum", k + 1 - U))
                        gather(pool, u, k, idx, mpn_table[i % 2], G, 0)

                    def stage(s, u, k, r):
                        if s == 2 and final:
                            inv_std(pool, u, k, 128, 4, 3, with_shift=True)

                    steps(pool, n_steps, EG, stage, (0, load))

                @block.tensor
                def _(pe):
                    def stage(s, u, k, r):
                        if s == 0:
                            pe.wait_ge(S(f"gathered{u}"), S.at(f"gathered{u}", (r + 1) * 64))
                            if not fresh(k):
                                pe.wait_ge(S("update_rows"), S.at("update_rows", k + 1 - U))
                            transposes(G[u], pA[u]).then_inc(S("cols_psum"), 1)
                        elif s == 1:
                            pe.wait_ge(S("cols_copied"), S.at("cols_copied", k + 1))
                            feature_major(pB[u], [(t0[u], Wm[:, i, :])]).then_inc(S("message_product"), 1)
                        elif s == 2:
                            pe.wait_ge(S("segments_summed"), S.at("segments_summed", k + 1))
                            to_node_major(pA[u], [(A[u][:, 1:GC + 1], Wu[:, i, :])], row=row_bu + i).then_inc(S("update_product"), 1)

                    steps(pe, n_steps, EG, stage)

                @block.scalar
                def _(act):
                    def stage(s, u, k, r):
                        if s == 0:
                            act.wait_ge(S("cols_psum"), S.at("cols_psum", k + 1))
                            nc.scalar.copy(t0[u][:, :], pA[u][:, :]).then_inc(S("cols_copied"), 1)
                        elif s == 1:
                            act.wait_ge(S("message_product"), S.at("message_product", k + 1))
                            if not fresh(k):
                                act.wait_ge(S("segments_summed"), S.at("segments_summed", k + 1 - U))
                            nc.scalar.activation(t1[u][:, :], pB[u][:, :], ACTF.Relu,
                                                 bias=cb[:, c_bm + i:c_bm + i + 1]).then_inc(S("messages"), 1)
                        elif s == 2:
                            act.wait_ge(S("update_product"), S.at("update_product", k + 1))
                            if not fresh(k):
                                act.wait_ge(S("state_updated"), S.at("state_updated", k + 1 - U))
                            nc.scalar.activation(t2[u][:, :], pA[u][:, :], ACTF.Relu).then_inc(S("update_rows"), 1)
                        elif s == 3:
                            if not fresh(k):
                                act.wait_ge(S(f"stored{u}"), S.at(f"stored{u}", r * 16))
                            normalise_on_act(act, u, k, 128, 4, nm(t5[u]), O[u], 3)

                    steps(act, n_steps, EG, stage)

                @block.vector
                def _(dve):
                    def stage(s, u, k, r):
                        if s == 1:
                            dve.wait_ge(S("messages"), S.at("messages", k + 1))
                            dve.wait_ge(S(f"loaded{u}"), S.at(f"loaded{u}", (r + 1) * per_load))
                            dve.wait_ge(S("segments_summed"), S.at("segments_summed", k))
                            scan(A[u], keep[u][:, :], t1[u][:, :], A[u - 1], ALU.mult, ALU.add).then_inc(S("segments_summed"), 1)
                            ins = nc.vector.tensor_tensor(nm(t3[u]), Dn[u][:, :, :],
                                                          cu[:, i, :].unsqueeze(1).to_broadcast([128, 4, D]),
                                                          ALU.subtract)
                            if final:
                                ins = nc.vector.tensor_tensor(nm(t4[u]), G2[u][:, :, :],
                                                              c_all[:, :].unsqueeze(1).to_broadcast([128, 4, D]), ALU.add)
                            ins.then_inc(S("state_shifted"), 1)
                        elif s == 2:
                            dve.wait_ge(S("update_rows"), S.at("update_rows", k + 1))
                            dve.wait_ge(S("state_shifted"), S.at("state_shifted", k + 1))
                            if final:
                                nc.vector.tensor_tensor(t5[u][:, :], t2[u][:, :], t3[u][:, :], ALU.add).then_inc(S("state_updated"), 1)
                                dve.wait_ge(S("state_updated"), S.at("state_updated", k + 1))
                                nc.vector.tensor_tensor(t5[u][:, :], t5[u][:, :], t4[u][:, :], ALU.add).then_inc(S("residual3"), 1)
                                stats(dve, u, k, 128, 4, nm(t5[u]), 3, negated=True)
                            else:
                                if not fresh(k):
                                    dve.wait_ge(S(f"stored{u}"), S.at(f"stored{u}", r * 16))
                                nc.vector.tensor_tensor(O[u][:, :, :], nm(t2[u]), nm(t3[u]), ALU.add).then_inc(S("state_updated"), 1)

                    steps(dve, n_steps, EG, stage)
            finish(EG, ["cols_psum", "cols_copied", "message_product", "messages", "segments_summed", "update_product", "update_rows", "state_updated", "state_shifted", "indices0"]
                   + (ln_signals(3) + ["inv_std_alone"] if final else []), gathered=64, loaded=per_load, stored=16)

        in_flight(6, 1, "G G2 Dn O keep A t0 t1 t2 t3 t4 t5")
        for i in range(ROUNDS):
            mpn_round(i)

        in_flight(7, 1, "G O zm attr t0 t1 t2 t3 t4 t5")
        with nc.Block() as block:
            @block.tensor
            def _(pe):
                nc.tensor.matmul(pGram[:, 0:D + 1], ident[:, :], zeros[:, :], start=True, stop=False,
                                 skip_group_check=True)
        chain(NG, True)

        REST = ET - NG
        assert REST >= 0
        if REST:
            with nc.Block() as block:
                @block.gpsimd
                def _(pool):
                    for i in range(REST):
                        u, r = i % U, i // U
                        if r:
                            pool.wait_ge(S(f"kept{u}"), S.at(f"kept{u}", r * 16))
                        nc.gpsimd.tensor_copy(idxs[u][:, 0:1], edge_i[:, NG + i:NG + i + 1]).then_inc(S("indices0"), 1)
                        pool.wait_ge(S("indices0"), S.at("indices0", i + 1))
                        tick(pool)
                        nc.gpsimd.indirect_dma_start(
                            out=attr[u][:, :], out_offset=None, in_=a["edge_attr_128"],
                            in_offset=bass.IndirectOffsetOnAxis(ap=idxs[u][:, 0:1], axis=0),
                        ).then_inc(S(f"gathered{u}"), 16)

                @block.sync
                def _(sp):
                    for i in range(REST):
                        u, r = i % U, i // U
                        sp.wait_ge(S(f"gathered{u}"), S.at(f"gathered{u}", (r + 1) * 16))
                        sp.dma_start(attr_slots[(NG + i) * 128:(NG + i + 1) * 128, :],
                                     attr[u][:, :]).then_inc(S(f"kept{u}"), 16)
                    for u in range(min(U, REST)):
                        sp.wait_ge(S(f"kept{u}"), S.at(f"kept{u}", 16 * len(range(u, REST, U))))
            finish(REST, ["indices0"], gathered=16, kept=16)
        in_flight(6, 1, "G G2 Dn keep A zm t0 t1 t2")

        with nc.Block() as block:
            @block.sync
            def _(sp):
                def load(u, k, r):
                    if not fresh(k):
                        sp.wait_ge(S("z_rows"), S.at("z_rows", k + 1 - U))
                    sp.dma_start(Dn[u][:, :, :], slot_rows(x3_table, k)).then_inc(S(f"loaded{u}"), 16)
                    sp.dma_start(keep[u][:, :], keep_cols(k)).then_inc(S(f"loaded{u}"), 16)
                    sp.dma_start(G2[u][:, :, :], attr_slots[bass.ds(k * GC, GC), :].rearrange(
                        "(j p) d -> p j d", j=4)).then_inc(S(f"loaded{u}"), 16)

                def stage(s, u, k, r):
                    if s == 3:
                        sp.wait_ge(S("z_masked"), S.at("z_masked", k + 1))
                        sp.dma_start(slot_rows(z_slots, k), zm[u][:, :, 0:D]).then_inc(S(f"stored{u}"), 16)

                steps(sp, 5, EG, stage, (2, load))
                for u in range(min(U, EG)):
                    sp.wait_ge(S(f"stored{u}"), S.at(f"stored{u}", 16 * len(range(u, EG, U))))

            @block.gpsimd
            def _(pool):
                def load(u, k, r):
                    if not fresh(k):
                        pool.wait_ge(S("edge_sums"), S.at("edge_sums", k + 1 - U))
                    gather(pool, u, k, idx, x3_table, G, 0)

                steps(pool, 5, EG, None, (0, load))

            @block.tensor
            def _(pe):
                def stage(s, u, k, r):
                    if s == 1:
                        pe.wait_ge(S("messages"), S.at("messages", k + 1))
                        transposes(nm(t1[u]), pA[u]).then_inc(S("cols_psum"), 1)
                    elif s == 2:
                        pe.wait_ge(S("segments_summed"), S.at("segments_summed", k + 1))
                        back_transposes(A[u][:, 1:GC + 1], pB[u]).then_inc(S("message_product"), 1)
                    elif s == 4:
                        pe.wait_ge(S("z_masked"), S.at("z_masked", k + 1))
                        for j in range(4):
                            ins = nc.tensor.matmul(pGram[:, 0:D + 1], zm[u][:, j, 0:D], zm[u][:, j, :], start=False,
                                                   stop=False, skip_group_check=True)
                        ins.then_inc(S("gram_added"), 1)

                steps(pe, 5, EG, stage)
                nc.tensor.matmul(pGram[:, 0:D + 1], ident[:, :], zeros[:, :], start=False, stop=True, skip_group_check=True)

            @block.scalar
            def _(act):
                def stage(s, u, k, r):
                    if s == 0:
                        act.wait_ge(S("edge_sums"), S.at("edge_sums", k + 1))
                        if not fresh(k):
                            act.wait_ge(S("cols_psum"), S.at("cols_psum", k + 1 - U))
                        nc.scalar.activation(t1[u][:, :], t0[u][:, :], ACTF.Relu).then_inc(S("messages"), 1)
                    elif s == 2:
                        act.wait_ge(S("z_rows"), S.at("z_rows", k + 1))
                        if not fresh(k):
                            act.wait_ge(S(f"stored{u}"), S.at(f"stored{u}", r * 16))
                            act.wait_ge(S("gram_added"), S.at("gram_added", k + 1 - U))
                        for j in range(4):
                            ins = nc.scalar.activation(zm[u][:, j, 0:D], nm(t2[u])[:, j, :], ACTF.Copy,
                                                       scale=last[:, bass.ds(4 * k + j, 1)])
                        ins.then_inc(S("z_masked"), 1)

                steps(act, 5, EG, stage)

            @block.vector
            def _(dve):
                def stage(s, u, k, r):
                    if s == 0:
                        dve.wait_ge(S(f"loaded{u}"), S.at(f"loaded{u}", (r + 1) * 48))
                        dve.wait_ge(S(f"gathered{u}"), S.at(f"gathered{u}", (r + 1) * 64))
                        if not fresh(k):
                            dve.wait_ge(S("messages"), S.at("messages", k + 1 - U))
                        nc.vector.tensor_tensor(nm(t0[u]), G[u][:, :, :], G2[u][:, :, :], ALU.add).then_inc(S("edge_sums"), 1)
                    elif s == 1:
                        dve.wait_ge(S("cols_psum"), S.at("cols_psum", k + 1))
                        dve.wait_ge(S("segments_summed"), S.at("segments_summed", k))
                        scan(A[u], keep[u][:, :], pA[u][:, :], A[u - 1], ALU.mult, ALU.add).then_inc(S("segments_summed"), 1)
                    elif s == 2:
                        dve.wait_ge(S("message_product"), S.at("message_product", k + 1))
                        if not fresh(k):
                            dve.wait_ge(S("z_masked"), S.at("z_masked", k + 1 - U))
                        nc.vector.scalar_tensor_tensor(nm(t2[u]), Dn[u][:, :, :], eps1[:, 0:1], nm(pB[u]), ALU.mult,
                                                       ALU.add).then_inc(S("z_rows"), 1)

                steps(dve, 5, EG, stage)
        finish(EG, ["edge_sums", "messages", "cols_psum", "segments_summed", "message_product", "z_rows", "z_masked", "gram_added", "indices0"], gathered=64,
               loaded=48, stored=16)

        with nc.Block() as block:
            @block.gpsimd
            def _(pool):
                nc.gpsimd.memset(small[:, 14:16], -0.5).then_inc(S("bn1_half"), 1)
                pool.wait_ge(S("bn1_half"), S.at("bn1_half", 1))
                pool.wait_ge(S("bn1_var"), S.at("bn1_var", 1))
                nc.gpsimd.tensor_tensor(small[:, 12:14], small[:, 8:10], small[:, 14:16], ALU.pow).then_inc(S("bn1_rstd"), 1)

            @block.vector
            def _(dve):
                ch = Chain(dve, "dve_setup")
                nc.vector.tensor_scalar(gram[:, :], pGram[:, 0:D + 1], 1.0 / N, None, ALU.mult).then_inc(S("gram_in"), 1)
                dve.wait_ge(S("mrow_p"), S.at("mrow_p", 1))
                nc.vector.tensor_copy(mrow[:, :], pMisc[0:1, 0:D]).then_inc(S("mrow_in"), 1)
                dve.wait_ge(S("outer_p"), S.at("outer_p", 1))
                nc.vector.tensor_tensor(gram[:, 0:D], gram[:, 0:D], pMisc[:, 128:256], ALU.subtract).then_inc(S("cov"), 1)
                dve.wait_ge(S("cw_p"), S.at("cw_p", 1))
                nc.vector.tensor_tensor(prod[:, :, :], V1[:, :, :],
                                        pMisc[:, 256:512].rearrange("p (c o) -> p c o", c=2), ALU.mult).then_inc(S("cwp"), 1)
                dve.wait_ge(S("mv_p"), S.at("mv_p", 1))
                ch.after(nc.vector.tensor_copy(small[:, 0:4], pA[0][:, 0:4]))
                nc.vector.tensor_scalar(small[:, 8:10], small[:, 2:4], BN_EPS, None, ALU.add).then_inc(S("bn1_var"), 1)
                dve.wait_ge(S("bn1_rstd"), S.at("bn1_rstd", 1))
                ch.after(nc.vector.tensor_tensor(bn[:, b_s1:b_s1 + 2], bn[:, b_g1:b_g1 + 2], small[:, 12:14], ALU.mult))
                ch.after(nc.vector.tensor_tensor(small[:, 4:6], small[:, 0:2], bn[:, b_s1:b_s1 + 2], ALU.mult))
                ch.after(nc.vector.tensor_tensor(bn[:, b_t1:b_t1 + 2], bn[:, b_b1:b_b1 + 2], small[:, 4:6], ALU.subtract))
                nc.vector.tensor_scalar(small[:, 6:8], bn[:, b_t1:b_t1 + 2], 0.0, None, ALU.max).then_inc(S("r0"), 1)
                dve.wait_ge(S("y0_p"), S.at("y0_p", 1))
                ch.after(nc.vector.tensor_copy(small[:, 16:17], pMisc[:, 0:1]))
                ch.close()

            @block.tensor
            def _(pe):
                pe.wait_ge(S("gram_in"), S.at("gram_in", 1))
                nc.tensor.transpose(pMisc[0:1, 0:D], gram[:, D:D + 1], ident[:, :]).then_inc(S("mrow_p"), 1)
                pe.wait_ge(S("mrow_in"), S.at("mrow_in", 1))
                nc.tensor.matmul(pMisc[:, 128:256], mrow[:, :], mrow[:, :], start=True, stop=True).then_inc(S("outer_p"), 1)
                pe.wait_ge(S("cov"), S.at("cov", 1))
                nc.tensor.matmul(pMisc[:, 256:512], gram[:, 0:D], V1[:, :, :], start=True, stop=True).then_inc(S("cw_p"), 1)
                pe.wait_ge(S("cwp"), S.at("cwp", 1))
                for c in range(2):
                    nc.tensor.matmul(pA[0][:, c:c + 1], V1[:, c, :], gram[:, D:D + 1], start=True, stop=True)
                for c in range(2):
                    ins = nc.tensor.matmul(pA[0][:, 2 + c:3 + c], prod[:, c, :], onesc[:, :], start=True, stop=True)
                ins.then_inc(S("mv_p"), 1)
                pe.wait_ge(S("r0"), S.at("r0", 1))
                for c in range(2):
                    ins = nc.tensor.matmul(pMisc[:, 0:1], V2[:, c, :], small[:, 6 + c:7 + c], start=(c == 0), stop=(c == 1))
                ins.then_inc(S("y0_p"), 1)

        def mlp(groups, dense):
            col0, g0 = (0, 0) if dense else (N, NG)

            with nc.Block() as block:
                @block.sync
                def _(sp):
                    def load(u, k, r):
                        P, J = shape(k, dense)
                        if not fresh(k):
                            sp.wait_ge(S("z_nodes" if dense else "cols_psum"), S.at("z_nodes" if dense else "cols_psum", k + 1 - U))
                        rows_ = node_rows(x3_nodes, k) if dense else slot_rows(z_slots, k)
                        sp.dma_start(G[u][0:P, 0:J, :], rows_).then_inc(S(f"loaded{u}"), 16)

                    def stage(s, u, k, r):
                        if s == 2:
                            P, J = shape(k, dense)
                            sp.wait_ge(S("y_copied"), S.at("y_copied", k + 1))
                            sp.dma_start(y_cols[:, bass.ds(k * GC + col0, P * J)], t4[u][:, 0:P * J]).then_inc(S(f"stored{u}"), 16)

                    steps(sp, 3, groups, stage, (1, load))
                    for u in range(min(U, groups)):
                        sp.wait_ge(S(f"stored{u}"), S.at(f"stored{u}", 16 * len(range(u, groups, U))))

                if dense:
                    @block.gpsimd
                    def _(pool):
                        def stage(s, u, k, r):
                            if s == 0:
                                P, J = shape(k)
                                pool.wait_ge(S(f"loaded{u}"), S.at(f"loaded{u}", (r + 1) * 16))
                                if not fresh(k):
                                    pool.wait_ge(S("cols_psum"), S.at("cols_psum", k + 1 - U))
                                nc.gpsimd.tensor_tensor(nm(t0[u])[0:P, 0:J, :], G[u][0:P, 0:J, :],
                                                        nmask[0:P, bass.ds(4 * k, J)].unsqueeze(2).to_broadcast([P, J, D]),
                                                        ALU.mult).then_inc(S("z_nodes"), 1)

                        steps(pool, 3, groups, stage)

                @block.tensor
                def _(pe):
                    def stage(s, u, k, r):
                        P, J = shape(k, dense)
                        C = P * J
                        if s == 0:
                            pe.wait_ge(S("z_nodes"), S.at("z_nodes", k + 1)) if dense else pe.wait_ge(S(f"loaded{u}"), S.at(f"loaded{u}", (r + 1) * 16))
                            transposes(nm(t0[u]) if dense else G[u], pA[u], P, J).then_inc(S("cols_psum"), 1)
                        elif s == 1:
                            pe.wait_ge(S("cols_copied"), S.at("cols_copied", k + 1))
                            feature_major(pB[u], [(t1[u], V1[:, 0, :])], C)
                            feature_major(pA[u], [(t1[u], V1[:, 1, :])], C).then_inc(S("hidden_product"), 1)
                        elif s == 2:
                            pe.wait_ge(S("hidden_cols"), S.at("hidden_cols", k + 1))
                            feature_major(pB[u], [(t2[u], V2[:, 0, :]), (t3[u], V2[:, 1, :])], C).then_inc(S("y_product"), 1)

                    steps(pe, 3, groups, stage)

                @block.scalar
                def _(act):
                    def stage(s, u, k, r):
                        P, J = shape(k, dense)
                        C = P * J
                        if s == 0:
                            act.wait_ge(S("cols_psum"), S.at("cols_psum", k + 1))
                            nc.scalar.copy(t1[u][:, 0:C], pA[u][:, 0:C]).then_inc(S("cols_copied"), 1)
                        elif s == 1:
                            act.wait_ge(S("hidden_product"), S.at("hidden_product", k + 1))
                            nc.scalar.activation(t2[u][:, 0:C], pB[u][:, 0:C], ACTF.Relu, bias=bn[:, b_t1:b_t1 + 1],
                                                 scale=bn[:, b_s1:b_s1 + 1])
                            nc.scalar.activation(t3[u][:, 0:C], pA[u][:, 0:C], ACTF.Relu, bias=bn[:, b_t1 + 1:b_t1 + 2],
                                                 scale=bn[:, b_s1 + 1:b_s1 + 2]).then_inc(S("hidden_cols"), 1)
                        elif s == 2:
                            act.wait_ge(S("y_product"), S.at("y_product", k + 1))
                            if not fresh(k):
                                act.wait_ge(S(f"stored{u}"), S.at(f"stored{u}", r * 16))
                            if not fresh(k):
                                act.wait_ge(S("y_moments"), S.at("y_moments", k + 1 - U))
                            nc.scalar.copy(t4[u][:, 0:C], pB[u][:, 0:C]).then_inc(S("y_copied"), 1)

                    steps(act, 3, groups, stage)

                @block.vector
                def _(dve):
                    def stage(s, u, k, r):
                        if s == 2:
                            P, J = shape(k, dense)
                            dve.wait_ge(S("y_copied"), S.at("y_copied", k + 1))
                            nc.vector.bn_stats(ystat[:, bass.ds(k + g0, 1), :].rearrange("p o s -> p (o s)"),
                                               t4[u][:, 0:P * J]).then_inc(S("y_moments"), 1)

                    steps(dve, 3, groups, stage)
            finish(groups, ["cols_psum", "cols_copied", "hidden_product", "hidden_cols", "y_product", "y_copied", "y_moments"] + (["z_nodes"] if dense else []),
                   loaded=16, stored=16)

        in_flight(4, 2, "G t0 t1 t2 t3 t4")
        mlp(EG, False)
        mlp(NG, True)

        with nc.Block() as block:
            @block.gpsimd
            def _(pool):
                pool.wait_ge(S("bn2_var"), S.at("bn2_var", 1))
                nc.gpsimd.tensor_tensor(small[:, 12:13], small[:, 8:9], small[:, 14:15], ALU.pow).then_inc(S("bn2_rstd"), 1)

            @block.vector
            def _(dve):
                ch = Chain(dve, "dve_setup")
                M = N + EP
                mean, var, y0 = small[:, 0:1], small[:, 1:2], small[:, 16:17]
                m, e, f = small[:, 2:3], small[:, 3:4], small[:, 4:5]

                def tt(o, x, y, op):
                    ch.after(nc.vector.tensor_tensor(o, x, y, op))

                def ts(o, x, s1, s2=None, op0=ALU.mult, op1=ALU.bypass):
                    ch.after(nc.vector.tensor_scalar(o, x, s1, s2, op0, op1) if s2 is not None
                             else nc.vector.tensor_scalar(o, x, s1, None, op0))

                ch.after(nc.vector.bn_aggr(small[:, 0:2], ystat[:, :, :].rearrange("p g s -> p (g s)")))
                tt(e, mean, y0, ALU.subtract)
                ts(e, e, EP / N)
                tt(m, mean, e, ALU.add)
                tt(e, e, e, ALU.mult)
                tt(e, e, var, ALU.add)
                ts(e, e, M / N)
                tt(f, y0, m, ALU.subtract)
                tt(f, f, f, ALU.mult)
                ts(f, f, EP / N)
                tt(e, e, f, ALU.subtract)
                nc.vector.tensor_scalar(small[:, 8:9], e, 0.0, BN_EPS, ALU.max, ALU.add).then_inc(S("bn2_var"), 1)
                dve.wait_ge(S("bn2_rstd"), S.at("bn2_rstd", 1))
                tt(bn[:, b_s2:b_s2 + 1], bn[:, b_g2:b_g2 + 1], small[:, 12:13], ALU.mult)
                tt(e, m, bn[:, b_s2:b_s2 + 1], ALU.mult)
                tt(bn[:, b_t2:b_t2 + 1], bn[:, b_b2:b_b2 + 1], e, ALU.subtract)
                ch.close()

        def last_norm(groups, dense):
            col0 = 0 if dense else N
            per_store, kind = (16, "stored") if dense else (64, "scattered")

            with nc.Block() as block:
                @block.sync
                def _(sp):
                    def load(u, k, r):
                        P, J = shape(k, dense)
                        if not fresh(k):
                            sp.wait_ge(S("hidden_cols"), S.at("hidden_cols", k + 1 - U))
                        sp.dma_start(t1[u][:, 0:P * J], y_cols[:, bass.ds(k * GC + col0, P * J)]).then_inc(S(f"loaded{u}"), 16)

                    def load_x3(u, k, r):
                        P, J = shape(k, dense)
                        if not fresh(k):
                            sp.wait_ge(S("residual1"), S.at("residual1", k + 1 - U))
                        rows_ = node_rows(x3_nodes, k) if dense else slot_rows(x3_table, k)
                        sp.dma_start(Dn[u][0:P, 0:J, :], rows_).then_inc(S(f"loaded{u}"), 16)

                    def stage(s, u, k, r):
                        if s == 3 and dense:
                            P, J = shape(k)
                            sp.wait_ge(S("normed1"), S.at("normed1", k + 1))
                            sp.dma_start(node_rows(out, k), O[u][0:P, 0:J, :]).then_inc(S(f"stored{u}"), 16)

                    steps(sp, 4, groups, stage, (0, load), (1, load_x3))
                    if dense:
                        for u in range(min(U, groups)):
                            sp.wait_ge(S(f"stored{u}"), S.at(f"stored{u}", 16 * len(range(u, groups, U))))

                @block.gpsimd
                def _(pool):
                    def stage(s, u, k, r):
                        P, J = shape(k, dense)
                        if s == 1:
                            inv_std(pool, u, k, P, J, 1, with_shift=True)
                        elif s == 3 and not dense:
                            pool.wait_ge(S("normed1"), S.at("normed1", k + 1))
                            scatter(pool, u, k, O, out)

                    steps(pool, 4, groups, stage)
                    if not dense:
                        for u in range(min(U, groups)):
                            pool.wait_ge(S(f"scattered{u}"), S.at(f"scattered{u}", 64 * len(range(u, groups, U))))

                @block.tensor
                def _(pe):
                    def stage(s, u, k, r):
                        if s == 0:
                            P, J = shape(k, dense)
                            pe.wait_ge(S("hidden_cols"), S.at("hidden_cols", k + 1))
                            if not fresh(k):
                                pe.wait_ge(S("residual1"), S.at("residual1", k + 1 - U))
                            back_transposes(t0[u], pA[u], P, J).then_inc(S("cols_psum"), 1)

                    steps(pe, 4, groups, stage)

                @block.scalar
                def _(act):
                    def stage(s, u, k, r):
                        if s == 0:
                            P, J = shape(k, dense)
                            act.wait_ge(S(f"loaded{u}"), S.at(f"loaded{u}", (r + 1) * 32))
                            if not fresh(k):
                                act.wait_ge(S("cols_psum"), S.at("cols_psum", k + 1 - U))
                            nc.scalar.activation(t0[u][:, 0:P * J], t1[u][:, 0:P * J], ACTF.Relu, bias=bn[:, b_t2:b_t2 + 1],
                                                 scale=bn[:, b_s2:b_s2 + 1]).then_inc(S("hidden_cols"), 1)
                        elif s == 2:
                            P, J = shape(k, dense)
                            if not fresh(k):
                                act.wait_ge(S(f"{kind}{u}"), S.at(f"{kind}{u}", r * per_store))
                            normalise_on_act(act, u, k, P, J, nm(t3[u]), O[u], 1)

                    steps(act, 4, groups, stage)

                @block.vector
                def _(dve):
                    def stage(s, u, k, r):
                        P, J = shape(k, dense)
                        if s == 1:
                            dve.wait_ge(S("cols_psum"), S.at("cols_psum", k + 1))
                            dve.wait_ge(S(f"loaded{u}"), S.at(f"loaded{u}", (r + 1) * 32))
                            if not fresh(k):
                                dve.wait_ge(S("normed1"), S.at("normed1", k + 1 - U))
                            nc.vector.scalar_tensor_tensor(nm(t3[u])[0:P, 0:J, :], Dn[u][0:P, 0:J, :], 2.0,
                                                           nm(pA[u])[0:P, 0:J, :], ALU.mult,
                                                           ALU.add).then_inc(S("residual1"), 1)
                            stats(dve, u, k, P, J, nm(t3[u]), 1, negated=True)

                    steps(dve, 4, groups, stage)
            finish(groups, ["hidden_cols", "cols_psum"] + ln_signals(1) + ["inv_std_alone"] + ([] if dense else ["indices0"]), loaded=32,
                   **{kind: per_store})

        in_flight(7, 1, "Dn O t0 t1 t3")
        last_norm(NG, True)
        last_norm(EG, False)


_INPUTS = ["x", "src", "dst", "edge_attr_128", "L0_gnn_W0", "L0_gnn_b0", "L0_gnn_W1", "L0_gnn_b1", "L0_gnn_W2",
           "L0_gnn_b2", "L1_gnn_W", "L1_gnn_att_src", "L1_gnn_att_dst", "L1_gnn_bias", "L1_gnn_fc_w", "L1_gnn_fc_b",
           "L2_gnn_Wi", "L2_gnn_bi", "L2_gnn_Wm", "L2_gnn_bm", "L2_gnn_Wu", "L2_gnn_bu", "L3_gnn_eps", "L3_gnn_W1",
           "L3_gnn_g1", "L3_gnn_b1", "L3_gnn_W2", "L3_gnn_g2", "L3_gnn_b2"]


def kernel(**inputs):
    import concourse.bacc as bacc
    from concourse.bass_utils import run_bass_kernel_spmd

    nc = bacc.Bacc("TRN2", target_bir_lowering=False, num_devices=1)
    arrays, views = {}, {}
    for name in _INPUTS:
        v = np.asarray(inputs[name])
        v = np.ascontiguousarray(v.reshape(v.shape or (1,)))
        arrays[f"in_{name}"] = v
        views[name] = nc.dram_tensor(f"in_{name}", v.shape, mybir.dt.from_np(v.dtype), kind="ExternalInput").ap()
    out = nc.dram_tensor("out", views["x"].shape, F32, kind="ExternalOutput").ap()
    build(nc, views, out)
    got = run_bass_kernel_spmd(nc, [arrays], core_ids=[0])
    return got.results[0]["out"]
```

```python
import numpy as np
import concourse.bass as bass
from concourse import mybir
from contextlib import ExitStack

F32, BF16, I32 = mybir.dt.float32, mybir.dt.bfloat16, mybir.dt.int32
ALU, ACTF, AX = mybir.AluOpType, mybir.ActivationFunctionType, mybir.AxisListType

MOST = 7
D = 128
GC = 512
LN_EPS = 1e-5
BN_EPS = 1e-5
SLOPE = 0.2
FAR = 1e30


class Signals:

    def __init__(self, nc, ctx):
        self.nc, self.ctx, self.handle, self.base, self.spare = nc, ctx, {}, {}, []

    def __call__(self, name):
        if name not in self.handle:
            if self.spare:
                self.handle[name], self.base[name] = self.spare.pop()
            else:
                self.handle[name], self.base[name] = self.ctx.enter_context(self.nc.semaphore(name)), 0
        return self.handle[name]

    def retire(self, names):
        for name in names:
            self.spare.append((self.handle.pop(name), self.base.pop(name)))

    def at(self, name, n):
        self(name)
        return n + self.base[name]

    def passed(self, totals):
        for name, n in totals.items():
            self(name)
            self.base[name] += n


def build(nc, a, out):
    N = a["x"].shape[0]
    E = a["src"].shape[0]
    EG = -(-E // GC)
    EP = EG * GC
    ET = EP // 128
    NF = N // GC
    R = N - NF * GC
    TJ = next(j for j in (4, 3, 2, 1) if R % j == 0 and (R // j) % 16 == 0 and R // j <= 128) if R else 4
    TP = R // TJ if R else 128
    NG = NF + (R > 0)
    EQ = next(p for p in range(128, 0, -1) if E % p == 0)
    EW = E // EQ
    PADS = EP + 128 - E
    HEADS, HID = a["L1_gnn_att_src"].shape
    HC = HID // 2
    ROUNDS = a["L2_gnn_Wm"].shape[0]
    assert HEADS * HC == D and N + EP < 1 << 24 and EG >= 2 and NG >= 2 and ET <= 128

    ctx = ExitStack()
    with ctx:
        def sb(name, shape, dt=F32):
            return ctx.enter_context(nc.sbuf_tensor(name, shape, dt))

        def dram(name, shape, dt=F32):
            return nc.dram_tensor(name, shape, dt).ap()

        S = Signals(nc, ctx)
        psum = [ctx.enter_context(nc.psum_tensor(f"bank{i}", [128, GC], F32)) for i in range(8)]
        pGram, pMisc = psum[7], psum[6]

        sorted_src = dram("sorted_src", [EP + 128], I32)
        sorted_dst = dram("sorted_dst", [EP + 128], I32)
        sorted_edge = dram("sorted_edge", [EP + 128], I32)
        keep_row = dram("keep_row", [EP])
        count_row = dram("count_row", [EP])
        way_row = dram("way_row", [EP])
        node_slot = dram("node_slot", [N])
        gcn_table = [dram(f"gcn_table{i}", [2 * EP, D]) for i in range(3)]
        gat_table = dram("gat_table", [2 * EP, D])
        mpn_table = [dram(f"mpn_table{i}", [2 * EP, D]) for i in range(2)]
        x0_slots = dram("x0_slots", [EP, D])
        x2_slots = dram("x2_slots", [EP, D])
        x3_table = dram("x3_table", [2 * EP, D])
        attr_slots = dram("attr_slots", [EP, D])
        z_slots = dram("z_slots", [EP, D])
        x3_nodes = dram("x3_nodes", [N, D])
        y_cols = dram("y_cols", [D, N + EP])

        ident = sb("ident", [128, 128])
        zeros = sb("zeros", [128, D + 1])
        ones_bf = sb("ones_bf", [128, 128], BF16)
        W0, W1, W2 = (sb(f"W{i}", [D, D]) for i in range(3))
        Wg = sb("Wg", [D, 2, D])
        fcw = sb("fcw", [D, 2, D])
        Wi = sb("Wi", [D, D])
        Wm = sb("Wm", [D, ROUNDS, D])
        Wu = sb("Wu", [D, ROUNDS, D])
        V1 = sb("V1", [D, 2, D])
        V2 = sb("V2", [D, 2, D])
        attS, attD, attSD = (sb(n, [D, D]) for n in ("attS", "attD", "attSD"))
        ROWS = 3 + ROUNDS
        row_b2, slot_fc, row_bi, row_bu = 0, 1, 2, 3
        rows = sb("rows", [128, ROWS, D])
        bias3 = sb("bias3", [128, ROWS, D], BF16)
        rowb0, rowb1 = sb("rowb0", [128, D]), sb("rowb1", [128, D])
        cu = sb("cu", [128, ROUNDS, D])
        c_all = sb("c_all", [128, D])
        cb = sb("cb", [128, 16])
        c_b0, c_b1, c_gat, c_bm, c_bu, c_cum = 0, 1, 2, 4, 8, 12
        bn = sb("bn", [128, 16])
        b_g1, b_b1, b_g2, b_b2, b_s1, b_t1, b_s2, b_t2 = 0, 2, 4, 5, 6, 8, 10, 11
        eps1 = sb("eps1", [128, 1])
        neg_half = sb("neg_half", [128, 4])
        neg_far = sb("neg_far", [128, 1])
        idx = sb("idx", [128, ET], I32)
        idx_own = sb("idx_own", [128, ET], I32)
        src_i = sb("src_i", [128, ET], I32)
        edge_i = sb("edge_i", [128, ET], I32)
        dst_g = sb("dst_g", [128, ET], I32)
        dst_s = sb("dst_s", [128, ET], I32)
        dinv = sb("dinv", [128, ET])
        slot_f = sb("slot_f", [128, ET])
        pos = sb("pos", [128, ET])
        posN = sb("posN", [128, 4 * NG])
        w0, w1 = sb("w0", [128, ET]), sb("w1", [128, ET])
        last = sb("last", [128, ET])
        nmask = sb("nmask", [128, 4 * NG])
        ystat = sb("ystat", [128, NG + EG, 6])
        small = sb("small", [128, 24])
        gram = sb("gram", [D, D + 1])
        mrow = sb("mrow", [1, D])
        prod = sb("prod", [D, 2, D])
        onesc = sb("onesc", [128, 1])

        loads = []

        def column(dst, vec):
            loads.append((dst, vec.rearrange("(p o) -> p o", o=1)))

        def row(dst, vec):
            loads.append((dst, vec.partition_broadcast(128)))

        for dst, name in ((W0, "L0_gnn_W0"), (W1, "L0_gnn_W1"), (W2, "L0_gnn_W2"), (Wi, "L2_gnn_Wi")):
            loads.append((dst[:, :], a[name]))
        loads.append((Wm[:, :, :], a["L2_gnn_Wm"].rearrange("r i o -> i r o")))
        loads.append((Wu[:, :, :], a["L2_gnn_Wu"].rearrange("r i o -> i r o")))
        loads.append((V1[:, :, :], a["L3_gnn_W1"].rearrange("i (c o) -> i c o", c=2)))
        loads.append((V2[:, :, :], a["L3_gnn_W2"].rearrange("(c i) o -> i c o", c=2)))
        for c in range(2):
            for h in range(HEADS):
                at = HID * h + HC * c
                loads.append((Wg[:, c, HC * h:HC * (h + 1)], a["L1_gnn_W"][:, at:at + HC]))
                loads.append((fcw[HC * h:HC * (h + 1), c, :], a["L1_gnn_fc_w"][at:at + HC, :]))
                column(cb[HC * h:HC * (h + 1), c_gat + c:c_gat + c + 1], a["L1_gnn_bias"][at:at + HC])
            column(bn[:, b_g1 + c:b_g1 + c + 1], a["L3_gnn_g1"][c * D:(c + 1) * D])
            column(bn[:, b_b1 + c:b_b1 + c + 1], a["L3_gnn_b1"][c * D:(c + 1) * D])
        column(bn[:, b_g2:b_g2 + 1], a["L3_gnn_g2"])
        column(bn[:, b_b2:b_b2 + 1], a["L3_gnn_b2"])
        column(cb[:, c_b0:c_b0 + 1], a["L0_gnn_b0"])
        column(cb[:, c_b1:c_b1 + 1], a["L0_gnn_b1"])
        row(rowb0[:, :], a["L0_gnn_b0"])
        row(rowb1[:, :], a["L0_gnn_b1"])
        row(rows[:, row_b2, :], a["L0_gnn_b2"])
        row(rows[:, slot_fc, :], a["L1_gnn_fc_b"])
        row(rows[:, row_bi, :], a["L2_gnn_bi"])
        for r in range(ROUNDS):
            column(cb[:, c_bm + r:c_bm + r + 1], a["L2_gnn_bm"][r])
            column(cb[:, c_bu + r:c_bu + r + 1], a["L2_gnn_bu"][r])
            row(rows[:, row_bu + r, :], a["L2_gnn_bu"][r])
        row(eps1[:, :], a["L3_gnn_eps"])

        def tick(eng, name="pool_tick"):
            eng.sem_inc(S(name), 1)

        class Chain:

            def __init__(self, eng, name):
                self.eng, self.name, self.n = eng, name, 0

            def after(self, ins):
                ins.then_inc(S(self.name), 1)
                self.n += 1
                self.eng.wait_ge(S(self.name), S.at(self.name, self.n))

            def close(self):
                S.passed({self.name: self.n})
                self.n = 0

        with ExitStack() as scratch:
            def tmp(name, shape, dt=F32):
                return scratch.enter_context(nc.sbuf_tensor(name, shape, dt))

            wraw = tmp("wraw", [D, HEADS * HID])
            attb = tmp("attb", [D, 2, HEADS * HID])
            attp = tmp("attp", [D, 2, HEADS * HID])
            att4 = tmp("att4", [D, 3, HEADS])
            hi, mid, lo = (tmp(n, [128, ROWS, D], BF16) for n in ("hi", "mid", "lo"))
            rest = tmp("rest", [128, ROWS, D])
            loads.append((wraw[:, :], a["L1_gnn_W"]))
            row(attb[:, 0, :], a["L1_gnn_att_src"].rearrange("h f -> (h f)"))
            row(attb[:, 1, :], a["L1_gnn_att_dst"].rearrange("h f -> (h f)"))
            dA, sA, eA = (tmp(n, [EQ, EW], I32) for n in ("dA", "sA", "eA"))
            dN = tmp("dN", [EQ, 1], I32)
            loads.append((dA[:, :], a["dst"].rearrange("(p w) -> p w", w=EW)))
            loads.append((sA[:, :], a["src"].rearrange("(p w) -> p w", w=EW)))
            loads.append((dN[0:EQ - 1, :], a["dst"][EW:E].rearrange("(p w) -> p w", w=EW)[:, 0:1]))
            viol = tmp("viol", [EQ, EW])
            violc = tmp("violc", [EQ, 1])
            ones_f = tmp("ones_f", [128, 1])
            flag = tmp("flag", [1, 1], I32)
            pad_d, pad_z = tmp("pad_d", [1, PADS], I32), tmp("pad_z", [1, PADS], I32)
            iota_i = tmp("iota_i", [128, 128], I32)
            iota_f = tmp("iota_f", [128, 128])

            with nc.Block() as block:
                @block.sync
                def _(sp):
                    with nc.allow_non_contiguous_dma(reason="bias columns"):
                        for dst, src in loads:
                            sp.dma_start(dst, src).then_inc(S("weights"), 16)
                    sp.wait_ge(S("weights"), S.at("weights", 16 * len(loads)))

                @block.gpsimd
                def _(pool):
                    nc.gpsimd.memset(neg_half[:, :], -0.5)
                    nc.gpsimd.memset(neg_far[:, :], -FAR)
                    nc.gpsimd.memset(onesc[:, :], 1.0)
                    nc.gpsimd.iota(iota_i[:, :], [[1, 128]], base=0, channel_multiplier=-1)
                    nc.gpsimd.iota(eA[:, :], [[1, EW]], base=0, channel_multiplier=EW)
                    nc.gpsimd.iota(pad_d[:, :], [[1, PADS]], base=N + E, channel_multiplier=0).then_inc(S("iotas"), 1)
                    nc.gpsimd.memset(pad_z[:, :], 0)

                @block.vector
                def _(dve):
                    ch = Chain(dve, "dve_setup")
                    nc.vector.memset(ones_bf[:, :], 1.0)
                    nc.vector.memset(zeros[:, :], 0.0)
                    nc.vector.memset(ones_f[:, :], 1.0)
                    ch.after(nc.vector.memset(viol[:, :], 0.0))
                    dve.wait_ge(S("iotas"), S.at("iotas", 1))
                    ch.after(nc.vector.tensor_copy(iota_f[:, :], iota_i[:, :]))
                    ch.after(nc.vector.tensor_scalar(ident[:, :], iota_f[:, :], 0.0, None, ALU.is_equal))
                    dve.wait_ge(S("weights"), S.at("weights", 16 * len(loads)))
                    for i in range(2):
                        ch.after(nc.vector.tensor_tensor(attp[:, i, :], wraw[:, :], attb[:, i, :], ALU.mult))
                    ch.after(nc.vector.tensor_reduce(att4[:, 0:2, :].rearrange("p i h -> p (i h)"),
                                                     attp[:, :, :].rearrange("p i (h f) -> p (i h) f", h=HEADS),
                                                     AX.X, ALU.add))
                    ch.after(nc.vector.tensor_tensor(att4[:, 2, :], att4[:, 0, :], att4[:, 1, :], ALU.add))
                    for i, w in enumerate((attS, attD, attSD)):
                        for h in range(HEADS):
                            nc.vector.tensor_copy(w[:, HC * h:HC * (h + 1)], att4[:, i, h:h + 1].to_broadcast([D,
                                                  HC]))
                    ch.after(nc.vector.tensor_copy(hi[:, :, :], rows[:, :, :]))
                    ch.after(nc.vector.tensor_tensor(rest[:, :, :], rows[:, :, :], hi[:, :, :], ALU.subtract))
                    ch.after(nc.vector.tensor_copy(mid[:, :, :], rest[:, :, :]))
                    ch.after(nc.vector.tensor_tensor(lo[:, :, :], rest[:, :, :], mid[:, :, :], ALU.subtract))
                    ch.after(nc.vector.tensor_scalar(bias3[:, :, :], hi[:, :, :], ident[:, 0:1], None, ALU.mult))
                    for i, part in ((1, mid), (2, lo)):
                        ch.after(nc.vector.scalar_tensor_tensor(bias3[:, :, :], part[:, :, :], ident[:, i:i + 1],
                                                                bias3[:, :, :], ALU.mult, ALU.add))
                    ch.after(nc.vector.tensor_scalar(cu[:, :, :], rows[:, row_bu:row_bu + ROUNDS, :], 0.0, None,
                             ALU.max))
                    ch.after(nc.vector.tensor_tensor(c_all[:, :], cu[:, 0, :], cu[:, 1, :], ALU.add))
                    for r in range(2, ROUNDS):
                        ch.after(nc.vector.tensor_tensor(c_all[:, :], c_all[:, :], cu[:, r, :], ALU.add))
                    ch.after(nc.vector.tensor_scalar(cb[:, c_bu:c_bu + ROUNDS], cb[:, c_bu:c_bu + ROUNDS], 0.0,
                             None, ALU.max))
                    ch.after(nc.vector.memset(cb[:, c_cum:c_cum + 1], 0.0))
                    for r in range(1, ROUNDS):
                        ch.after(nc.vector.tensor_tensor(cb[:, c_cum + r:c_cum + r + 1], cb[:,
                                 c_cum + r - 1:c_cum + r],
                                                         cb[:, c_bu + r - 1:c_bu + r], ALU.add))
                    S("cum")
                    nc.vector.tensor_scalar(eps1[:, :], eps1[:, :], 1.0, None, ALU.add).then_inc(S("cum"), 1)
                    dve.wait_ge(S("cum_p"), S.at("cum_p", 1))
                    ch.after(nc.vector.tensor_tensor(cb[:, c_bm:c_bm + ROUNDS], cb[:, c_bm:c_bm + ROUNDS],
                                                     pMisc[:, 0:ROUNDS], ALU.add))
                    ch.after(nc.vector.tensor_tensor(viol[:, 0:EW - 1], dA[:, 1:EW], dA[:, 0:EW - 1], ALU.is_lt))
                    ch.after(nc.vector.tensor_tensor(viol[0:EQ - 1, EW - 1:EW], dN[0:EQ - 1, :],
                                                     dA[0:EQ - 1, EW - 1:EW], ALU.is_lt))
                    nc.vector.tensor_reduce(violc[:, :], viol[:, :], AX.X, ALU.add).then_inc(S("violc"), 1)
                    dve.wait_ge(S("viol_p"), S.at("viol_p", 1))
                    ch.after(nc.vector.tensor_copy(flag[:, :], pMisc[0:1, 8:9]))
                    ch.close()

                @block.tensor
                def _(pe):
                    pe.wait_ge(S("cum"), S.at("cum", 1))
                    for r in range(ROUNDS):
                        ins = nc.tensor.matmul(pMisc[:, r:r + 1], Wm[:, r, :], cb[:, c_cum + r:c_cum + r + 1],
                                               start=True, stop=True)
                    ins.then_inc(S("cum_p"), 1)
                    pe.wait_ge(S("violc"), S.at("violc", 1))
                    nc.tensor.matmul(pMisc[0:1, 8:9], violc[:, :], ones_f[0:EQ, :],
                                     start=True, stop=True).then_inc(S("viol_p"), 1)
            S.passed({"weights": 16 * len(loads), "iotas": 1, "cum": 1, "cum_p": 1, "violc": 1, "viol_p": 1})

            EF = E // 128
            ER = E - EF * 128
            DT_ = EF + (ER > 0)
            drow = tmp("drow", [128, E], I32)
            irow = tmp("irow", [128, E], I32)
            before_me = tmp("before_me", [128, E], BF16)
            equal_me = tmp("equal_me", [128, E], BF16)
            me = tmp("me", [128, 3, 1])
            me_i = tmp("me_i", [128, 4], I32)

            with nc.Block() as block:
                @block.sync
                def _(sp):
                    sp.dma_start(sorted_dst[E:EP + 128].rearrange("(o w) -> o w", o=1), pad_d[:,
                                 :]).then_inc(S("pads"), 16)
                    sp.dma_start(sorted_src[E:EP + 128].rearrange("(o w) -> o w", o=1), pad_z[:,
                                 :]).then_inc(S("pads"), 16)
                    sp.dma_start(sorted_edge[E:EP + 128].rearrange("(o w) -> o w", o=1), pad_z[:,
                                 :]).then_inc(S("pads"), 16)
                    sp.wait_ge(S("pads"), S.at("pads", 48))
                    unsorted = sp.value_load(flag[0:1, 0:1], min_val=0, max_val=E)
                    with sp.If(unsorted == 0):
                        for to, frm in ((sorted_dst, dA), (sorted_src, sA), (sorted_edge, eA)):
                            sp.dma_start(to[0:E].rearrange("(p w) -> p w", w=EW), frm[:, :]).then_inc(S("copied"), 16)
                        sp.wait_ge(S("copied"), S.at("copied", 48))

                @block.vector
                def _(dve):
                    unsorted = dve.value_load(flag[0:1, 0:1], min_val=0, max_val=E)
                    with dve.If(unsorted > 0):
                        dve.wait_ge(S("rank_in"), S.at("rank_in", 1))

                        def tile(t, P):
                            dve.wait_ge(S("me_in"), S.at("me_in", t + 1))
                            nc.vector.tensor_scalar(before_me[0:P, :], irow[0:P, :], me[0:P, 1, :], None,
                                                    ALU.is_lt).then_inc(S("rk0"), 1)
                            dve.wait_ge(S("rk0"), S.at("rk0", t + 1))
                            nc.vector.scalar_tensor_tensor(equal_me[0:P, :], drow[0:P, :], me[0:P, 0, :],
                                                           before_me[0:P, :],
                                                           ALU.is_equal, ALU.mult).then_inc(S("rk1"), 1)
                            dve.wait_ge(S("rk1"), S.at("rk1", t + 1))
                            nc.vector.scalar_tensor_tensor(before_me[0:P, :], drow[0:P, :], me[0:P, 0, :],
                                                           equal_me[0:P, :],
                                                           ALU.is_lt, ALU.add, accum_out=me[0:P, 2,
                                                                   :]).then_inc(S("rk2"), 1)
                            dve.wait_ge(S("rk2"), S.at("rk2", t + 1))
                            nc.vector.tensor_copy(me_i[0:P, 3:4], me[0:P, 2, :]).then_inc(S("rank"), 1)

                        with dve.Fori(0, EF) as t:
                            tile(t, 128)
                        if ER:
                            tile(EF, ER)

                @block.gpsimd
                def _(pool):
                    unsorted = pool.value_load(flag[0:1, 0:1], min_val=0, max_val=E)
                    with pool.If(unsorted > 0):
                        nc.gpsimd.iota(irow[:, :], [[1, E]], base=0, channel_multiplier=0).then_inc(S("rank_iota"), 1)
                        pool.dma_start(drow[:, :], a["dst"].partition_broadcast(128)).then_inc(S("rank_row"), 16)
                        pool.wait_ge(S("rank_iota"), S.at("rank_iota", 1))
                        pool.wait_ge(S("rank_row"), S.at("rank_row", 16))
                        nc.gpsimd.memset(me_i[:, :], 0).then_inc(S("rank_in"), 1)
                        pool.wait_ge(S("rank_in"), S.at("rank_in", 1))

                        def tile(t, P):
                            for i, frm in ((0, a["dst"]), (1, a["src"])):
                                pool.dma_start(me_i[0:P, i:i + 1],
                                               frm[bass.ds(t * 128, P)].rearrange("(p o) -> p o",
                                                           o=1)).then_inc(S("me_ld"), 16)
                            pool.wait_ge(S("me_ld"), S.at("me_ld", t * 32 + 32))
                            tick(pool)
                            nc.gpsimd.tensor_copy(me[0:P, 0, :], me_i[0:P, 0:1]).then_inc(S("me_d"), 1)
                            pool.wait_ge(S("me_d"), S.at("me_d", t + 1))
                            tick(pool)
                            nc.gpsimd.tensor_copy(me_i[0:P, 2:3], pos[0:P, :]).then_inc(S("me_p"), 1)
                            pool.wait_ge(S("me_p"), S.at("me_p", t + 1))
                            tick(pool)
                            nc.gpsimd.tensor_copy(me[0:P, 1, :], me_i[0:P, 2:3]).then_inc(S("me_in"), 1)
                            pool.wait_ge(S("me_in"), S.at("me_in", t + 1))
                            nc.gpsimd.tensor_tensor(pos[:, :], pos[:, :], step128[:, :],
                                                    ALU.add).then_inc(S("me_n"), 1)
                            pool.wait_ge(S("me_n"), S.at("me_n", t + 1))
                            pool.wait_ge(S("rank"), S.at("rank", t + 1))
                            tick(pool)
                            for i, to in ((0, sorted_dst), (1, sorted_src), (2, sorted_edge)):
                                nc.gpsimd.indirect_dma_start(
                                    out=to.rearrange("(n o) -> n o", o=1), in_=me_i[0:P, i:i + 1], in_offset=None,
                                    out_offset=bass.IndirectOffsetOnAxis(ap=me_i[0:P, 3:4],
                                            axis=0)).then_inc(S("me_out"), 16)
                            pool.wait_ge(S("me_out"), S.at("me_out", t * 48 + 48))

                        pos, step128 = iota_i[:, 0:1], iota_i[:, 1:2]
                        nc.gpsimd.iota(pos, [[0, 1]], base=0, channel_multiplier=1).then_inc(S("me_c"), 1)
                        nc.gpsimd.iota(step128, [[0, 1]], base=128, channel_multiplier=0).then_inc(S("me_c"), 1)
                        pool.wait_ge(S("me_c"), S.at("me_c", 2))
                        with pool.Fori(0, EF) as t:
                            tile(t, 128)
                        if ER:
                            tile(EF, ER)
            S.passed({"pads": 48})

        NP_ = next(p for p in range(128, 0, -1) if N % p == 0)
        with ExitStack() as scratch:
            def tmp(name, shape, dt=F32):
                return scratch.enter_context(nc.sbuf_tensor(name, shape, dt))

            dT, sT, eT, pT, nT = (tmp(n, [ET, 128], I32) for n in ("dT", "sT", "eT", "pT", "nT"))
            flags = tmp("flags", [ET, 7, 128])
            real = tmp("real", [ET, 128])
            keep1, count1, way1 = tmp("keep_line", [1, EP + 1]), tmp("count_line", [1, EP]), tmp("way_line", [1, EP])
            one1 = tmp("one1", [1, 1])
            cols = tmp("cols", [128, 6, ET])
            slot_i, far_i = tmp("slot_i", [128, ET], I32), tmp("far_i", [128, ET], I32)
            far_f = tmp("far_f", [128, ET])
            none = tmp("none", [NP_, N // NP_])
            tiles = [(sorted_dst, dT), (sorted_src, sT), (sorted_edge, eT)]

            def as_tiles(t, first=0):
                return t[first:first + EP].rearrange("(t p) -> t p", p=128)

            with nc.Block() as block:
                @block.sync
                def _(sp):
                    for frm, to in tiles:
                        sp.dma_start(to[:, :], as_tiles(frm)).then_inc(S("tiles_in"), 16)
                    sp.dma_start(nT[:, :], as_tiles(sorted_dst, 1)).then_inc(S("tiles_in"), 16)
                    sp.dma_start(pT[1:ET, :], sorted_dst[127:EP - 1].rearrange("(t p) -> t p",
                                 p=128)).then_inc(S("tiles_in"), 16)
                    sp.dma_start(pT[0:1, 1:128], sorted_dst[0:127].rearrange("(t p) -> t p",
                                 t=1)).then_inc(S("tiles_in"), 16)
                    sp.wait_ge(S("keep_ok"), S.at("keep_ok", 1))
                    sp.dma_start(as_tiles(keep_row), flags[:, 3, :]).then_inc(S("rows_io"), 16)
                    sp.wait_ge(S("rows_io"), S.at("rows_io", 16))
                    sp.dma_start(keep1[:, 0:EP], keep_row.rearrange("(o w) -> o w", o=1)).then_inc(S("rows_io"), 16)
                    sp.wait_ge(S("rows_io"), S.at("rows_io", 32))
                    sp.nop().then_inc(S("keep1_in"), 1)
                    sp.wait_ge(S("count_ok"), S.at("count_ok", 1))
                    sp.dma_start(count_row.rearrange("(o w) -> o w", o=1), count1[:, :]).then_inc(S("rows_io"), 16)
                    sp.wait_ge(S("rows_io"), S.at("rows_io", 48))
                    sp.dma_start(flags[:, 5, :], as_tiles(count_row)).then_inc(S("rows_io"), 16)
                    sp.wait_ge(S("rows_io"), S.at("rows_io", 64))
                    sp.wait_ge(S("way_ok"), S.at("way_ok", 1))
                    sp.dma_start(way_row.rearrange("(o w) -> o w", o=1), way1[:, :]).then_inc(S("rows_io"), 16)
                    sp.wait_ge(S("rows_io"), S.at("rows_io", 80))
                    sp.dma_start(flags[:, 6, :], as_tiles(way_row)).then_inc(S("rows_io"), 16)
                    sp.wait_ge(S("none_ok"), S.at("none_ok", 1))
                    sp.dma_start(node_slot.rearrange("(p w) -> p w", p=NP_), none[:, :]).then_inc(S("none_out"), 16)
                    sp.wait_ge(S("rows_io"), S.at("rows_io", 96))
                    sp.wait_ge(S("none_out"), S.at("none_out", 16))

                @block.gpsimd
                def _(pool):
                    nc.gpsimd.iota(slot_i[:, :], [[128, ET]], base=0, channel_multiplier=1)
                    nc.gpsimd.iota(far_i[:, :], [[128, ET]], base=N,
                                   channel_multiplier=1).then_inc(S("slot_iotas"), 1)

                @block.vector
                def _(dve):
                    ch = Chain(dve, "dve_setup")
                    nc.vector.memset(pT[0:1, 0:1], -1).then_inc(S("first_prev"), 1)
                    nc.vector.memset(one1[:, :], 1.0)
                    ch.after(nc.vector.memset(keep1[:, EP:EP + 1], 0.0))
                    nc.vector.memset(none[:, :], -1.0).then_inc(S("none_ok"), 1)
                    dve.wait_ge(S("slot_iotas"), S.at("slot_iotas", 1))
                    nc.vector.tensor_copy(slot_f[:, :], slot_i[:, :])
                    nc.vector.tensor_copy(far_f[:, :], far_i[:, :])
                    dve.wait_ge(S("first_prev"), S.at("first_prev", 1))
                    dve.wait_ge(S("tiles_in"), S.at("tiles_in", 96))
                    nc.vector.tensor_tensor(flags[:, 3, :], dT[:, :], pT[:, :],
                                            ALU.is_equal).then_inc(S("keep_ok"), 1)
                    for i, t in enumerate((dT, sT, eT)):
                        nc.vector.tensor_copy(flags[:, i, :], t[:, :])
                    nc.vector.tensor_scalar(real[:, :], dT[:, :], float(N), None, ALU.is_lt)
                    ch.after(nc.vector.tensor_tensor(flags[:, 4, :], dT[:, :], nT[:, :], ALU.not_equal))
                    ch.after(nc.vector.tensor_tensor(flags[:, 4, :], flags[:, 4, :], real[:, :], ALU.mult))
                    dve.wait_ge(S("keep1_in"), S.at("keep1_in", 1))
                    nc.vector.tensor_tensor_scan(count1[:, :], keep1[:, 0:EP], one1[:, 0:1].to_broadcast([1, EP]),
                                                 0.0,
                                                 ALU.mult, ALU.add).then_inc(S("count_ok"), 1)
                    nc.vector.tensor_tensor_scan(way1[:, ::-1], keep1[:, EP:0:-1], keep1[:, EP:0:-1], 0.0,
                                                 ALU.mult, ALU.add).then_inc(S("way_ok"), 1)
                    dve.wait_ge(S("flags_p"), S.at("flags_p", 1))
                    ch.after(nc.vector.tensor_copy(cols[:, 0:4, :], pMisc[:,
                             0:4 * ET].rearrange("p (i t) -> p i t", i=4)))
                    ch.after(nc.vector.tensor_copy(cols[:, 4:6, :], pGram[:,
                             0:2 * ET].rearrange("p (i t) -> p i t", i=2)))
                    nc.vector.tensor_copy(src_i[:, :], cols[:, 1, :])
                    nc.vector.tensor_copy(edge_i[:, :], cols[:, 2, :])
                    nc.vector.tensor_copy(last[:, :], cols[:, 3, :])
                    ch.after(nc.vector.tensor_scalar(w0[:, :], cols[:, 0, :], float(N), None, ALU.is_lt))
                    ch.after(nc.vector.tensor_tensor(dst_g[:, :], w0[:, :], cols[:, 0, :], ALU.mult))
                    ch.after(nc.vector.tensor_tensor(w0[:, :], cols[:, 0, :], far_f[:, :], ALU.subtract))
                    ch.after(nc.vector.tensor_tensor(w0[:, :], w0[:, :], cols[:, 3, :], ALU.mult))
                    ch.after(nc.vector.tensor_tensor(dst_s[:, :], w0[:, :], far_f[:, :], ALU.add))
                    ch.after(nc.vector.tensor_scalar(dinv[:, :], cols[:, 4, :], 1.0, None, ALU.add))
                    ch.after(nc.vector.tensor_tensor(idx_own[:, :], cols[:, 5, :], slot_f[:, :], ALU.add))
                    ch.close()

                @block.tensor
                def _(pe):
                    pe.wait_ge(S("count_ok"), S.at("count_ok", 1))
                    pe.wait_ge(S("rows_io"), S.at("rows_io", 96))
                    for at, i in enumerate((0, 1, 2, 4)):
                        nc.tensor.transpose(pMisc[:, at * ET:(at + 1) * ET], flags[:, i, :], ident[0:ET, 0:ET])
                    nc.tensor.transpose(pGram[:, 0:ET], flags[:, 5, :], ident[0:ET, 0:ET])
                    nc.tensor.transpose(pGram[:, ET:2 * ET], flags[:, 6, :], ident[0:ET,
                                        0:ET]).then_inc(S("flags_p"), 1)
            S.passed({"tiles_in": 96, "keep_ok": 1, "rows_io": 96, "way_ok": 1, "none_out": 16, "keep1_in": 1,
                     "count_ok": 1, "none_ok": 1,
                      "slot_iotas": 1, "first_prev": 1, "flags_p": 1})

        for u in range(MOST):
            S(f"gathered{u}")
            S(f"scattered{u}")
        S.retire(["weights", "iotas", "cum", "cum_p", "violc", "viol_p", "pads", "tiles_in", "keep_ok", "rows_io",
                  "none_out", "keep1_in", "count_ok", "way_ok", "none_ok", "slot_iotas", "first_prev", "flags_p"])

        U = phases = 0
        held = ctx.enter_context(ExitStack())
        SHAPES = {"A": [128, GC + 1], "Mx": [128, GC + 1], "Sc0": [128, GC + 1], "Sc1": [128, GC + 1],
                  "keep": [128, GC], "soft": [128, 3, GC], "zm": [128, 4, D + 1], "st": [128, 4, 6],
                  "mv": [128, 4, 2], "vpe": [128, 4], "shift": [128, 4], "rstd": [128, 4], "idxs": [128, 8],
                         "G": [128, 4, D], "G2": [128, 4, D], "attr": [128, D], "own_x": [128, D],
                  "own_h": [128, D], "look": [128, 1],
                  "Dn": [128, 4, D], "O": [128, 4, D], **{f"t{i}": [128, GC] for i in range(8)}}
        buffers = {name: [] for name in SHAPES}
        G, G2, Dn, O, keep, soft, zm = (buffers[n] for n in ("G", "G2", "Dn", "O", "keep", "soft", "zm"))
        A, Mx, Sc0, Sc1 = (buffers[n] for n in ("A", "Mx", "Sc0", "Sc1"))
        st, mv, vpe, shift, rstd, idxs = (buffers[n] for n in ("st", "mv", "vpe", "shift", "rstd", "idxs"))
        attr, own_x, own_h, look = (buffers[n] for n in ("attr", "own_x", "own_h", "look"))
        t0, t1, t2, t3, t4, t5, t6, t7 = (buffers[f"t{i}"] for i in range(8))
        pA, pB = [], []

        def in_flight(n, banks, names):
            nonlocal U, phases
            U, phases = n, phases + 1
            pA[:] = psum[0:n]
            pB[:] = psum[0:n] if banks == 1 else psum[n:2 * n]
            held.close()
            names = names.split() + ["st", "mv", "vpe", "shift", "rstd", "idxs"]
            for name in buffers:
                buffers[name][:] = [held.enter_context(nc.sbuf_tensor(
                    f"{name}_{phases}_{u}", SHAPES[name], I32 if name == "idxs" else F32))
                    for u in range(n)] if name in names else []
            with nc.Block() as block:
                @block.vector
                def _(dve):
                    for name in ("A", "Mx", "Sc0", "Sc1"):
                        if name in names:
                            nc.vector.memset(buffers[name][n - 1][:, :], 0.0)
                    for z in zm:
                        nc.vector.memset(z[:, :, :], 1.0)

        def nm(t):
            return t[:, 0:GC].rearrange("p (j d) -> p j d", j=4)

        def shape(k, dense=True):
            return (TP, TJ) if dense and isinstance(k, int) and k >= NF else (128, 4)

        def steps(eng, steps_n, groups, stage, *loads):
            nb = -(-groups // U)

            def body(b):
                for s in range(steps_n):
                    at_step = []
                    for u in range(U):
                        t = s - u * steps_n // U
                        back = 1 if t < 0 else 0
                        k, r = b * U + (u - U * back), b - back
                        if not isinstance(k, int) or 0 <= k < groups:
                            at_step.append((t + steps_n * back, u, k, r))
                    for step, u, k, r in at_step:
                        if stage:
                            stage(step, u, k, r)
                    for step, u, k, r in at_step:
                        for ahead, load in loads:
                            if step == ahead and not (isinstance(k, int) and k + U >= groups):
                                load(u, k + U, r + 1)

            for k in range(min(U, groups)):
                for _, load in loads:
                    load(k, k, 0)
            if nb >= 4:
                body(0)
                with eng.Fori(1, nb - 2) as b:
                    body(b)
                for b in range(nb - 2, nb + 1):
                    body(b)
            else:
                for b in range(nb + 1):
                    body(b)

        def fresh(k):
            return isinstance(k, int) and k < U

        def finish(groups, engine, **dma):
            tot = dict.fromkeys(engine, groups)
            for name, per in dma.items():
                for u in range(U):
                    tot[f"{name}{u}"] = per * len(range(u, groups, U))
            S.passed(tot)

        CREDITED = {"biased_rows": "vector", "scaled_rows": "scalar", "state_rows": "scalar", "state_updated": "vector", "segments_summed": "vector",
                    "update_rows": "scalar", "messages": "scalar", "cols_psum": "tensor", "z_masked": "gpsimd", "y_moments": "vector", "loop_added": "vector",
                    "residual1": "vector", "residual3": "vector"}

        def transposes(src, bank, P=128, J=4):
            for j in range(J):
                ins = nc.tensor.transpose(bank[:, j * P:(j + 1) * P], src[0:P, j, :], ident[0:P, 0:P])
            return ins

        def back_transposes(cols, bank, P=128, J=4):
            for j in range(J):
                ins = nc.tensor.transpose(bank[0:P, j * D:(j + 1) * D], cols[:, j * P:(j + 1) * P], ident[:, :])
            return ins

        def to_node_major(bank, parts, P=128, J=4, row=None):
            if row is not None:
                nc.tensor.matmul(bank[0:P, 0:J * D].rearrange("p (j d) -> p j d", j=J), ones_bf[:, 0:P],
                                 bias3[:, row, :].unsqueeze(1).to_broadcast([128, J, D]), start=True, stop=False,
                                 skip_group_check=True)
            for j in range(J):
                for i, (cols, w) in enumerate(parts):
                    ins = nc.tensor.matmul(bank[0:P, j * D:(j + 1) * D], cols[:, j * P:(j + 1) * P], w,
                                           start=(row is None and j == 0 and i == 0),
                                           stop=(i == len(parts) - 1), skip_group_check=True)
            return ins

        def feature_major(bank, parts, C=GC):
            for i, (cols, w) in enumerate(parts):
                ins = nc.tensor.matmul(bank[:, 0:C], w, cols[:, 0:C], start=(i == 0), stop=(i == len(parts) - 1))
            return ins

        def stats(dve, u, k, P, J, src, tag, negated=False):
            dve.wait_ge(S(f"residual{tag}"), S.at(f"residual{tag}", k + 1))
            for j in range(J):
                ins = nc.vector.bn_stats(st[u][0:P, j, :], src[0:P, j, :])
            ins.then_inc(S(f"moments{tag}"), 1)
            dve.wait_ge(S(f"moments{tag}"), S.at(f"moments{tag}", k + 1))
            tick(dve, "vector_tick")
            for j in range(J):
                ins = nc.vector.bn_aggr(mv[u][0:P, j, :], st[u][0:P, j, :])
            ins.then_inc(S(f"variance{tag}"), 1)
            dve.wait_ge(S(f"variance{tag}"), S.at(f"variance{tag}", k + 1))
            if negated:
                nc.vector.tensor_scalar(mv[u][0:P, 0:J, 0], mv[u][0:P, 0:J, 0], -1.0, None, ALU.mult)
            nc.vector.tensor_scalar(vpe[u][0:P, 0:J], mv[u][0:P, 0:J, 1], LN_EPS, None,
                                    ALU.add).then_inc(S(f"var_eps{tag}"), 1)

        def inv_std(pool, u, k, P, J, tag, with_shift=False):
            pool.wait_ge(S(f"var_eps{tag}"), S.at(f"var_eps{tag}", k + 1))
            ins = nc.gpsimd.tensor_tensor(rstd[u][0:P, 0:J], vpe[u][0:P, 0:J], neg_half[0:P, 0:J], ALU.pow)
            if with_shift:
                ins.then_inc(S("inv_std_alone"), 1)
                pool.wait_ge(S("inv_std_alone"), S.at("inv_std_alone", k + 1))
                ins = nc.gpsimd.tensor_tensor(shift[u][0:P, 0:J], mv[u][0:P, 0:J, 0], rstd[u][0:P, 0:J], ALU.mult)
            ins.then_inc(S(f"inv_std{tag}"), 1)

        def normalise(dve, u, k, P, J, src, dst, tag):
            dve.wait_ge(S(f"inv_std{tag}"), S.at(f"inv_std{tag}", k + 1))
            for j in range(J):
                ins = nc.vector.tensor_scalar(dst[0:P, j, :], src[0:P, j, :], mv[u][0:P, j, 0:1],
                                              rstd[u][0:P, j:j + 1], ALU.subtract, ALU.mult)
            ins.then_inc(S(f"normed{tag}"), 1)

        def normalise_on_act(act, u, k, P, J, src, dst, tag):
            act.wait_ge(S(f"inv_std{tag}"), S.at(f"inv_std{tag}", k + 1))
            for j in range(J):
                ins = nc.scalar.activation(dst[0:P, j, :], src[0:P, j, :], ACTF.Identity, bias=shift[u][0:P, j:j + 1],
                                           scale=rstd[u][0:P, j:j + 1])
            ins.then_inc(S(f"normed{tag}"), 1)

        def ln_signals(*tags):
            return [f"{n}{t}" for t in tags for n in ("residual", "moments", "variance", "var_eps", "inv_std",
                                                      "normed")]

        def scan(dst, d0, d1, before, op0, op1):
            return nc.vector.tensor_tensor_scan(dst[:, 1:GC + 1], d0, d1, before[:, GC:GC + 1], op0, op1)

        def gather(pool, u, k, cols, table, dst, at):
            nc.gpsimd.tensor_copy(idxs[u][:, at:at + 4], cols[:, bass.ds(4 * k, 4)]).then_inc(S(f"indices{at}"), 1)
            pool.wait_ge(S(f"indices{at}"), S.at(f"indices{at}", k + 1))
            tick(pool)
            for j in range(4):
                nc.gpsimd.indirect_dma_start(
                    out=dst[u][:, j, :], out_offset=None, in_=table,
                    in_offset=bass.IndirectOffsetOnAxis(ap=idxs[u][:, at + j:at + j + 1], axis=0),
                ).then_inc(S(f"gathered{u}"), 16)

        def place_last_slots(u, k, r):
            pool = pool_
            if not fresh(k):
                pool.wait_ge(S(f"scattered{u}"), S.at(f"scattered{u}", r * 64))
                tick(pool)
            nc.gpsimd.tensor_copy(idxs[u][:, 4:8], dst_s[:, bass.ds(4 * k, 4)])
            nc.gpsimd.tensor_copy(shift[u][:, 0:4], slot_f[:, bass.ds(4 * k, 4)]).then_inc(S("slots_in"), 1)
            pool.wait_ge(S("slots_in"), S.at("slots_in", k + 1))
            tick(pool)
            for j in range(4):
                nc.gpsimd.indirect_dma_start(
                    out=node_slot.rearrange("(n o) -> n o", o=1), in_=shift[u][:, j:j + 1], in_offset=None,
                    out_offset=bass.IndirectOffsetOnAxis(ap=idxs[u][:, 4 + j:5 + j], axis=0),
                    bounds_check=N - 1, oob_is_err=False).then_inc(S(f"scattered{u}"), 16)

        def fetch_tile(pool, u, t, n, r):
            if not fresh(n):
                pool.wait_ge(S("looked_up"), S.at("looked_up", n + 1 - U))
                tick(pool)
                pool.wait_ge(S(f"kept{u}"), S.at(f"kept{u}", r * 48))
                tick(pool)
            nc.gpsimd.tensor_copy(idxs[u][:, 0:1], edge_i[:, bass.ds(t, 1)])
            nc.gpsimd.tensor_copy(idxs[u][:, 1:2], dst_g[:, bass.ds(t, 1)])
            nc.gpsimd.tensor_copy(idxs[u][:, 2:3], src_i[:, bass.ds(t, 1)]).then_inc(S("indices0"), 1)
            pool.wait_ge(S("indices0"), S.at("indices0", n + 1))
            tick(pool)
            for i, (dst, table) in enumerate(((attr, a["edge_attr_128"]), (own_x, a["x"]),
                                              (look, node_slot.rearrange("(n o) -> n o", o=1)))):
                nc.gpsimd.indirect_dma_start(
                    out=dst[u][:, :], out_offset=None, in_=table,
                    in_offset=bass.IndirectOffsetOnAxis(ap=idxs[u][:, i:i + 1],
                                                        axis=0)).then_inc(S(f"gathered{u}"), 16)

        def keep_lookup(pool, u, t, n, r):
            pool.wait_ge(S(f"gathered{u}"), S.at(f"gathered{u}", (r + 1) * 48))
            tick(pool)
            nc.gpsimd.tensor_copy(pos[:, bass.ds(t, 1)], look[u][:, :]).then_inc(S("looked_up"), 1)

        def scale_tile(act, u, t, r):
            act.wait_ge(S(f"gathered{u}"), S.at(f"gathered{u}", (r + 1) * 48))
            nc.scalar.activation(own_h[u][:, :], own_x[u][:, :], ACTF.Copy,
                                 scale=dinv[:, bass.ds(t, 1)]).then_inc(S("scaled_rows"), 1)

        def store_tile(sp, u, t, n):
            sp.wait_ge(S("scaled_rows"), S.at("scaled_rows", n + 1))
            for table, rows_ in ((attr_slots, attr), (x0_slots, own_x), (gcn_table[0], own_h)):
                sp.dma_start(table[bass.ds(t * 128, 128), :], rows_[u][:, :]).then_inc(S(f"kept{u}"), 16)

        def scatter(pool, u, k, src, table):
            nc.gpsimd.tensor_copy(idxs[u][:, 0:4], dst_s[:, bass.ds(4 * k, 4)]).then_inc(S("indices0"), 1)
            pool.wait_ge(S("indices0"), S.at("indices0", k + 1))
            tick(pool)
            for j in range(4):
                nc.gpsimd.indirect_dma_start(
                    out=table, in_=src[u][:, j, :], in_offset=None,
                    out_offset=bass.IndirectOffsetOnAxis(ap=idxs[u][:, j:j + 1], axis=0),
                    bounds_check=N - 1, oob_is_err=False).then_inc(S(f"scattered{u}"), 16)

        def slot_rows(t, k, half=0):
            return t[bass.ds(k * GC + half * EP, GC), :].rearrange("(j p) d -> p j d", j=4)

        def node_rows(t, k):
            P, J = shape(k)
            return t[bass.ds(k * GC, P * J), :].rearrange("(p j) d -> p j d", j=J)

        def keep_cols(k):
            return keep_row[bass.ds(k * GC, GC)].partition_broadcast(128)

        with nc.Block() as block:
            @block.vector
            def _(dve):
                for name, owner in CREDITED.items():
                    if owner == "vector":
                        dve.nop().then_inc(S(name), MOST)

            @block.scalar
            def _(act):
                for name, owner in CREDITED.items():
                    if owner == "scalar":
                        act.nop().then_inc(S(name), MOST)

            @block.gpsimd
            def _(pool):
                for name, owner in CREDITED.items():
                    if owner == "gpsimd":
                        pool.nop().then_inc(S(name), MOST)

            @block.tensor
            def _(pe):
                for name, owner in CREDITED.items():
                    if owner == "tensor":
                        pe.nop().then_inc(S(name), MOST)
        S.passed({name: MOST for name in CREDITED})

        def chain(groups, dense):
            walk = list(range(15)) if dense else [0, 1, "rows of h1", 2, "rows of h2", *range(3, 12), "residual", 12]
            n_steps, after_residual = len(walk), walk.index(3)
            per_store = 16 if dense else 16 * 6

            def sp_load(u, k, r):
                if not fresh(k):
                    sp_.wait_ge(S("residual1"), S.at("residual1", k + 1 - U))
                P, J = shape(k)
                sp_.dma_start(G[u][0:P, 0:J, :], node_rows(a["x"], k)).then_inc(S(f"loaded{u}"), 16)

            def pool_load(u, k, r):
                if not fresh(k):
                    pool_.wait_ge(S("residual1"), S.at("residual1", k + 1 - U))
                    pool_.wait_ge(S(f"kept{u}"), S.at(f"kept{u}", r * 16))
                gather(pool_, u, k, src_i, a["x"], G, 0)

            def arrived(eng, u, r):
                if dense:
                    eng.wait_ge(S(f"loaded{u}"), S.at(f"loaded{u}", (r + 1) * 16))
                else:
                    eng.wait_ge(S(f"gathered{u}"), S.at(f"gathered{u}", (r + 1) * 64))

            with nc.Block() as block:
                @block.sync
                def _(sp):
                    nonlocal sp_
                    sp_ = sp

                    def stage(step, u, k, r):
                        s = walk[step]
                        if dense and s == 12:
                            P, J = shape(k)
                            sp.wait_ge(S("normed3"), S.at("normed3", k + 1))
                            sp.dma_start(node_rows(x3_nodes, k), O[u][0:P, 0:J, :]).then_inc(S(f"stored{u}"), 16)
                        if dense and s == 9:
                            store_tile(sp, u, k, k)
                        if not dense:
                            if s == 0:
                                sp.wait_ge(S(f"gathered{u}"), S.at(f"gathered{u}", (r + 1) * 64))
                                sp.dma_start(slot_rows(gcn_table[0], k, 1), G[u][:, :, :]).then_inc(S(f"kept{u}"), 16)
                            elif s == "rows of h1":
                                sp.wait_ge(S("h1_rows"), S.at("h1_rows", k + 1))
                                sp.dma_start(slot_rows(gcn_table[1], k, 1), O[u][:, :,
                                             :]).then_inc(S(f"stored{u}"), 16)
                            elif s == "rows of h2":
                                sp.wait_ge(S("h2_rows"), S.at("h2_rows", k + 1))
                                sp.dma_start(slot_rows(gcn_table[2], k, 1), G2[u][:, :,
                                             :]).then_inc(S(f"stored{u}"), 16)
                            elif s == 4:
                                sp.wait_ge(S("normed1"), S.at("normed1", k + 1))
                                sp.dma_start(slot_rows(gat_table, k, 1), nm(t4[u])).then_inc(S(f"stored{u}"), 16)
                            elif s == 11:
                                sp.wait_ge(S("state_rows"), S.at("state_rows", k + 1))
                                for t in mpn_table:
                                    sp.dma_start(slot_rows(t, k, 1), Dn[u][:, :, :]).then_inc(S(f"stored{u}"), 16)
                            elif s == 12:
                                sp.wait_ge(S("normed3"), S.at("normed3", k + 1))
                                sp.dma_start(slot_rows(x3_table, k, 1), nm(t5[u])).then_inc(S(f"stored{u}"), 16)

                    steps(sp, n_steps, groups, stage, *([(after_residual, sp_load)] if dense else []))
                    for u in range(min(U, groups)):
                        sp.wait_ge(S(f"stored{u}"), S.at(f"stored{u}", per_store * len(range(u, groups, U))))
                    for u in range(min(U, groups)):
                        sp.wait_ge(S(f"kept{u}"), S.at(f"kept{u}", (48 if dense else 16) * len(range(u, groups, U))))

                @block.gpsimd
                def _(pool):
                    nonlocal pool_
                    pool_ = pool

                    def stage(step, u, k, r):
                        s = walk[step]
                        P, J = shape(k, dense)
                        if s == 7 and dense:
                            keep_lookup(pool, u, k, k, r)
                        elif s == 3:
                            inv_std(pool, u, k, P, J, 1)
                        elif s == 8:
                            inv_std(pool, u, k, P, J, 2)
                        elif s == 10:
                            pool.wait_ge(S("normed2"), S.at("normed2", k + 1))
                            nc.gpsimd.tensor_tensor(nm(t2[u])[0:P, 0:J, :], nm(t5[u])[0:P, 0:J, :],
                                                    c_all[0:P, :].unsqueeze(1).to_broadcast([P, J, D]),
                                                    ALU.add).then_inc(S("x2_with_gains"), 1)
                        elif s == (11 if dense else "residual"):
                            inv_std(pool, u, k, P, J, 3)

                    steps(pool, n_steps, groups, stage, *([(12, lambda u, k, r: fetch_tile(pool_, u, k, k,
                          r))] if dense else [(after_residual, pool_load), (8, place_last_slots)]))
                    if not dense:
                        for u in range(min(U, groups)):
                            pool.wait_ge(S(f"scattered{u}"), S.at(f"scattered{u}", 64 * len(range(u, groups, U))))

                @block.tensor
                def _(pe):
                    def stage(step, u, k, r):
                        s = walk[step]
                        P, J = shape(k, dense)
                        C = P * J
                        if s == 0:
                            arrived(pe, u, r)
                            if not fresh(k):
                                pe.wait_ge(S("residual3"), S.at("residual3", k + 1 - U))
                            transposes(G[u], pA[u], P, J).then_inc(S("x_transposed"), 1)
                        elif s == 1:
                            pe.wait_ge(S("x_cols"), S.at("x_cols", k + 1))
                            feature_major(pB[u], [(t0[u], W0[:, :])], C).then_inc(S("h1_product"), 1)
                        elif s == "rows of h1":
                            pe.wait_ge(S("h1_cols"), S.at("h1_cols", k + 1))
                            back_transposes(t1[u], pB[u]).then_inc(S("h1_back"), 1)
                        elif s == "rows of h2":
                            pe.wait_ge(S("h2_cols"), S.at("h2_cols", k + 1))
                            back_transposes(t2[u], pA[u]).then_inc(S("h2_back"), 1)
                        elif s == 2:
                            pe.wait_ge(S("h1_cols" if dense else "h1_rows"),
                                       S.at("h1_cols" if dense else "h1_rows", k + 1))
                            feature_major(pA[u], [(t1[u], W1[:, :])], C).then_inc(S("h2_product"), 1)
                        elif s == 3:
                            pe.wait_ge(S("h2_cols" if dense else "h2_rows"),
                                       S.at("h2_cols" if dense else "h2_rows", k + 1))
                            to_node_major(pB[u], [(t2[u], W2[:, :])], P, J, row_b2).then_inc(S("h3_product"), 1)
                        elif s == 5:
                            pe.wait_ge(S("normed1"), S.at("normed1", k + 1))
                            transposes(nm(t4[u]), pA[u], P, J).then_inc(S("x1_transposed"), 1)
                        elif s == 6:
                            pe.wait_ge(S("x1_cols"), S.at("x1_cols", k + 1))
                            feature_major(pB[u], [(t0[u], Wg[:, 0, :])], C).then_inc(S("head_product0"), 1)
                        elif s == 7:
                            pe.wait_ge(S("head_relu0"), S.at("head_relu0", k + 1))
                            feature_major(pA[u], [(t0[u], Wg[:, 1, :])], C).then_inc(S("head_product1"), 1)
                        elif s == 8:
                            pe.wait_ge(S("head_relu1"), S.at("head_relu1", k + 1))
                            to_node_major(pB[u], [(t1[u], fcw[:, 0, :]), (t2[u], fcw[:, 1, :])], P, J,
                                          slot_fc).then_inc(S("gat_product"), 1)
                        elif s == 10:
                            pe.wait_ge(S("normed2"), S.at("normed2", k + 1))
                            transposes(nm(t5[u]), pA[u], P, J).then_inc(S("x2_transposed"), 1)
                        elif s == 11:
                            pe.wait_ge(S("x2_cols"), S.at("x2_cols", k + 1))
                            to_node_major(pB[u], [(t0[u], Wi[:, :])], P, J, row_bi).then_inc(S("state_product"), 1)
                        elif s == 14:
                            pe.wait_ge(S("z_masked"), S.at("z_masked", k + 1))
                            for j in range(J):
                                nc.tensor.matmul(pGram[:, 0:D + 1], zm[u][0:P, j, 0:D], zm[u][0:P, j, :],
                                                 start=False, stop=False, skip_group_check=True)

                    steps(pe, n_steps, groups, stage)

                @block.scalar
                def _(act):
                    def relu(out_, in_, bias=0.0):
                        return nc.scalar.activation(out_, in_, ACTF.Relu, bias=bias)

                    def stage(step, u, k, r):
                        s = walk[step]
                        P, J = shape(k, dense)
                        C = P * J
                        if s == 0:
                            act.wait_ge(S("x_transposed"), S.at("x_transposed", k + 1))
                            nc.scalar.copy(t0[u][:, 0:C], pA[u][:, 0:C]).then_inc(S("x_cols"), 1)
                        elif s == 1:
                            act.wait_ge(S("h1_product"), S.at("h1_product", k + 1))
                            relu(t1[u][:, 0:C], pB[u][:, 0:C], cb[:, c_b0:c_b0 + 1]).then_inc(S("h1_cols"), 1)
                        elif s == 2:
                            act.wait_ge(S("h2_product"), S.at("h2_product", k + 1))
                            relu(t2[u][:, 0:C], pA[u][:, 0:C], cb[:, c_b1:c_b1 + 1]).then_inc(S("h2_cols"), 1)
                        elif s == 5:
                            act.wait_ge(S("x1_transposed"), S.at("x1_transposed", k + 1))
                            nc.scalar.copy(t0[u][:, 0:C], pA[u][:, 0:C]).then_inc(S("x1_cols"), 1)
                        elif s == 6:
                            act.wait_ge(S("head_product0"), S.at("head_product0", k + 1))
                            relu(t1[u][:, 0:C], pB[u][:, 0:C], cb[:, c_gat:c_gat + 1]).then_inc(S("head_relu0"), 1)
                        elif s == 7:
                            act.wait_ge(S("head_product1"), S.at("head_product1", k + 1))
                            relu(t2[u][:, 0:C], pA[u][:, 0:C], cb[:,
                                 c_gat + 1:c_gat + 2]).then_inc(S("head_relu1"), 1)
                        elif s == 8 and dense:
                            scale_tile(act, u, k, r)
                        elif s == 13:
                            act.wait_ge(S("normed3"), S.at("normed3", k + 1))
                            for j in range(J):
                                ins = nc.scalar.activation(zm[u][0:P, j, 0:D], O[u][0:P, j, :], ACTF.Copy,
                                                           scale=nmask[0:P, bass.ds(4 * k + j, 1)])
                            ins.then_inc(S("z_masked"), 1)
                        elif s == 10:
                            act.wait_ge(S("x2_transposed"), S.at("x2_transposed", k + 1))
                            nc.scalar.copy(t0[u][:, 0:C], pA[u][:, 0:C]).then_inc(S("x2_cols"), 1)
                        elif s == 11 and not dense:
                            act.wait_ge(S("state_product"), S.at("state_product", k + 1))
                            if not fresh(k):
                                act.wait_ge(S(f"stored{u}"), S.at(f"stored{u}", r * per_store))
                            relu(Dn[u][:, :, :], nm(pB[u])).then_inc(S("state_rows"), 1)

                    steps(act, n_steps, groups, stage)

                @block.vector
                def _(dve):
                    def stage(step, u, k, r):
                        s = walk[step]
                        P, J = shape(k, dense)
                        if s == "rows of h1":
                            dve.wait_ge(S("h1_back"), S.at("h1_back", k + 1))
                            if not fresh(k):
                                dve.wait_ge(S(f"stored{u}"), S.at(f"stored{u}", r * per_store))
                            nc.vector.tensor_copy(O[u][:, :, :], nm(pB[u])).then_inc(S("h1_rows"), 1)
                        elif s == "rows of h2":
                            dve.wait_ge(S("h2_back"), S.at("h2_back", k + 1))
                            nc.vector.tensor_copy(G2[u][:, :, :], nm(pA[u])).then_inc(S("h2_rows"), 1)
                        elif s == 3:
                            dve.wait_ge(S("h3_product"), S.at("h3_product", k + 1))
                            arrived(dve, u, r)
                            nc.vector.scalar_tensor_tensor(nm(t3[u])[0:P, 0:J, :], G[u][0:P, 0:J, :], 2.0,
                                                           nm(pB[u])[0:P, 0:J, :], ALU.mult,
                                                           ALU.add).then_inc(S("residual1"), 1)
                            stats(dve, u, k, P, J, nm(t3[u]), 1)
                        elif s == 4:
                            normalise(dve, u, k, P, J, nm(t3[u]), nm(t4[u]), 1)
                        elif s == 8:
                            dve.wait_ge(S("gat_product"), S.at("gat_product", k + 1))
                            dve.wait_ge(S("normed1"), S.at("normed1", k + 1))
                            nc.vector.tensor_tensor(nm(t3[u])[0:P, 0:J, :], nm(t4[u])[0:P, 0:J, :],
                                                    nm(pB[u])[0:P, 0:J, :], ALU.add).then_inc(S("residual2"), 1)
                            stats(dve, u, k, P, J, nm(t3[u]), 2)
                        elif s == 9:
                            normalise(dve, u, k, P, J, nm(t3[u]), nm(t5[u]), 2)
                        elif s == (11 if dense else "residual"):
                            if dense:
                                dve.wait_ge(S("state_product"), S.at("state_product", k + 1))
                            else:
                                dve.wait_ge(S("state_rows"), S.at("state_rows", k + 1))
                            dve.wait_ge(S("x2_with_gains"), S.at("x2_with_gains", k + 1))
                            nc.vector.scalar_tensor_tensor(nm(t3[u])[0:P, 0:J, :],
                                                           nm(pB[u])[0:P, 0:J, :] if dense else Dn[u][:, :, :], 0.0,
                                                           nm(t2[u])[0:P, 0:J, :], ALU.max,
                                                           ALU.add).then_inc(S("residual3"), 1)
                            stats(dve, u, k, P, J, nm(t3[u]), 3)
                        elif s == 12:
                            if not fresh(k) and dense:
                                dve.wait_ge(S(f"stored{u}"), S.at(f"stored{u}", r * per_store))
                            normalise(dve, u, k, P, J, nm(t3[u]), O[u] if dense else nm(t5[u]), 3)

                    steps(dve, n_steps, groups, stage)

            names = ["x_transposed", "x_cols", "h1_product", "h1_cols", "h2_product", "h2_cols", "h3_product",
                     "x1_transposed", "x1_cols", "head_product0", "head_product1", "head_relu0", "head_relu1", "gat_product",
                     "x2_transposed", "x2_cols", "state_product"] + ln_signals(1, 2, 3) + ["x2_with_gains"]
            if dense:
                finish(groups, names + ["z_masked", "indices0", "looked_up", "scaled_rows"], loaded=16, stored=16,
                       gathered=48, kept=48)
            else:
                finish(groups, names + ["h1_back", "h2_back", "h1_rows", "h2_rows", "state_rows", "indices0",
                       "slots_in"], gathered=64,
                       scattered=64, kept=16, stored=per_store)

        sp_ = pool_ = None
        in_flight(7, 1, "G G2 Dn O t0 t1 t2 t3 t4 t5")
        chain(EG, False)

        with nc.Block() as block:
            @block.sync
            def _(sp):
                with nc.allow_non_contiguous_dma(reason="a node's slot for each row of a group"):
                    sp.dma_start(posN[:, 0:4 * NF].rearrange("p (g j) -> p g j", j=4),
                                 node_slot[0:NF * GC].rearrange("(g p j) -> p g j", p=128,
                                                                j=4)).then_inc(S("pos_n"), 16)
                    if R:
                        sp.dma_start(posN[0:TP, 4 * NF:4 * NF + TJ],
                                     node_slot[NF * GC:N].rearrange("(p j) -> p j", j=TJ)).then_inc(S("pos_n"), 16)

            @block.gpsimd
            def _(pool):
                nc.gpsimd.tensor_tensor(dinv[:, :], dinv[:, :], neg_half[:, 0:1].to_broadcast([128, ET]), ALU.pow)

            @block.vector
            def _(dve):
                nc.vector.memset(ystat[:, 0, :], 0.0)
                dve.wait_ge(S("pos_n"), 16 + 16 * (R > 0))
                nc.vector.tensor_scalar(nmask[:, 0:4 * NF], posN[:, 0:4 * NF], 0.0, eps1[:, 0:1], ALU.is_lt, ALU.mult)
                if R:
                    nc.vector.tensor_scalar(nmask[0:TP, 4 * NF:4 * NF + TJ], posN[0:TP, 4 * NF:4 * NF + TJ], 0.0,
                                            eps1[0:TP, 0:1], ALU.is_lt, ALU.mult)

        in_flight(7, 1, "G O zm attr own_x own_h look t0 t1 t2 t3 t4 t5")
        with nc.Block() as block:
            @block.tensor
            def _(pe):
                nc.tensor.matmul(pGram[:, 0:D + 1], ident[:, :], zeros[:, :], start=True, stop=False,
                                 skip_group_check=True)
        chain(NG, True)

        REST = ET - NG
        assert REST >= 0
        with nc.Block() as block:
            @block.gpsimd
            def _(pool):
                for i in range(REST):
                    u, r = i % U, i // U
                    if r:
                        keep_lookup(pool, u, NG + i - U, i - U, r - 1)
                    fetch_tile(pool, u, NG + i, i, r)
                for i in range(max(0, REST - U), REST):
                    keep_lookup(pool, i % U, NG + i, i, i // U)

            @block.scalar
            def _(act):
                for i in range(REST):
                    scale_tile(act, i % U, NG + i, i // U)

            @block.sync
            def _(sp):
                for i in range(REST):
                    store_tile(sp, i % U, NG + i, i)
                for u in range(min(U, REST)):
                    sp.wait_ge(S(f"kept{u}"), S.at(f"kept{u}", 48 * len(range(u, REST, U))))

            @block.tensor
            def _(pe):
                nc.tensor.matmul(pGram[:, 0:D + 1], ident[:, :], zeros[:, :], start=False, stop=True,
                                 skip_group_check=True)
        finish(REST, ["indices0", "looked_up", "scaled_rows"], gathered=48, kept=48)

        with nc.Block() as block:
            @block.vector
            def _(dve):
                ch = Chain(dve, "dve_setup")
                nc.vector.tensor_scalar(w0[:, :], slot_f[:, :], float(EP), None, ALU.add)
                ch.after(nc.vector.tensor_scalar(w1[:, :], pos[:, :], 0.0, None, ALU.is_ge))
                ch.after(nc.vector.tensor_tensor(pos[:, :], pos[:, :], w0[:, :], ALU.subtract))
                ch.after(nc.vector.tensor_tensor(pos[:, :], pos[:, :], w1[:, :], ALU.mult))
                ch.after(nc.vector.tensor_tensor(idx[:, :], pos[:, :], w0[:, :], ALU.add))
                nc.vector.tensor_copy(gram[:, :], pGram[:, 0:D + 1])
                ch.close()

        def gcn_layer(i):
            final = i == 2
            W = (W0, W1, W2)[i]
            row_b = (rowb0[:, :], rowb1[:, :], rows[:, row_b2, :])[i]
            per_load = 48 if final else 32
            n_steps = 3 if final else 2

            with nc.Block() as block:
                @block.sync
                def _(sp):
                    def load(u, k, r):
                        if not fresh(k) and final:
                            sp.wait_ge(S("residual1"), S.at("residual1", k + 1 - U))
                        if not fresh(k) and not final:
                            sp.wait_ge(S("loop_added"), S.at("loop_added", k + 1 - U))
                        sp.dma_start(Dn[u][:, :, :], slot_rows(gcn_table[i], k)).then_inc(S(f"loaded{u}"), 16)
                        sp.dma_start(keep[u][:, :], keep_cols(k)).then_inc(S(f"loaded{u}"), 16)
                        if final:
                            sp.dma_start(G2[u][:, :, :], slot_rows(x0_slots, k)).then_inc(S(f"loaded{u}"), 16)

                    def stage(s, u, k, r):
                        if s == n_steps - 1:
                            sp.wait_ge(S("normed1" if final else "scaled_rows"),
                                       S.at("normed1" if final else "scaled_rows", k + 1))
                            sp.dma_start(slot_rows(gat_table if final else gcn_table[i + 1], k),
                                         O[u][:, :, :]).then_inc(S(f"stored{u}"), 16)

                    steps(sp, n_steps, EG, stage, (1 if final else 0, load))
                    for u in range(min(U, EG)):
                        sp.wait_ge(S(f"stored{u}"), S.at(f"stored{u}", 16 * len(range(u, EG, U))))

                @block.gpsimd
                def _(pool):
                    def load(u, k, r):
                        if not fresh(k):
                            pool.wait_ge(S("columns_ready"), S.at("columns_ready", k + 1 - U))
                        gather(pool, u, k, idx, gcn_table[i], G, 0)

                    def stage(s, u, k, r):
                        if final and s == 1:
                            inv_std(pool, u, k, 128, 4, 1, with_shift=True)

                    steps(pool, n_steps, EG, stage, (0, load))

                @block.tensor
                def _(pe):
                    def stage(s, u, k, r):
                        if s == 0:
                            pe.wait_ge(S(f"gathered{u}"), S.at(f"gathered{u}", (r + 1) * 64))
                            pe.wait_ge(S(f"loaded{u}"), S.at(f"loaded{u}", (r + 1) * per_load))
                            if not fresh(k):
                                pe.wait_ge(S("biased_rows"), S.at("biased_rows", k + 1 - U))
                            transposes(G[u], pA[u])
                            transposes(Dn[u], pB[u]).then_inc(S("columns_ready"), 1)
                        elif s == 1:
                            pe.wait_ge(S("loop_added"), S.at("loop_added", k + 1))
                            to_node_major(pA[u], [(t0[u], W[:, :])]).then_inc(S("message_product"), 1)

                    steps(pe, n_steps, EG, stage)

                @block.vector
                def _(dve):
                    def stage(s, u, k, r):
                        if s == 0:
                            dve.wait_ge(S("columns_ready"), S.at("columns_ready", k + 1))
                            dve.wait_ge(S(f"loaded{u}"), S.at(f"loaded{u}", (r + 1) * per_load))
                            dve.wait_ge(S("segments_summed"), S.at("segments_summed", k))
                            scan(A[u], keep[u][:, :], pA[u][:, :], A[u - 1], ALU.mult,
                                 ALU.add).then_inc(S("segments_summed"), 1)
                            dve.wait_ge(S("segments_summed"), S.at("segments_summed", k + 1))
                            nc.vector.tensor_tensor(t0[u][:, :], A[u][:, 1:GC + 1], pB[u][:, :],
                                                    ALU.add).then_inc(S("loop_added"), 1)
                        elif s == 1:
                            dve.wait_ge(S("message_product"), S.at("message_product", k + 1))
                            if not final and not fresh(k):
                                dve.wait_ge(S("scaled_rows"), S.at("scaled_rows", k + 1 - U))
                            for j in range(4):
                                ins = nc.vector.scalar_tensor_tensor(
                                    nm(t1[u])[:, j, :], pA[u][:, j * D:(j + 1) * D], dinv[:, bass.ds(4 * k + j, 1)],
                                    row_b, ALU.mult, ALU.add)
                            ins.then_inc(S("biased_rows"), 1)
                            if final:
                                dve.wait_ge(S("biased_rows"), S.at("biased_rows", k + 1))
                                if not fresh(k):
                                    dve.wait_ge(S("normed1"), S.at("normed1", k + 1 - U))
                                nc.vector.scalar_tensor_tensor(nm(t2[u]), G2[u][:, :, :], 2.0, nm(t1[u]), ALU.mult,
                                                               ALU.add).then_inc(S("residual1"), 1)
                                stats(dve, u, k, 128, 4, nm(t2[u]), 1, negated=True)

                    steps(dve, n_steps, EG, stage)

                @block.scalar
                def _(act):
                    def stage(s, u, k, r):
                        if s == 2:
                            if not fresh(k):
                                act.wait_ge(S(f"stored{u}"), S.at(f"stored{u}", r * 16))
                            normalise_on_act(act, u, k, 128, 4, nm(t2[u]), O[u], 1)
                        elif s == 1 and not final:
                            act.wait_ge(S("biased_rows"), S.at("biased_rows", k + 1))
                            if not fresh(k):
                                act.wait_ge(S(f"stored{u}"), S.at(f"stored{u}", r * 16))
                            for j in range(4):
                                ins = nc.scalar.activation(O[u][:, j, :], nm(t1[u])[:, j, :], ACTF.Relu,
                                                           scale=dinv[:, bass.ds(4 * k + j, 1)])
                            ins.then_inc(S("scaled_rows"), 1)

                    steps(act, n_steps, EG, stage)

            finish(EG, ["columns_ready", "segments_summed", "loop_added", "message_product", "biased_rows",
                   "indices0"] + (ln_signals(1) + ["inv_std_alone"] if final else ["scaled_rows"]),
                   gathered=64, loaded=per_load, stored=16)

        in_flight(4, 2, "G G2 Dn O keep A t0 t1 t2")
        for i in range(3):
            gcn_layer(i)

        in_flight(4, 2, "G G2 Dn O keep soft A Mx Sc0 Sc1 t0 t1 t2 t3 t4 t5 t6 t7")

        walk = [0, 1, 2, 3, None, 4, 5, 6, 7, 8, 9, None]
        with nc.Block() as block:
            @block.sync
            def _(sp):
                def load(u, k, r):
                    if not fresh(k):
                        sp.wait_ge(S("residual2"), S.at("residual2", k + 1 - U))
                    sp.dma_start(keep[u][:, :], keep_cols(k)).then_inc(S(f"loaded{u}"), 16)

                def stage(step, u, k, r):
                    s = walk[step]
                    if s == 7:
                        sp.wait_ge(S("normed2"), S.at("normed2", k + 1))
                        sp.dma_start(slot_rows(x2_slots, k), O[u][:, :, :]).then_inc(S(f"stored{u}"), 16)
                    elif s == 9:
                        sp.wait_ge(S("state_rows"), S.at("state_rows", k + 1))
                        sp.dma_start(slot_rows(mpn_table[0], k), nm(t7[u])).then_inc(S(f"stored{u}"), 16)

                steps(sp, len(walk), EG, stage, (walk.index(6), load))
                for u in range(min(U, EG)):
                    sp.wait_ge(S(f"stored{u}"), S.at(f"stored{u}", 32 * len(range(u, EG, U))))

            @block.gpsimd
            def _(pool):
                def load_source(u, k, r):
                    if not fresh(k):
                        pool.wait_ge(S("x1_transposed"), S.at("x1_transposed", k + 1 - U))
                    gather(pool, u, k, idx, gat_table, G, 0)

                def load_own(u, k, r):
                    if not fresh(k):
                        pool.wait_ge(S("residual2"), S.at("residual2", k + 1 - U))
                    gather(pool, u, k, idx_own, gat_table, Dn, 4)

                def stage(step, u, k, r):
                    s = walk[step]
                    if s == 2:
                        pool.wait_ge(S("maxima"), S.at("maxima", k + 1))
                        nc.gpsimd.tensor_tensor(soft[u][:, 2, :], t3[u][:, :], Mx[u][:, 1:GC + 1],
                                                ALU.subtract).then_inc(S("loop_exponents"), 1)
                    elif s == 4 or s == 5:
                        c = s - 4
                        pool.wait_ge(S(f"numerator{c}"), S.at(f"numerator{c}", k + 1))
                        nc.gpsimd.tensor_tensor((t4, t3)[c][u][:, :], t2[u][:, :], t5[u][:, :],
                                                ALU.mult).then_inc(S(f"head_mean{c}"), 1)
                    elif s == 6:
                        inv_std(pool, u, k, 128, 4, 2, with_shift=True)

                steps(pool, len(walk), EG, stage, (0, load_source), (walk.index(6), load_own))

            @block.tensor
            def _(pe):
                def stage(step, u, k, r):
                    s = walk[step]
                    if s == 0:
                        pe.wait_ge(S(f"gathered{u}"), S.at(f"gathered{u}", (r + 1) * 128))
                        if not fresh(k):
                            pe.wait_ge(S("state_rows"), S.at("state_rows", k + 1 - U))
                        transposes(G[u], pA[u])
                        transposes(Dn[u], pB[u]).then_inc(S("x1_transposed"), 1)
                    elif s == 1:
                        pe.wait_ge(S("x1_cols"), S.at("x1_cols", k + 1))
                        feature_major(pA[u], [(t0[u], attS[:, :]), (t1[u], attD[:, :])])
                        feature_major(pB[u], [(t1[u], attSD[:, :])]).then_inc(S("scores_product"), 1)
                    elif s == 3 or s == 5:
                        c = s // 2 - 1
                        pe.wait_ge(S("weighted0" if c else "scores"), S.at("weighted0" if c else "scores", k + 1))
                        feature_major(pA[u], [(t0[u], Wg[:, c, :])])
                        feature_major(pB[u], [(t1[u], Wg[:, c, :])]).then_inc(S(f"weighted_product{c}"), 1)
                    elif s == 6:
                        pe.wait_ge(S("head_relu1"), S.at("head_relu1", k + 1))
                        to_node_major(pA[u], [(G2[u][:, :, :].rearrange("p j d -> p (j d)"), fcw[:, 0, :]),
                                              (t6[u], fcw[:, 1, :])], row=slot_fc).then_inc(S("gat_product"), 1)
                    elif s == 8:
                        pe.wait_ge(S("normed2"), S.at("normed2", k + 1))
                        transposes(O[u], pB[u]).then_inc(S("x2_transposed"), 1)
                    elif s == 9:
                        pe.wait_ge(S("x2_cols"), S.at("x2_cols", k + 1))
                        to_node_major(pA[u], [(t0[u], Wi[:, :])], row=row_bi).then_inc(S("state_product"), 1)

                steps(pe, len(walk), EG, stage)

            @block.scalar
            def _(act):
                def stage(step, u, k, r):
                    s = walk[step]
                    if s == 0:
                        act.wait_ge(S("x1_transposed"), S.at("x1_transposed", k + 1))
                        nc.scalar.copy(t0[u][:, :], pA[u][:, :])
                        nc.scalar.copy(t1[u][:, :], pB[u][:, :]).then_inc(S("x1_cols"), 1)
                    elif s == 1:
                        act.wait_ge(S("scores_product"), S.at("scores_product", k + 1))
                        nc.scalar.copy(soft[u][:, 0, :], pA[u][:, :])
                        nc.scalar.copy(soft[u][:, 1, :], pB[u][:, :])
                        act.wait_ge(S(f"loaded{u}"), S.at(f"loaded{u}", (r + 1) * 16))
                        nc.scalar.activation(t5[u][:, :], keep[u][:, :], ACTF.Identity, bias=neg_far[:, 0:1],
                                             scale=FAR).then_inc(S("scores"), 1)
                    elif s == 2:
                        act.wait_ge(S("exponents"), S.at("exponents", k + 1))
                        act.wait_ge(S("loop_exponents"), S.at("loop_exponents", k + 1))
                        nc.scalar.activation(soft[u][:, :, :], soft[u][:, :, :],
                                             ACTF.Exp).then_inc(S("exponentials"), 1)
                    elif s == 4:
                        act.wait_ge(S("head_mean0"), S.at("head_mean0", k + 1))
                        nc.scalar.activation(G2[u][:, :, :].rearrange("p j d -> p (j d)"), t4[u][:, :], ACTF.Relu,
                                             bias=cb[:, c_gat:c_gat + 1]).then_inc(S("head_relu0"), 1)
                    elif s == 5:
                        act.wait_ge(S("head_mean1"), S.at("head_mean1", k + 1))
                        nc.scalar.activation(t6[u][:, :], t3[u][:, :], ACTF.Relu,
                                             bias=cb[:, c_gat + 1:c_gat + 2]).then_inc(S("head_relu1"), 1)
                    elif s == 7:
                        if not fresh(k):
                            act.wait_ge(S(f"stored{u}"), S.at(f"stored{u}", r * 32))
                        normalise_on_act(act, u, k, 128, 4, nm(t2[u]), O[u], 2)
                    elif s == 8:
                        act.wait_ge(S("x2_transposed"), S.at("x2_transposed", k + 1))
                        nc.scalar.copy(t0[u][:, :], pB[u][:, :]).then_inc(S("x2_cols"), 1)
                    elif s == 9:
                        act.wait_ge(S("state_product"), S.at("state_product", k + 1))
                        if not fresh(k):
                            act.wait_ge(S(f"stored{u}"), S.at(f"stored{u}", r * 32))
                        nc.scalar.activation(t7[u][:, :], pA[u][:, :], ACTF.Relu).then_inc(S("state_rows"), 1)

                steps(act, len(walk), EG, stage)

            @block.vector
            def _(dve):
                def stt(out_, in0, scalar, in1, op0, op1):
                    return nc.vector.scalar_tensor_tensor(out_, in0, scalar, in1, op0, op1)

                def tt(out_, in0, in1, op):
                    return nc.vector.tensor_tensor(out_, in0, in1, op)

                def stage(step, u, k, r):
                    s = walk[step]
                    decay, p_edge, p_loop = soft[u][:, 0, :], soft[u][:, 1, :], soft[u][:, 2, :]
                    m_now, m_before = Mx[u][:, 1:GC + 1], Mx[u][:, 0:GC]
                    if s == 2:
                        dve.wait_ge(S("scores"), S.at("scores", k + 1))
                        stt(t2[u][:, :], soft[u][:, 0, :], SLOPE, soft[u][:, 0, :], ALU.mult, ALU.max)
                        stt(t3[u][:, :], soft[u][:, 1, :], SLOPE, soft[u][:, 1, :], ALU.mult,
                            ALU.max).then_inc(S("leaky_scores"), 1)
                        dve.wait_ge(S("leaky_scores"), S.at("leaky_scores", k + 1))
                        tt(t4[u][:, :], t2[u][:, :], t3[u][:, :], ALU.max).then_inc(S("scores_with_loop"), 1)
                        dve.wait_ge(S("scores_with_loop"), S.at("scores_with_loop", k + 1))
                        dve.wait_ge(S("maxima"), S.at("maxima", k))
                        nc.vector.tensor_copy(Mx[u][:, 0:1], Mx[u - 1][:, GC:GC + 1])
                        scan(Mx[u], t5[u][:, :], t4[u][:, :], Mx[u - 1], ALU.add, ALU.max).then_inc(S("maxima"), 1)
                        dve.wait_ge(S("maxima"), S.at("maxima", k + 1))
                        tt(soft[u][:, 1, :], t2[u][:, :], m_now, ALU.subtract)
                        tt(soft[u][:, 0, :], m_before, t5[u][:, :], ALU.add).then_inc(S("exponents_part"), 1)
                        dve.wait_ge(S("exponents_part"), S.at("exponents_part", k + 1))
                        tt(soft[u][:, 0, :], soft[u][:, 0, :], m_now, ALU.subtract).then_inc(S("exponents"), 1)
                    elif s == 3:
                        dve.wait_ge(S("exponentials"), S.at("exponentials", k + 1))
                        dve.wait_ge(S("segments_summed"), S.at("segments_summed", k))
                        scan(A[u], decay, p_edge, A[u - 1], ALU.mult, ALU.add).then_inc(S("segments_summed"), 1)
                        dve.wait_ge(S("segments_summed"), S.at("segments_summed", k + 1))
                        tt(t5[u][:, :], A[u][:, 1:GC + 1], p_loop, ALU.add).then_inc(S("denominator"), 1)
                        dve.wait_ge(S("denominator"), S.at("denominator", k + 1))
                        nc.vector.reciprocal(t5[u][:, :], t5[u][:, :]).then_inc(S("inv_denominator"), 1)
                    elif s == 4 or s == 5:
                        c = s - 4
                        Sc = (Sc0, Sc1)[c]
                        dve.wait_ge(S(f"weighted_product{c}"), S.at(f"weighted_product{c}", k + 1))
                        dve.wait_ge(S(f"head_mean0" if c else "inv_denominator"),
                                    S.at(f"head_mean0" if c else "inv_denominator", k + 1))
                        tt(t2[u][:, :], p_edge, pA[u][:, :], ALU.mult)
                        tt(t3[u][:, :], p_loop, pB[u][:, :], ALU.mult).then_inc(S(f"weighted{c}"), 1)
                        dve.wait_ge(S(f"weighted{c}"), S.at(f"weighted{c}", k + 1))
                        dve.wait_ge(S(f"weighted_sums{c}"), S.at(f"weighted_sums{c}", k))
                        scan(Sc[u], decay, t2[u][:, :], Sc[u - 1], ALU.mult,
                             ALU.add).then_inc(S(f"weighted_sums{c}"), 1)
                        dve.wait_ge(S(f"weighted_sums{c}"), S.at(f"weighted_sums{c}", k + 1))
                        tt(t2[u][:, :], Sc[u][:, 1:GC + 1], t3[u][:, :], ALU.add).then_inc(S(f"numerator{c}"), 1)
                    elif s == 6:
                        dve.wait_ge(S("gat_product"), S.at("gat_product", k + 1))
                        tt(nm(t2[u]), Dn[u][:, :, :], nm(pA[u]), ALU.add).then_inc(S("residual2"), 1)
                        stats(dve, u, k, 128, 4, nm(t2[u]), 2, negated=True)

                steps(dve, len(walk), EG, stage)
        finish(EG, ["x1_transposed", "x1_cols", "scores_product", "scores", "leaky_scores", "scores_with_loop",
               "maxima", "exponents_part", "exponents", "exponentials", "segments_summed",
                    "denominator", "inv_denominator", "weighted_product0", "weighted_product1", "weighted0", "weighted1", "weighted_sums0", "weighted_sums1", "numerator0", "numerator1",
                    "head_mean0", "head_mean1", "head_relu0", "head_relu1", "gat_product", "x2_transposed", "x2_cols", "state_product", "state_rows", "indices0", "indices4"]
               + ln_signals(2) + ["inv_std_alone", "loop_exponents"], gathered=128, loaded=16, stored=32)
        S.retire(["scores_product", "scores", "leaky_scores", "scores_with_loop", "maxima", "exponents_part",
                 "exponents",
                  "exponentials", "denominator", "inv_denominator", "weighted_product0", "weighted_product1", "weighted0", "weighted1",
                  "weighted_sums0", "weighted_sums1", "numerator0", "numerator1", "head_mean0", "head_mean1"])

        def mpn_round(i):
            final = i == ROUNDS - 1
            per_load = 48 if final else 32
            n_steps = 5 if final else 3

            with nc.Block() as block:
                @block.sync
                def _(sp):
                    def load(u, k, r):
                        if not fresh(k):
                            sp.wait_ge(S("state_shifted"), S.at("state_shifted", k + 1 - U))
                        sp.dma_start(Dn[u][:, :, :], slot_rows(mpn_table[i % 2], k)).then_inc(S(f"loaded{u}"), 16)
                        sp.dma_start(keep[u][:, :], keep_cols(k)).then_inc(S(f"loaded{u}"), 16)
                        if final:
                            sp.dma_start(G2[u][:, :, :], slot_rows(x2_slots, k)).then_inc(S(f"loaded{u}"), 16)

                    def stage(s, u, k, r):
                        if s == n_steps - 1:
                            sp.wait_ge(S("normed3" if final else "state_updated"),
                                       S.at("normed3" if final else "state_updated", k + 1))
                            sp.dma_start(slot_rows(x3_table if final else mpn_table[(i + 1) % 2], k),
                                         O[u][:, :, :]).then_inc(S(f"stored{u}"), 16)

                    steps(sp, n_steps, EG, stage, (1, load))
                    for u in range(min(U, EG)):
                        sp.wait_ge(S(f"stored{u}"), S.at(f"stored{u}", 16 * len(range(u, EG, U))))

                @block.gpsimd
                def _(pool):
                    def load(u, k, r):
                        if not fresh(k):
                            pool.wait_ge(S("cols_psum"), S.at("cols_psum", k + 1 - U))
                        gather(pool, u, k, idx, mpn_table[i % 2], G, 0)

                    def stage(s, u, k, r):
                        if s == 3 and final:
                            inv_std(pool, u, k, 128, 4, 3, with_shift=True)

                    steps(pool, n_steps, EG, stage, (0, load))

                @block.tensor
                def _(pe):
                    def stage(s, u, k, r):
                        if s == 0:
                            pe.wait_ge(S(f"gathered{u}"), S.at(f"gathered{u}", (r + 1) * 64))
                            if not fresh(k):
                                pe.wait_ge(S("update_rows"), S.at("update_rows", k + 1 - U))
                            transposes(G[u], pA[u]).then_inc(S("cols_psum"), 1)
                        elif s == 1:
                            pe.wait_ge(S("cols_copied"), S.at("cols_copied", k + 1))
                            feature_major(pB[u], [(t0[u], Wm[:, i, :])]).then_inc(S("message_product"), 1)
                        elif s == 2:
                            pe.wait_ge(S("segments_summed"), S.at("segments_summed", k + 1))
                            to_node_major(pA[u], [(A[u][:, 1:GC + 1], Wu[:, i, :])],
                                          row=row_bu + i).then_inc(S("update_product"), 1)

                    steps(pe, n_steps, EG, stage)

                @block.scalar
                def _(act):
                    def stage(s, u, k, r):
                        if s == 0:
                            act.wait_ge(S("cols_psum"), S.at("cols_psum", k + 1))
                            nc.scalar.copy(t0[u][:, :], pA[u][:, :]).then_inc(S("cols_copied"), 1)
                        elif s == 1:
                            act.wait_ge(S("message_product"), S.at("message_product", k + 1))
                            if not fresh(k):
                                act.wait_ge(S("segments_summed"), S.at("segments_summed", k + 1 - U))
                            nc.scalar.activation(t1[u][:, :], pB[u][:, :], ACTF.Relu,
                                                 bias=cb[:, c_bm + i:c_bm + i + 1]).then_inc(S("messages"), 1)
                        elif s == 2:
                            act.wait_ge(S("update_product"), S.at("update_product", k + 1))
                            if not fresh(k):
                                act.wait_ge(S("state_updated"), S.at("state_updated", k + 1 - U))
                            nc.scalar.activation(t2[u][:, :], pA[u][:, :], ACTF.Relu).then_inc(S("update_rows"), 1)
                        elif s == 4:
                            if not fresh(k):
                                act.wait_ge(S(f"stored{u}"), S.at(f"stored{u}", r * 16))
                            normalise_on_act(act, u, k, 128, 4, nm(t5[u]), O[u], 3)

                    steps(act, n_steps, EG, stage)

                @block.vector
                def _(dve):
                    def stage(s, u, k, r):
                        if s == 1:
                            dve.wait_ge(S("messages"), S.at("messages", k + 1))
                            dve.wait_ge(S(f"loaded{u}"), S.at(f"loaded{u}", (r + 1) * per_load))
                            dve.wait_ge(S("segments_summed"), S.at("segments_summed", k))
                            scan(A[u], keep[u][:, :], t1[u][:, :], A[u - 1], ALU.mult,
                                 ALU.add).then_inc(S("segments_summed"), 1)
                            ins = nc.vector.tensor_tensor(nm(t3[u]), Dn[u][:, :, :],
                                                          cu[:, i, :].unsqueeze(1).to_broadcast([128, 4, D]),
                                                          ALU.subtract)
                            if final:
                                ins = nc.vector.tensor_tensor(nm(t4[u]), G2[u][:, :, :],
                                                              c_all[:, :].unsqueeze(1).to_broadcast([128, 4, D]),
                                                                      ALU.add)
                            ins.then_inc(S("state_shifted"), 1)
                        elif s == (3 if final else 2):
                            dve.wait_ge(S("update_rows"), S.at("update_rows", k + 1))
                            dve.wait_ge(S("state_shifted"), S.at("state_shifted", k + 1))
                            if final:
                                nc.vector.tensor_tensor(t5[u][:, :], t2[u][:, :], t3[u][:, :],
                                                        ALU.add).then_inc(S("state_updated"), 1)
                                dve.wait_ge(S("state_updated"), S.at("state_updated", k + 1))
                                nc.vector.tensor_tensor(t5[u][:, :], t5[u][:, :], t4[u][:, :],
                                                        ALU.add).then_inc(S("residual3"), 1)
                                stats(dve, u, k, 128, 4, nm(t5[u]), 3, negated=True)
                            else:
                                if not fresh(k):
                                    dve.wait_ge(S(f"stored{u}"), S.at(f"stored{u}", r * 16))
                                nc.vector.tensor_tensor(O[u][:, :, :], nm(t2[u]), nm(t3[u]),
                                                        ALU.add).then_inc(S("state_updated"), 1)

                    steps(dve, n_steps, EG, stage)
            finish(EG, ["cols_psum", "cols_copied", "message_product", "messages", "segments_summed",
                   "update_product", "update_rows", "state_updated", "state_shifted", "indices0"]
                   + (ln_signals(3) + ["inv_std_alone"] if final else []), gathered=64, loaded=per_load, stored=16)

        in_flight(6, 1, "G G2 Dn O keep A t0 t1 t2 t3 t4 t5")
        for i in range(ROUNDS):
            mpn_round(i)

        in_flight(6, 1, "G G2 Dn keep A zm t0 t1 t2")
        with nc.Block() as block:
            @block.tensor
            def _(pe):
                nc.tensor.matmul(pGram[:, 0:D + 1], ident[:, :], gram[:, :], start=True, stop=False,
                                 skip_group_check=True)

        with nc.Block() as block:
            @block.sync
            def _(sp):
                def load(u, k, r):
                    if not fresh(k):
                        sp.wait_ge(S("z_rows"), S.at("z_rows", k + 1 - U))
                    sp.dma_start(Dn[u][:, :, :], slot_rows(x3_table, k)).then_inc(S(f"loaded{u}"), 16)
                    sp.dma_start(keep[u][:, :], keep_cols(k)).then_inc(S(f"loaded{u}"), 16)
                    sp.dma_start(G2[u][:, :, :], slot_rows(attr_slots, k)).then_inc(S(f"loaded{u}"), 16)

                def stage(s, u, k, r):
                    if s == 3:
                        sp.wait_ge(S("z_masked"), S.at("z_masked", k + 1))
                        sp.dma_start(slot_rows(z_slots, k), zm[u][:, :, 0:D]).then_inc(S(f"stored{u}"), 16)

                steps(sp, 5, EG, stage, (2, load))
                for u in range(min(U, EG)):
                    sp.wait_ge(S(f"stored{u}"), S.at(f"stored{u}", 16 * len(range(u, EG, U))))

            @block.gpsimd
            def _(pool):
                def load(u, k, r):
                    if not fresh(k):
                        pool.wait_ge(S("edge_sums"), S.at("edge_sums", k + 1 - U))
                    gather(pool, u, k, idx, x3_table, G, 0)

                steps(pool, 5, EG, None, (0, load))

            @block.tensor
            def _(pe):
                def stage(s, u, k, r):
                    if s == 1:
                        pe.wait_ge(S("messages"), S.at("messages", k + 1))
                        transposes(nm(t1[u]), pA[u]).then_inc(S("cols_psum"), 1)
                    elif s == 2:
                        pe.wait_ge(S("segments_summed"), S.at("segments_summed", k + 1))
                        back_transposes(A[u][:, 1:GC + 1], pB[u]).then_inc(S("message_product"), 1)
                    elif s == 4:
                        pe.wait_ge(S("z_masked"), S.at("z_masked", k + 1))
                        for j in range(4):
                            ins = nc.tensor.matmul(pGram[:, 0:D + 1], zm[u][:, j, 0:D], zm[u][:, j, :], start=False,
                                                   stop=False, skip_group_check=True)
                        ins.then_inc(S("gram_added"), 1)

                steps(pe, 5, EG, stage)
                nc.tensor.matmul(pGram[:, 0:D + 1], ident[:, :], zeros[:, :], start=False, stop=True,
                                 skip_group_check=True)

            @block.scalar
            def _(act):
                def stage(s, u, k, r):
                    if s == 0:
                        act.wait_ge(S("edge_sums"), S.at("edge_sums", k + 1))
                        if not fresh(k):
                            act.wait_ge(S("cols_psum"), S.at("cols_psum", k + 1 - U))
                        nc.scalar.activation(t1[u][:, :], t0[u][:, :], ACTF.Relu).then_inc(S("messages"), 1)
                    elif s == 2:
                        act.wait_ge(S("z_rows"), S.at("z_rows", k + 1))
                        if not fresh(k):
                            act.wait_ge(S(f"stored{u}"), S.at(f"stored{u}", r * 16))
                            act.wait_ge(S("gram_added"), S.at("gram_added", k + 1 - U))
                        for j in range(4):
                            ins = nc.scalar.activation(zm[u][:, j, 0:D], nm(t2[u])[:, j, :], ACTF.Copy,
                                                       scale=last[:, bass.ds(4 * k + j, 1)])
                        ins.then_inc(S("z_masked"), 1)

                steps(act, 5, EG, stage)

            @block.vector
            def _(dve):
                def stage(s, u, k, r):
                    if s == 0:
                        dve.wait_ge(S(f"loaded{u}"), S.at(f"loaded{u}", (r + 1) * 48))
                        dve.wait_ge(S(f"gathered{u}"), S.at(f"gathered{u}", (r + 1) * 64))
                        if not fresh(k):
                            dve.wait_ge(S("messages"), S.at("messages", k + 1 - U))
                        nc.vector.tensor_tensor(nm(t0[u]), G[u][:, :, :], G2[u][:, :, :],
                                                ALU.add).then_inc(S("edge_sums"), 1)
                    elif s == 1:
                        dve.wait_ge(S("cols_psum"), S.at("cols_psum", k + 1))
                        dve.wait_ge(S("segments_summed"), S.at("segments_summed", k))
                        scan(A[u], keep[u][:, :], pA[u][:, :], A[u - 1], ALU.mult,
                             ALU.add).then_inc(S("segments_summed"), 1)
                    elif s == 2:
                        dve.wait_ge(S("message_product"), S.at("message_product", k + 1))
                        if not fresh(k):
                            dve.wait_ge(S("z_masked"), S.at("z_masked", k + 1 - U))
                        nc.vector.scalar_tensor_tensor(nm(t2[u]), Dn[u][:, :, :], eps1[:, 0:1], nm(pB[u]), ALU.mult,
                                                       ALU.add).then_inc(S("z_rows"), 1)

                steps(dve, 5, EG, stage)
        finish(EG, ["edge_sums", "messages", "cols_psum", "segments_summed", "message_product", "z_rows",
               "z_masked", "gram_added", "indices0"], gathered=64,
               loaded=48, stored=16)

        with nc.Block() as block:
            @block.gpsimd
            def _(pool):
                nc.gpsimd.memset(small[:, 14:16], -0.5).then_inc(S("bn1_half"), 1)
                pool.wait_ge(S("bn1_half"), S.at("bn1_half", 1))
                pool.wait_ge(S("bn1_var"), S.at("bn1_var", 1))
                nc.gpsimd.tensor_tensor(small[:, 12:14], small[:, 8:10], small[:, 14:16],
                                        ALU.pow).then_inc(S("bn1_rstd"), 1)

            @block.vector
            def _(dve):
                ch = Chain(dve, "dve_setup")
                nc.vector.tensor_scalar(gram[:, :], pGram[:, 0:D + 1], 1.0 / N, None,
                                        ALU.mult).then_inc(S("gram_in"), 1)
                dve.wait_ge(S("mrow_p"), S.at("mrow_p", 1))
                nc.vector.tensor_copy(mrow[:, :], pMisc[0:1, 0:D]).then_inc(S("mrow_in"), 1)
                dve.wait_ge(S("outer_p"), S.at("outer_p", 1))
                nc.vector.tensor_tensor(gram[:, 0:D], gram[:, 0:D], pMisc[:, 128:256],
                                        ALU.subtract).then_inc(S("cov"), 1)
                dve.wait_ge(S("cw_p"), S.at("cw_p", 1))
                nc.vector.tensor_tensor(prod[:, :, :], V1[:, :, :],
                                        pMisc[:, 256:512].rearrange("p (c o) -> p c o", c=2),
                                                                    ALU.mult).then_inc(S("cwp"), 1)
                dve.wait_ge(S("mv_p"), S.at("mv_p", 1))
                ch.after(nc.vector.tensor_copy(small[:, 0:4], pA[0][:, 0:4]))
                nc.vector.tensor_scalar(small[:, 8:10], small[:, 2:4], BN_EPS, None,
                                        ALU.add).then_inc(S("bn1_var"), 1)
                dve.wait_ge(S("bn1_rstd"), S.at("bn1_rstd", 1))
                ch.after(nc.vector.tensor_tensor(bn[:, b_s1:b_s1 + 2], bn[:, b_g1:b_g1 + 2], small[:, 12:14],
                         ALU.mult))
                ch.after(nc.vector.tensor_tensor(small[:, 4:6], small[:, 0:2], bn[:, b_s1:b_s1 + 2], ALU.mult))
                ch.after(nc.vector.tensor_tensor(bn[:, b_t1:b_t1 + 2], bn[:, b_b1:b_b1 + 2], small[:, 4:6],
                         ALU.subtract))
                nc.vector.tensor_scalar(small[:, 6:8], bn[:, b_t1:b_t1 + 2], 0.0, None, ALU.max).then_inc(S("r0"), 1)
                dve.wait_ge(S("y0_p"), S.at("y0_p", 1))
                ch.after(nc.vector.tensor_copy(small[:, 16:17], pMisc[:, 0:1]))
                ch.close()

            @block.tensor
            def _(pe):
                pe.wait_ge(S("gram_in"), S.at("gram_in", 1))
                nc.tensor.transpose(pMisc[0:1, 0:D], gram[:, D:D + 1], ident[:, :]).then_inc(S("mrow_p"), 1)
                pe.wait_ge(S("mrow_in"), S.at("mrow_in", 1))
                nc.tensor.matmul(pMisc[:, 128:256], mrow[:, :], mrow[:, :], start=True,
                                 stop=True).then_inc(S("outer_p"), 1)
                pe.wait_ge(S("cov"), S.at("cov", 1))
                nc.tensor.matmul(pMisc[:, 256:512], gram[:, 0:D], V1[:, :, :], start=True,
                                 stop=True).then_inc(S("cw_p"), 1)
                pe.wait_ge(S("cwp"), S.at("cwp", 1))
                for c in range(2):
                    nc.tensor.matmul(pA[0][:, c:c + 1], V1[:, c, :], gram[:, D:D + 1], start=True, stop=True)
                for c in range(2):
                    ins = nc.tensor.matmul(pA[0][:, 2 + c:3 + c], prod[:, c, :], onesc[:, :], start=True, stop=True)
                ins.then_inc(S("mv_p"), 1)
                pe.wait_ge(S("r0"), S.at("r0", 1))
                for c in range(2):
                    ins = nc.tensor.matmul(pMisc[:, 0:1], V2[:, c, :], small[:, 6 + c:7 + c], start=(c == 0),
                                           stop=(c == 1))
                ins.then_inc(S("y0_p"), 1)

        def mlp(groups, dense):
            col0, g0 = (0, 0) if dense else (N, NG)

            with nc.Block() as block:
                @block.sync
                def _(sp):
                    def load(u, k, r):
                        P, J = shape(k, dense)
                        if not fresh(k):
                            sp.wait_ge(S("z_nodes" if dense else "cols_psum"),
                                       S.at("z_nodes" if dense else "cols_psum", k + 1 - U))
                        rows_ = node_rows(x3_nodes, k) if dense else slot_rows(z_slots, k)
                        sp.dma_start(G[u][0:P, 0:J, :], rows_).then_inc(S(f"loaded{u}"), 16)

                    def stage(s, u, k, r):
                        if s == 2:
                            P, J = shape(k, dense)
                            sp.wait_ge(S("y_copied"), S.at("y_copied", k + 1))
                            sp.dma_start(y_cols[:, bass.ds(k * GC + col0, P * J)], t4[u][:,
                                         0:P * J]).then_inc(S(f"stored{u}"), 16)

                    steps(sp, 3, groups, stage, (1, load))
                    for u in range(min(U, groups)):
                        sp.wait_ge(S(f"stored{u}"), S.at(f"stored{u}", 16 * len(range(u, groups, U))))

                if dense:
                    @block.gpsimd
                    def _(pool):
                        def stage(s, u, k, r):
                            if s == 0:
                                P, J = shape(k)
                                pool.wait_ge(S(f"loaded{u}"), S.at(f"loaded{u}", (r + 1) * 16))
                                if not fresh(k):
                                    pool.wait_ge(S("cols_psum"), S.at("cols_psum", k + 1 - U))
                                nc.gpsimd.tensor_tensor(nm(t0[u])[0:P, 0:J, :], G[u][0:P, 0:J, :],
                                                        nmask[0:P, bass.ds(4 * k, J)].unsqueeze(2).to_broadcast([P,
                                                                J, D]),
                                                        ALU.mult).then_inc(S("z_nodes"), 1)

                        steps(pool, 3, groups, stage)

                @block.tensor
                def _(pe):
                    def stage(s, u, k, r):
                        P, J = shape(k, dense)
                        C = P * J
                        if s == 0:
                            pe.wait_ge(S("z_nodes"),
                                       S.at("z_nodes", k + 1)) if dense else pe.wait_ge(S(f"loaded{u}"), S.at(f"loaded{u}", (r + 1) * 16))
                            transposes(nm(t0[u]) if dense else G[u], pA[u], P, J).then_inc(S("cols_psum"), 1)
                        elif s == 1:
                            pe.wait_ge(S("cols_copied"), S.at("cols_copied", k + 1))
                            feature_major(pB[u], [(t1[u], V1[:, 0, :])], C)
                            feature_major(pA[u], [(t1[u], V1[:, 1, :])], C).then_inc(S("hidden_product"), 1)
                        elif s == 2:
                            pe.wait_ge(S("hidden_cols"), S.at("hidden_cols", k + 1))
                            feature_major(pB[u], [(t2[u], V2[:, 0, :]), (t3[u], V2[:, 1, :])],
                                          C).then_inc(S("y_product"), 1)

                    steps(pe, 3, groups, stage)

                @block.scalar
                def _(act):
                    def stage(s, u, k, r):
                        P, J = shape(k, dense)
                        C = P * J
                        if s == 0:
                            act.wait_ge(S("cols_psum"), S.at("cols_psum", k + 1))
                            nc.scalar.copy(t1[u][:, 0:C], pA[u][:, 0:C]).then_inc(S("cols_copied"), 1)
                        elif s == 1:
                            act.wait_ge(S("hidden_product"), S.at("hidden_product", k + 1))
                            nc.scalar.activation(t2[u][:, 0:C], pB[u][:, 0:C], ACTF.Relu, bias=bn[:, b_t1:b_t1 + 1],
                                                 scale=bn[:, b_s1:b_s1 + 1])
                            nc.scalar.activation(t3[u][:, 0:C], pA[u][:, 0:C], ACTF.Relu, bias=bn[:,
                                                 b_t1 + 1:b_t1 + 2],
                                                 scale=bn[:, b_s1 + 1:b_s1 + 2]).then_inc(S("hidden_cols"), 1)
                        elif s == 2:
                            act.wait_ge(S("y_product"), S.at("y_product", k + 1))
                            if not fresh(k):
                                act.wait_ge(S(f"stored{u}"), S.at(f"stored{u}", r * 16))
                            if not fresh(k):
                                act.wait_ge(S("y_moments"), S.at("y_moments", k + 1 - U))
                            nc.scalar.copy(t4[u][:, 0:C], pB[u][:, 0:C]).then_inc(S("y_copied"), 1)

                    steps(act, 3, groups, stage)

                @block.vector
                def _(dve):
                    def stage(s, u, k, r):
                        if s == 2:
                            P, J = shape(k, dense)
                            dve.wait_ge(S("y_copied"), S.at("y_copied", k + 1))
                            nc.vector.bn_stats(ystat[:, bass.ds(k + g0, 1), :].rearrange("p o s -> p (o s)"),
                                               t4[u][:, 0:P * J]).then_inc(S("y_moments"), 1)

                    steps(dve, 3, groups, stage)
            finish(groups, ["cols_psum", "cols_copied", "hidden_product", "hidden_cols", "y_product", "y_copied",
                   "y_moments"] + (["z_nodes"] if dense else []),
                   loaded=16, stored=16)

        in_flight(4, 2, "G t0 t1 t2 t3 t4")
        mlp(EG, False)
        mlp(NG, True)

        with nc.Block() as block:
            @block.gpsimd
            def _(pool):
                pool.wait_ge(S("bn2_var"), S.at("bn2_var", 1))
                nc.gpsimd.tensor_tensor(small[:, 12:13], small[:, 8:9], small[:, 14:15],
                                        ALU.pow).then_inc(S("bn2_rstd"), 1)

            @block.vector
            def _(dve):
                ch = Chain(dve, "dve_setup")
                M = N + EP
                mean, var, y0 = small[:, 0:1], small[:, 1:2], small[:, 16:17]
                m, e, f = small[:, 2:3], small[:, 3:4], small[:, 4:5]

                def tt(o, x, y, op):
                    ch.after(nc.vector.tensor_tensor(o, x, y, op))

                def ts(o, x, s1, s2=None, op0=ALU.mult, op1=ALU.bypass):
                    ch.after(nc.vector.tensor_scalar(o, x, s1, s2, op0, op1) if s2 is not None
                             else nc.vector.tensor_scalar(o, x, s1, None, op0))

                ch.after(nc.vector.bn_aggr(small[:, 0:2], ystat[:, :, :].rearrange("p g s -> p (g s)")))
                tt(e, mean, y0, ALU.subtract)
                ts(e, e, EP / N)
                tt(m, mean, e, ALU.add)
                tt(e, e, e, ALU.mult)
                tt(e, e, var, ALU.add)
                ts(e, e, M / N)
                tt(f, y0, m, ALU.subtract)
                tt(f, f, f, ALU.mult)
                ts(f, f, EP / N)
                tt(e, e, f, ALU.subtract)
                nc.vector.tensor_scalar(small[:, 8:9], e, 0.0, BN_EPS, ALU.max, ALU.add).then_inc(S("bn2_var"), 1)
                dve.wait_ge(S("bn2_rstd"), S.at("bn2_rstd", 1))
                tt(bn[:, b_s2:b_s2 + 1], bn[:, b_g2:b_g2 + 1], small[:, 12:13], ALU.mult)
                tt(e, m, bn[:, b_s2:b_s2 + 1], ALU.mult)
                tt(bn[:, b_t2:b_t2 + 1], bn[:, b_b2:b_b2 + 1], e, ALU.subtract)
                ch.close()

        def last_norm(groups, dense):
            col0 = 0 if dense else N
            per_store, kind = (16, "stored") if dense else (64, "scattered")

            with nc.Block() as block:
                @block.sync
                def _(sp):
                    def load(u, k, r):
                        P, J = shape(k, dense)
                        if not fresh(k):
                            sp.wait_ge(S("hidden_cols"), S.at("hidden_cols", k + 1 - U))
                        sp.dma_start(t1[u][:, 0:P * J], y_cols[:, bass.ds(k * GC + col0,
                                     P * J)]).then_inc(S(f"loaded{u}"), 16)

                    def load_x3(u, k, r):
                        P, J = shape(k, dense)
                        if not fresh(k):
                            sp.wait_ge(S("residual1"), S.at("residual1", k + 1 - U))
                        rows_ = node_rows(x3_nodes, k) if dense else slot_rows(x3_table, k)
                        sp.dma_start(Dn[u][0:P, 0:J, :], rows_).then_inc(S(f"loaded{u}"), 16)

                    def stage(s, u, k, r):
                        if s == 3 and dense:
                            P, J = shape(k)
                            sp.wait_ge(S("normed1"), S.at("normed1", k + 1))
                            sp.dma_start(node_rows(out, k), O[u][0:P, 0:J, :]).then_inc(S(f"stored{u}"), 16)

                    steps(sp, 4, groups, stage, (0, load), (1, load_x3))
                    if dense:
                        for u in range(min(U, groups)):
                            sp.wait_ge(S(f"stored{u}"), S.at(f"stored{u}", 16 * len(range(u, groups, U))))

                @block.gpsimd
                def _(pool):
                    def stage(s, u, k, r):
                        P, J = shape(k, dense)
                        if s == 1:
                            inv_std(pool, u, k, P, J, 1, with_shift=True)
                        elif s == 3 and not dense:
                            pool.wait_ge(S("normed1"), S.at("normed1", k + 1))
                            scatter(pool, u, k, O, out)

                    steps(pool, 4, groups, stage)
                    if not dense:
                        for u in range(min(U, groups)):
                            pool.wait_ge(S(f"scattered{u}"), S.at(f"scattered{u}", 64 * len(range(u, groups, U))))

                @block.tensor
                def _(pe):
                    def stage(s, u, k, r):
                        if s == 0:
                            P, J = shape(k, dense)
                            pe.wait_ge(S("hidden_cols"), S.at("hidden_cols", k + 1))
                            if not fresh(k):
                                pe.wait_ge(S("residual1"), S.at("residual1", k + 1 - U))
                            back_transposes(t0[u], pA[u], P, J).then_inc(S("cols_psum"), 1)

                    steps(pe, 4, groups, stage)

                @block.scalar
                def _(act):
                    def stage(s, u, k, r):
                        if s == 0:
                            P, J = shape(k, dense)
                            act.wait_ge(S(f"loaded{u}"), S.at(f"loaded{u}", (r + 1) * 32))
                            if not fresh(k):
                                act.wait_ge(S("cols_psum"), S.at("cols_psum", k + 1 - U))
                            nc.scalar.activation(t0[u][:, 0:P * J], t1[u][:, 0:P * J], ACTF.Relu, bias=bn[:,
                                                 b_t2:b_t2 + 1],
                                                 scale=bn[:, b_s2:b_s2 + 1]).then_inc(S("hidden_cols"), 1)
                        elif s == 2:
                            P, J = shape(k, dense)
                            if not fresh(k):
                                act.wait_ge(S(f"{kind}{u}"), S.at(f"{kind}{u}", r * per_store))
                            normalise_on_act(act, u, k, P, J, nm(t3[u]), O[u], 1)

                    steps(act, 4, groups, stage)

                @block.vector
                def _(dve):
                    def stage(s, u, k, r):
                        P, J = shape(k, dense)
                        if s == 1:
                            dve.wait_ge(S("cols_psum"), S.at("cols_psum", k + 1))
                            dve.wait_ge(S(f"loaded{u}"), S.at(f"loaded{u}", (r + 1) * 32))
                            if not fresh(k):
                                dve.wait_ge(S("normed1"), S.at("normed1", k + 1 - U))
                            nc.vector.scalar_tensor_tensor(nm(t3[u])[0:P, 0:J, :], Dn[u][0:P, 0:J, :], 2.0,
                                                           nm(pA[u])[0:P, 0:J, :], ALU.mult,
                                                           ALU.add).then_inc(S("residual1"), 1)
                            stats(dve, u, k, P, J, nm(t3[u]), 1, negated=True)

                    steps(dve, 4, groups, stage)
            finish(groups, ["hidden_cols",
                   "cols_psum"] + ln_signals(1) + ["inv_std_alone"] + ([] if dense else ["indices0"]), loaded=32,
                   **{kind: per_store})

        in_flight(7, 1, "Dn O t0 t1 t3")
        last_norm(NG, True)
        last_norm(EG, False)


_INPUTS = ["x", "src", "dst", "edge_attr_128", "L0_gnn_W0", "L0_gnn_b0", "L0_gnn_W1", "L0_gnn_b1", "L0_gnn_W2",
           "L0_gnn_b2", "L1_gnn_W", "L1_gnn_att_src", "L1_gnn_att_dst", "L1_gnn_bias", "L1_gnn_fc_w", "L1_gnn_fc_b",
           "L2_gnn_Wi", "L2_gnn_bi", "L2_gnn_Wm", "L2_gnn_bm", "L2_gnn_Wu", "L2_gnn_bu", "L3_gnn_eps", "L3_gnn_W1",
           "L3_gnn_g1", "L3_gnn_b1", "L3_gnn_W2", "L3_gnn_g2", "L3_gnn_b2"]


def kernel(**inputs):
    import concourse.bacc as bacc
    from concourse.bass_utils import run_bass_kernel_spmd

    nc = bacc.Bacc("TRN2", target_bir_lowering=False, num_devices=1)
    arrays, views = {}, {}
    for name in _INPUTS:
        v = np.asarray(inputs[name])
        v = np.ascontiguousarray(v.reshape(v.shape or (1,)))
        arrays[f"in_{name}"] = v
        views[name] = nc.dram_tensor(f"in_{name}", v.shape, mybir.dt.from_np(v.dtype), kind="ExternalInput").ap()
    out = nc.dram_tensor("out", views["x"].shape, F32, kind="ExternalOutput").ap()
    build(nc, views, out)
    got = run_bass_kernel_spmd(nc, [arrays], core_ids=[0])
    return got.results[0]["out"]
```
